# Optimizing a Trainium2 kernel written in Bass

```python
import numpy as np
import jax
import jax.numpy as jnp

def _softmax(x, axis=-1):
    return jax.nn.softmax(x, axis=axis)

def _gelu(x):
    return jax.nn.gelu(x, approximate=True)

def _silu(x):
    return jax.nn.silu(x)

def _sigmoid(x):
    return jax.nn.sigmoid(x)

def _layernorm(x, axis=-1, eps=1e-05):
    m = jnp.mean(x, axis=axis, keepdims=True)
    v = jnp.var(x, axis=axis, keepdims=True)
    return (x - m) / jnp.sqrt(v + eps)

def _scatter_add(tgt, idx, src, axis=0):
    return tgt.at[idx].add(src)

def _segment_sum(src, seg, n):
    return jax.ops.segment_sum(src, seg, n)
kernel_name = 'mk_early_fusion_embed_d1_tok_img512_r4_d51876'

def setup_inputs(seed: int=0):
    np.random.seed(seed)
    _w = jnp.asarray

    def _rec_inputs():
        import jax
        import jax.numpy as jnp
        _rk = jax.random.key(seed)
        x = 7.57192e-06 + 1.00007 * jax.random.normal(jax.random.fold_in(_rk, 1), (64, 96, 96, 3), jnp.float32)
        x_txt = jax.random.randint(jax.random.fold_in(_rk, 51), (64, 32), 0, 51, jnp.int32)
        return (x, x_txt)
    x, x_txt = _rec_inputs()

    def _L0_tok_setup():
        import jax, jax.numpy as jnp
        import numpy as np
        B, H, W, C = (64, 224, 224, 3)
        P, D = (16, 128)
        LN_EPS = 0.001

        def _shift4(x):
            pad = lambda a, spec: jnp.pad(a, spec)
            right = pad(x[:, :, :-1, :], ((0, 0), (0, 0), (1, 0), (0, 0)))
            left = pad(x[:, :, 1:, :], ((0, 0), (0, 0), (0, 1), (0, 0)))
            down = pad(x[:, :-1, :, :], ((0, 0), (1, 0), (0, 0), (0, 0)))
            up = pad(x[:, 1:, :, :], ((0, 0), (0, 1), (0, 0), (0, 0)))
            return [right, left, down, up]
        key = jax.random.key(seed)
        k0, k1, k2 = jax.random.split(key, 3)
        x = jax.random.normal(k0, (B, H, W, C), jnp.float32)
        conv_w = jax.random.normal(k1, (P, P, 5 * C, D), jnp.float32) * 0.02
        conv_b = jnp.zeros((D,), jnp.float32)
        gamma = jnp.ones((D,), jnp.float32)
        beta = jnp.zeros((D,), jnp.float32)
        dense_w = jax.random.normal(k2, (D, D), jnp.float32) * 0.02
        dense_b = jnp.zeros((D,), jnp.float32)
        return {'x': x, 'conv_w': conv_w, 'conv_b': conv_b, 'gamma': gamma, 'beta': beta, 'dense_w': dense_w, 'dense_b': dense_b}
    _L0_tok_all = _L0_tok_setup()
    _L0_tok_in = {k: v for k, v in _L0_tok_all.items() if k in ('conv_w', 'conv_b', 'gamma', 'beta', 'dense_w', 'dense_b')}
    del _L0_tok_all

    def _L0_txt_setup():
        import jax, jax.numpy as jnp
        import numpy as np
        C, L = (32, 1024)
        NUM_BINS, HID, D = (51, 128, 128)
        key = jax.random.key(seed)
        k1, k2, k3, k4, k5, k6 = jax.random.split(key, 6)
        expr_tokens = jax.random.randint(k1, (C, L), 0, NUM_BINS, dtype=jnp.int64)
        bin_embeddings = jax.random.normal(k2, (NUM_BINS, D), dtype=jnp.float32)
        w1 = jax.random.normal(k3, (1, HID), dtype=jnp.float32) * 1.0
        b1 = jax.random.normal(k4, (HID,), dtype=jnp.float32) * 0.1
        w2 = jax.random.normal(k5, (HID, D), dtype=jnp.float32) * (1.0 / np.sqrt(HID))
        b2 = jax.random.normal(k6, (D,), dtype=jnp.float32) * 0.1
        return {'expr_tokens': expr_tokens, 'bin_embeddings': bin_embeddings, 'w1': w1, 'b1': b1, 'w2': w2, 'b2': b2}
    _L0_txt_all = _L0_txt_setup()
    _L0_txt_in = {k: v for k, v in _L0_txt_all.items() if k in ('bin_embeddings', 'w1', 'b1', 'w2', 'b2')}
    del _L0_txt_all

    def _L0_attn_setup():
        import jax, jax.numpy as jnp
        import numpy as np
        DIM = 128
        QK_DIM = DIM // 8
        EXPAND_DIM = DIM * 2
        LN_EPS = 1e-05

        def _layer_norm(x):
            mu = jnp.mean(x, axis=-1, keepdims=True)
            var = jnp.mean(jnp.square(x - mu), axis=-1, keepdims=True)
            return (x - mu) * jax.lax.rsqrt(var + LN_EPS)
        key = jax.random.key(seed)
        k1, k2, k3 = jax.random.split(key, 3)
        B, N = (8, 512)
        x = jax.random.normal(k1, (B, N, DIM), dtype=jnp.float32)
        out_e = 2 * QK_DIM + 2 * EXPAND_DIM
        be = float(np.sqrt(6.0 / (DIM + out_e)))
        expand = jax.random.uniform(k2, (DIM, out_e), minval=-be, maxval=be, dtype=jnp.float32)
        bp = float(np.sqrt(6.0 / (EXPAND_DIM + DIM)))
        project = jax.random.uniform(k3, (EXPAND_DIM, DIM), minval=-bp, maxval=bp, dtype=jnp.float32)
        position_bias_mult = jnp.array(4.0, dtype=jnp.float32)
        return {'x': x, 'expand': expand, 'project': project, 'position_bias_mult': position_bias_mult}
    _L0_attn_all = _L0_attn_setup()
    _L0_attn_in = {k: v for k, v in _L0_attn_all.items() if k in ('expand', 'project', 'position_bias_mult')}
    del _L0_attn_all

    def _L0_ffn_setup():
        import jax, jax.numpy as jnp
        import numpy as np
        NUM_TILES = 64
        TPC = 8
        GRID = 16
        EPS = 1e-05
        key = jax.random.key(seed)
        ks = jax.random.split(key, 6)
        B, S, D, T, DH, G = (2, 256, 128, NUM_TILES, 128, GRID)
        x = jax.random.normal(ks[0], (B, S, D), dtype=jnp.float32)
        gamma = jnp.ones((D,), jnp.float32)
        beta = jnp.zeros((D,), jnp.float32)
        Wd = jax.random.normal(ks[1], (T, DH, D), dtype=jnp.float32) * 0.02
        spline_bases = jax.random.normal(ks[2], (T, DH, G), dtype=jnp.float32) * 0.1
        spline_slopes = jax.random.normal(ks[3], (T, DH, G), dtype=jnp.float32) * 0.1
        Wu = jax.random.normal(ks[4], (T, D, DH), dtype=jnp.float32) * 0.02
        scale = jnp.full((T,), 0.1, jnp.float32)
        return {'x': x, 'gamma': gamma, 'beta': beta, 'Wd': Wd, 'spline_bases': spline_bases, 'spline_slopes': spline_slopes, 'Wu': Wu, 'scale': scale}
    _L0_ffn_all = _L0_ffn_setup()
    _L0_ffn_in = {k: v for k, v in _L0_ffn_all.items() if k in ('gamma', 'beta', 'Wd', 'spline_bases', 'spline_slopes', 'Wu', 'scale')}
    del _L0_ffn_all
    return {'x': x, 'x_txt': x_txt, 'L0_tok_conv_w': _L0_tok_in['conv_w'], 'L0_tok_conv_b': _L0_tok_in['conv_b'], 'L0_tok_gamma': _L0_tok_in['gamma'], 'L0_tok_beta': _L0_tok_in['beta'], 'L0_tok_dense_w': _L0_tok_in['dense_w'], 'L0_tok_dense_b': _L0_tok_in['dense_b'], 'L0_txt_bin_embeddings': _L0_txt_in['bin_embeddings'], 'L0_txt_w1': _L0_txt_in['w1'], 'L0_txt_b1': _L0_txt_in['b1'], 'L0_txt_w2': _L0_txt_in['w2'], 'L0_txt_b2': _L0_txt_in['b2'], 'L0_attn_expand': _L0_attn_in['expand'], 'L0_attn_project': _L0_attn_in['project'], 'L0_attn_position_bias_mult': _L0_attn_in['position_bias_mult'], 'L0_ffn_gamma': _L0_ffn_in['gamma'], 'L0_ffn_beta': _L0_ffn_in['beta'], 'L0_ffn_Wd': _L0_ffn_in['Wd'], 'L0_ffn_spline_bases': _L0_ffn_in['spline_bases'], 'L0_ffn_spline_slopes': _L0_ffn_in['spline_slopes'], 'L0_ffn_Wu': _L0_ffn_in['Wu'], 'L0_ffn_scale': _L0_ffn_in['scale']}

def reference(x, x_txt, L0_tok_conv_w, L0_tok_conv_b, L0_tok_gamma, L0_tok_beta, L0_tok_dense_w, L0_tok_dense_b, L0_txt_bin_embeddings, L0_txt_w1, L0_txt_b1, L0_txt_w2, L0_txt_b2, L0_attn_expand, L0_attn_project, L0_attn_position_bias_mult, L0_ffn_gamma, L0_ffn_beta, L0_ffn_Wd, L0_ffn_spline_bases, L0_ffn_spline_slopes, L0_ffn_Wu, L0_ffn_scale):
    import jax
    import jax.numpy as jnp

    def _L0_tok_ref(x, conv_w, conv_b, gamma, beta, dense_w, dense_b):
        import jax, jax.numpy as jnp
        import numpy as np
        B, H, W, C = (64, 224, 224, 3)
        P, D = (16, 128)
        LN_EPS = 0.001

        def _shift4(x):
            pad = lambda a, spec: jnp.pad(a, spec)
            right = pad(x[:, :, :-1, :], ((0, 0), (0, 0), (1, 0), (0, 0)))
            left = pad(x[:, :, 1:, :], ((0, 0), (0, 0), (0, 1), (0, 0)))
            down = pad(x[:, :-1, :, :], ((0, 0), (1, 0), (0, 0), (0, 0)))
            up = pad(x[:, 1:, :, :], ((0, 0), (0, 1), (0, 0), (0, 0)))
            return [right, left, down, up]
        xs = jnp.concatenate([x, *_shift4(x)], axis=-1)
        y = jax.lax.conv_general_dilated(xs, conv_w, window_strides=(P, P), padding='VALID', dimension_numbers=('NHWC', 'HWIO', 'NHWC')) + conv_b
        y = y.reshape(y.shape[0], -1, D)
        mu = jnp.mean(y, axis=-1, keepdims=True)
        var = jnp.mean(jnp.square(y - mu), axis=-1, keepdims=True)
        y = (y - mu) * jax.lax.rsqrt(var + LN_EPS) * gamma + beta
        return y @ dense_w + dense_b

    def _L0_txt_ref(expr_tokens, bin_embeddings, w1, b1, w2, b2):
        import jax, jax.numpy as jnp
        import numpy as np
        C, L = (32, 1024)
        NUM_BINS, HID, D = (51, 128, 128)
        zero_mask = expr_tokens == 0
        x = expr_tokens.astype(jnp.float32)[..., None]
        h = jax.nn.relu(jnp.matmul(x, w1) + b1)
        enc = jnp.matmul(h, w2) + b2
        bins = bin_embeddings[1:]
        sim = jnp.einsum('cld,nd->cln', enc, bins)
        probs = jax.nn.softmax(sim, axis=-1)
        emb = jnp.einsum('cln,nd->cld', probs, bins)
        out = jnp.where(zero_mask[..., None], bin_embeddings[0], emb)
        return out

    def _L0_attn_ref(x, expand, project, position_bias_mult):
        import jax, jax.numpy as jnp
        import numpy as np
        DIM = 128
        QK_DIM = DIM // 8
        EXPAND_DIM = DIM * 2
        LN_EPS = 1e-05

        def _layer_norm(x):
            mu = jnp.mean(x, axis=-1, keepdims=True)
            var = jnp.mean(jnp.square(x - mu), axis=-1, keepdims=True)
            return (x - mu) * jax.lax.rsqrt(var + LN_EPS)
        B, N, _ = x.shape
        nx = _layer_norm(x)
        h = nx @ expand
        q = h[..., :QK_DIM]
        k = h[..., QK_DIM:2 * QK_DIM]
        linear = h[..., 2 * QK_DIM:2 * QK_DIM + EXPAND_DIM]
        pre_gelu = h[..., 2 * QK_DIM + EXPAND_DIM:]
        gated = linear * jax.nn.gelu(pre_gelu, approximate=False)
        local = gated[..., :EXPAND_DIM - DIM]
        v = gated[..., EXPAND_DIM - DIM:]
        pos = jnp.arange(N)
        rel = (pos[None, :] - pos[:, None]).astype(x.dtype)
        causal = pos[None, :] <= pos[:, None]
        mask = jnp.where(causal, jax.nn.sigmoid(rel + position_bias_mult), -jnp.inf)
        logits = jnp.einsum('bqd,bkd->bqk', q, k) / jnp.sqrt(jnp.array(QK_DIM, dtype=x.dtype)) + mask
        scores = jax.nn.softmax(logits, axis=-1)
        attn = jnp.einsum('bqk,bkd->bqd', scores, v)
        return x + jnp.concatenate([local, attn], axis=-1) @ project

    def _L0_ffn_ref(x, gamma, beta, Wd, spline_bases, spline_slopes, Wu, scale):
        import jax, jax.numpy as jnp
        import numpy as np
        NUM_TILES = 64
        TPC = 8
        GRID = 16
        EPS = 1e-05
        B, S, D = x.shape
        T, DH, _ = Wd.shape
        C = T // TPC
        N = B * S
        mu = x.mean(-1, keepdims=True)
        var = ((x - mu) ** 2).mean(-1, keepdims=True)
        xn = (x - mu) * jax.lax.rsqrt(var + EPS) * gamma + beta
        xf = xn.reshape(N, D)
        tile_sigs = jnp.sign(Wd.mean(axis=1))
        cluster_sigs = jnp.sign(tile_sigs.reshape(C, TPC, D).mean(1))
        in_sigs = jnp.sign(xf)
        best_c = jnp.argmax(in_sigs @ cluster_sigs.T, axis=-1)
        tile_scores = (in_sigs @ tile_sigs.T).reshape(N, C, TPC)
        sc = jnp.take_along_axis(tile_scores, best_c[:, None, None], axis=1)[:, 0, :]
        local_best = jnp.argmax(sc, axis=-1)
        tidx = best_c * TPC + local_best
        h = jnp.einsum('nd,nhd->nh', xf, Wd[tidx])
        hn = jax.nn.sigmoid(h)
        idx = jnp.clip((hn * GRID).astype(jnp.int32), 0, GRID - 1)
        base = jnp.take_along_axis(spline_bases[tidx], idx[..., None], axis=-1)[..., 0]
        slope = jnp.take_along_axis(spline_slopes[tidx], idx[..., None], axis=-1)[..., 0]
        local_pos = hn * GRID - idx.astype(h.dtype)
        hs = base + slope * local_pos
        y = jnp.einsum('nh,ndh->nd', hs, Wu[tidx]) * scale[tidx][:, None]
        return x + y.reshape(B, S, D)
    h = _L0_tok_ref(x, L0_tok_conv_w, L0_tok_conv_b, L0_tok_gamma, L0_tok_beta, L0_tok_dense_w, L0_tok_dense_b)
    h = jnp.concatenate([h, _L0_txt_ref(x_txt, L0_txt_bin_embeddings, L0_txt_w1, L0_txt_b1, L0_txt_w2, L0_txt_b2)], axis=1)
    h = h + _L0_attn_ref(_layernorm(h, axis=-1), L0_attn_expand, L0_attn_project, L0_attn_position_bias_mult)
    h = h + _L0_ffn_ref(_layernorm(h, axis=-1), L0_ffn_gamma, L0_ffn_beta, L0_ffn_Wd, L0_ffn_spline_bases, L0_ffn_spline_slopes, L0_ffn_Wu, L0_ffn_scale)
    return h

_drawn_inputs = setup_inputs


def setup_inputs(seed=0):
    import zlib

    import numpy as np

    out = dict(_drawn_inputs(seed))
    spreads = {'L0_tok_conv_b': (0.0, 0.1),
     'L0_tok_gamma': (1.0, 0.2),
     'L0_tok_beta': (0.0, 0.1),
     'L0_tok_dense_b': (0.0, 0.1),
     'L0_ffn_gamma': (1.0, 0.6),
     'L0_ffn_beta': (0.0, 0.8),
     'L0_ffn_scale': (0.10000000149011612, 0.6)}
    factors = {'L0_txt_b1': 4.395,
     'L0_txt_b2': 8.0,
     'L0_ffn_Wd': 8.0,
     'L0_ffn_spline_bases': 8.0,
     'L0_ffn_spline_slopes': 8.0,
     'L0_ffn_Wu': 8.0}
    for name, (base, spread) in spreads.items():
        noise = np.random.default_rng([zlib.crc32(name.encode()), seed]).standard_normal(out[name].shape)
        drawn = base * np.exp(spread * noise) if base else spread * noise
        out[name] = jnp.asarray(drawn.astype(out[name].dtype))
    for name, factor in factors.items():
        out[name] = (out[name] * factor).astype(out[name].dtype)
    return out
```

```python
from contextlib import ExitStack

import numpy as np

import concourse.bass as bass
from concourse import mybir

F32 = mybir.dt.float32
BF16 = mybir.dt.bfloat16
I32 = mybir.dt.int32
ALU = mybir.AluOpType
ACT = mybir.ActivationFunctionType
AX = mybir.AxisListType

P = 128
D = 128
B = 64
IMG = 96
PATCH = 16
CH = 3
GRID_W = IMG // PATCH
S_IMG = GRID_W * GRID_W
S_TXT = 32
S = S_IMG + S_TXT
N = B * S
GB = 4
NG = B // GB
GI = GB * S_IMG
HI = GI // 2
GT = GB * S_TXT
GS = GB * S
WIN = PATCH + 2
KCH = 8
KP = (WIN * WIN - 4) * CH // KCH
BINS = 51
NB = BINS - 1
QK = 16
KOFF = 32
E = 64
CL = 8
TPC = E // CL
GRID = 16
T = N // P
TT = 2 * P
NT2 = N // TT
ST = 32
NTILE = -(-(E + (N - E) // ST) // 8) * 8
TI = 8
SI = TI * ST
NI = NTILE // TI
SLOTS = NTILE * ST
WROW = 2 * D + 2 * GRID
SIG_C = 8
EPS_TOK = 1e-3
EPS = 1e-5
HUGE = 3.0e38
RING = 4
YR = 4


def fixed(g):
    return isinstance(g, int)


def pipelined(eng, n, stages, unroll=2):
    stages = sorted(stages, key=lambda at: -at[0])
    depth = stages[0][0]
    head = -(-(depth + 2) // unroll) * unroll
    rest = (n - head) // unroll * unroll + head

    def peeled(i):
        for lag, stage in stages:
            if 0 <= i - lag < n:
                stage(i - lag, (i - lag) % unroll)

    for i in range(head):
        peeled(i)
    with eng.Fori(head // unroll, rest // unroll) as turn:
        for u in range(unroll):
            for lag, stage in stages:
                stage(turn * unroll + (u - lag), (u - lag) % unroll)
    for i in range(rest, n + depth):
        peeled(i)


def free_again(eng, sem, g, slots):
    if not fixed(g) or g >= slots:
        eng.wait_ge(sem, g - slots + 1)


def spread_to(ap, dim, count):
    ap = ap.unsqueeze(dim)
    return ap.broadcast_to([count if i == dim else n for i, n in enumerate(ap.shape)])


def build(nc, t, out):
    with ExitStack() as ctx:
        def sb(name, shape, dt=F32):
            return ctx.enter_context(nc.sbuf_tensor(name, shape, dt))

        def sem(name):
            return ctx.enter_context(nc.semaphore(name))

        bank = [ctx.enter_context(nc.psum_tensor(f"bank{i}", [P, 512], F32)) for i in range(8)]

        xs_dram = nc.dram_tensor("slots_in", (SLOTS, D), F32).ap()
        ys_dram = nc.dram_tensor("slots_out", (SLOTS, D), F32).ap()

        ident = sb("ident", [P, P])
        centre = sb("centre", [P, P])
        c128 = sb("c128", [P, 2])
        before = sb("before", [P, P], BF16)
        upto = sb("upto", [E, E], BF16)
        ones_bf = sb("ones_bf", [P, P], BF16)
        tie = sb("tie", [P, E])
        tile_no = sb("tile_no", [E, NTILE])
        rel = sb("rel", [S, S])
        causal = sb("causal", [S, S])
        veil = sb("veil", [S, S])
        mask = sb("mask", [S, S])
        pbm = sb("pbm", [P, 1])
        eps = sb("eps", [P, 3])
        cols = sb("cols", [P, 9])
        w2 = sb("w2", [P, D])
        bins_t = sb("bins_t", [P, NB])
        bins = sb("bins", [BINS, D])
        x_txt = sb("x_txt", [P, B * S_TXT], I32)
        x_col = sb("x_col", [GT, NG], I32)
        is0 = sb("is0", [GT, NG])
        not0 = sb("not0", [GT, NG])
        dense = sb("dense", [P, D])
        dense_bias = sb("dense_bias", [P, 1])
        expand = sb("expand", [P, 4 * P + 64])
        project = sb("project", [P, 2, D])
        scale_row = sb("scale_row", [P, E])

        hT = sb("hT", [P, N])
        nxT = sb("nxT", [P, N])
        gate_loc = sb("gate_loc", [P, N])
        gate_v = sb("gate_v", [P, N])
        h2T = sb("h2T", [P, N])
        xf_tok = gate_loc[:, :].rearrange("p (i d) -> p i d", d=D)
        res_tok = gate_v[:, :].rearrange("p (i d) -> p i d", d=D)
        onehot = hT[:, 0:E * T].rearrange("p (e i) -> p e i", i=T)
        weighed = hT[:, E * T:2 * E * T]
        upto_here = nxT[:, 0:E * T]
        place_of = nxT[:, E * T:2 * E * T]

        big = sb("big", [P, RING * KCH * GI + 5 * KCH * D])
        patches = big[0:KP, 0:RING * KCH * GI].rearrange("p (r k n) -> p r k n", r=RING, k=KCH)
        w5 = big[0:KP, RING * KCH * GI:].rearrange("p (s k) -> p s k", s=5)
        LOOK = 2 * GRID // 2 * SI
        look = big[:, 0:2 * LOOK].rearrange("p (r a k n) -> p r a k n", r=2, a=2, k=GRID // 2)

        s_a = sb("s_a", [P, 2, GS])
        s_b = sb("s_b", [P, 2, GS])
        s_c = sb("s_c", [P, 2, GS])
        s_d = sb("s_d", [P, 2, GS])
        s_e = sb("s_e", [P, 2, GS])
        s_f = sb("s_f", [P, 2, GS])
        s_g = sb("s_g", [P, 2, GS])
        s_v = sb("s_v", [P, 2, GB * D])
        roots = sb("roots", [P, 2, 8])
        recips = sb("recips", [P, 2, 8])
        signs = sb("signs", [P, 2, TT], BF16)
        keys = sb("keys", [P, 2, 2 * E])
        best = sb("best", [P, 2, 2])
        small = sb("small", [P, 2, 8])

        sig_sum = sb("sig_sum", [P, E])
        sig_tile = sb("sig_tile", [P, E])
        sig_clsum = sb("sig_clsum", [P, CL])
        sig_cl = sb("sig_cl", [P, CL])
        w_tile = sb("w_tile", [P, E], BF16)
        w_cl = sb("w_cl", [P, E], BF16)
        cnt = sb("cnt", [P, E], BF16)
        tot_i = sb("tot_i", [E, 2], I32)
        ntile = sb("ntile", [E, 2], BF16)
        ends = sb("ends", [E, 1])
        started = sb("started", [E, NTILE], BF16)
        owner = sb("owner", [P, NTILE], I32)
        base = sb("base", [P, E])
        slot_f = sb("slot_f", [P, T])
        slot_i = sb("slot_i", [P, T], I32)
        scale_tok = sb("scale_tok", [P, T])

        wts = sb("wts", [P, 2, TI, WROW])
        rows_in = sb("rows_in", [P, 2, 2, D])
        zeros = rows_in[:, :, :, :].rearrange("p a b d -> p (a b d)")
        bits = sb("bits", [P, 2, 4, SI])
        rem = sb("rem", [P, 5, SI])
        rows_out = sb("rows_out", [P, YR, 2 * D])

        s_ld = {k: sem(f"ld_{k}") for k in ("const", "text", "image", "attn", "route")}
        s_patch = [sem(f"patch{i}") for i in range(RING)]
        names = """conv_used fold_done fold_step setup_step mask_ready
            hid_ready enc_mm enc_ready sim_mm top_ready exp_ready prob_step prob_ready pt_mm pt_ready
            emb_mm emb_ready txt_cols
            conv_mm conv_ready ctr_mm ctr_ready var_mm root_ready recip_ready spread_mm norm_ready
            dense_mm img_ready bias_mm bias_ready
            ctr1_mm ctr1_ready var1_mm root1_ready recip1_ready spread1_mm x1_ready nx1_ready hx_ready
            pre_mm gate_ready
            qk_mm q_ready k_ready lin_mm loc_ready vT_ready vt_mm v_ready s_mm soft_step sum_step shifted_ready
            expd_ready p_ready pp_mm pp_ready av_mm at_ready out_mm h2_ready
            ctr2_mm ctr2_ready var2_mm root2_ready recip2_ready spread2_mm x2_ready res_ready xf_ready sign_ready
            turn_mm xf_out res_out score_mm key_step choice_ready
            sig_used sig_red sig_step sig_ready
            cnt_ready scan_ready place_step route_mm route_dve owner_ready slots_ready zero_set zero_filled scattered scale_step
            turn3_mm x3_ready h3_mm cell_ready fill_ready wait_carried look_step spline_ready y_mm y_ready y_stored
            owner_cast final_out stored""".split()
        s = {name: sem(name) for name in names}
        s_sig = [sem("sig0"), sem("sig1")]
        s_rows = [sem("rows0"), sem("rows1")]
        s_wts = [sem("wts0"), sem("wts1")]
        s_yst = [sem("yst0"), sem("yst1")]
        s_fetch = [sem(f"fetch{i}") for i in range(YR)]

        COLS = dict(w1=0, b1=1, b2=2, conv_b=3, tok_gamma=4, tok_beta=5, dense_b=6, ffn_gamma=7, ffn_beta=8)

        def col(name):
            return cols[:, COLS[name]:COLS[name] + 1]

        def cols_of(g, width):
            return bass.ds(g * width, width)

        sig_buf = wts[:, :, :, 0:D]
        block = ctx.enter_context(nc.Block())

        @block.sync
        def _(sp):
            for name, dst in (("w2", w2), ("bins_t", bins_t), ("bins", bins), ("cols", cols)):
                sp.dma_start(dst[:, :], t[name]).then_inc(s_ld["text"], 16)
            sp.dma_start(x_txt[:, :], t["x_row"].partition_broadcast(P)).then_inc(s_ld["text"], 16)
            sp.dma_start(x_col[:, :], t["x_col"]).then_inc(s_ld["text"], 16)
            sp.dma_start(ident[:, :], t["ident"]).then_inc(s_ld["const"], 16)
            sp.dma_start(centre[:, :], t["centre"]).then_inc(s_ld["const"], 16)
            sp.dma_start(c128[:, :], t["c128"]).then_inc(s_ld["const"], 16)
            sp.dma_start(eps[:, :], t["eps"]).then_inc(s_ld["const"], 16)
            sp.dma_start(w5, t["w5"]).then_inc(s_ld["image"], 16)
            sp.dma_start(dense[:, :], t["dense"]).then_inc(s_ld["image"], 16)
            for g in range(NG):
                if g >= RING:
                    sp.wait_ge(s["conv_mm"], g - RING + 1)
                sp.dma_start(patches[:, g % RING], t["patches"][g]).then_inc(s_patch[g % RING], 16)
            for c in range(E // SIG_C):
                if c >= 2:
                    sp.wait_ge(s["sig_red"], c - 1)
                sp.dma_start(sig_buf[:, c % 2],
                             t["packs"][c * SIG_C:(c + 1) * SIG_C, :, 0:D].rearrange("e p h -> p e h")
                             ).then_inc(s_sig[c % 2], 16)

            sp.wait_ge(s["owner_ready"], 1)

            def load(g, par):
                if not fixed(g) or g >= 2:
                    sp.wait_ge(s["y_mm"], g - 1)
                else:
                    sp.wait_ge(s["sig_red"], E // SIG_C)
                for j in range(TI):
                    e = sp.value_load(owner[0:1, bass.ds(g * TI + j, 1)], min_val=0, max_val=E - 1)
                    sp.dma_start(wts[:, par, j, :], t["packs"][bass.ds(e, 1)].rearrange("e p w -> (e p) w")
                                 ).then_inc(s_wts[par], 16)
                if fixed(g) and g == 0:
                    sp.wait_ge(s["scattered"], 16 * T)
                sp.dma_start(rows_in[:, par],
                             xs_dram[bass.ds(g * SI, SI), :].rearrange("(a p) d -> p a d", p=P)
                             ).then_inc(s_rows[par], 16)

            pipelined(sp, NI, [(0, load)])

            for i in range(T):
                sp.wait_ge(s["final_out"], i + 1)
                sp.dma_start(out[i * P:(i + 1) * P, :], res_tok[:, i, :]).then_inc(s["stored"], 16)
            sp.wait_ge(s["stored"], 16 * T)

        @block.gpsimd
        def _(pool):
            pool.memset(zeros, 0.0).then_inc(s["zero_set"], 1)
            pool.wait_ge(s["zero_set"], 1)
            rows_per = 4
            for c in range(0, SLOTS, P * rows_per):
                n = min(rows_per, (SLOTS - c) // P)
                pool.dma_start(xs_dram[c:c + n * P, :].rearrange("(p a) d -> p (a d)", p=P),
                               zeros[:, 0:n * D]).then_inc(s["zero_filled"], 16)
            n_zero = -(-SLOTS // (P * rows_per))

            def add_norm(g, par):
                pool.wait_ge(s["x1_ready"], g + 1)
                here = hT[:, cols_of(g, GS)]
                pool.tensor_tensor(here, here, s_d[:, par], ALU.add).then_inc(s["hx_ready"], 1)

            pipelined(pool, NG, [(3, add_norm)])

            def add_res(g, par):
                pool.wait_ge(s["x2_ready"], g + 1)
                free_again(pool, s["turn_mm"], g, 2)
                pool.tensor_tensor(s_e[:, par, 0:TT], h2T[:, cols_of(g, TT)], s_d[:, par, 0:TT],
                                   ALU.add).then_inc(s["res_ready"], 1)

            pipelined(pool, NT2, [(2, add_res)])

            pool.wait_ge(s["zero_filled"], 16 * n_zero)
            pool.wait_ge(s["slots_ready"], 1)
            pool.wait_ge(s["xf_out"], NT2)
            for i in range(T):
                pool.indirect_dma_start(xs_dram[:, :], bass.IndirectOffsetOnAxis(ap=slot_i[:, i:i + 1], axis=0),
                                        xf_tok[:, i, :], None).then_inc(s["scattered"], 16)

            for k in range(2):
                pool.wait_ge(s_yst[k], 16 * len(range(k, NI, 2)))
            for i in range(T):
                if i >= YR:
                    pool.wait_ge(s["final_out"], i - YR + 1)
                pool.indirect_dma_start(rows_out[:, i % YR, 0:D], None, ys_dram[:, :],
                                        bass.IndirectOffsetOnAxis(ap=slot_i[:, i:i + 1], axis=0)
                                        ).then_inc(s_fetch[i % YR], 16)

        @block.scalar
        def _(act):
            for name, dst in (("rel", rel), ("causal", causal), ("veil", veil), ("expand", expand)):
                act.dma_start(dst[:, :], t[name]).then_inc(s_ld["attn"], 16)
            act.dma_start(project[:, :, :], t["project"]).then_inc(s_ld["attn"], 16)
            act.dma_start(pbm[:, :], t["pbm"].partition_broadcast(P)).then_inc(s_ld["attn"], 16)
            for name, dst in (("before", before), ("upto", upto), ("ones_bf", ones_bf), ("tie", tie),
                              ("tile_no", tile_no)):
                act.dma_start(dst[:, :], t[name]).then_inc(s_ld["route"], 16)
            act.dma_start(scale_row[:, :], t["scale"].partition_broadcast(P)).then_inc(s_ld["route"], 16)

            act.wait_ge(s_ld["attn"], 16 * 6)
            act.activation(mask[:, :], rel[:, :], ACT.Sigmoid, bias=pbm[0:S, :]).then_inc(s["mask_ready"], 1)

            act.wait_ge(s_ld["text"], 16 * 6)

            def hidden(g, par):
                free_again(act, s["enc_mm"], g, 2)
                act.activation(s_a[:, par, 0:GT], x_txt[:, cols_of(g, GT)], ACT.Relu, bias=col("b1"),
                               scale=col("w1")).then_inc(s["hid_ready"], 1)

            def encoded(g, par):
                act.wait_ge(s["enc_mm"], g + 1)
                free_again(act, s["sim_mm"], g, 2)
                act.activation(s_b[:, par, 0:GT], bank[0][:, 0:GT], ACT.Identity, bias=col("b2")
                               ).then_inc(s["enc_ready"], 1)

            def exps(g, par):
                act.wait_ge(s["top_ready"], g + 1)
                free_again(act, s["prob_ready"], g, 2)
                act.activation(s_c[:, par, 0:NB], bank[1][:, 0:NB], ACT.Exp, bias=small[:, par, 0:1],
                               accum_out=small[:, par, 1:2]).then_inc(s["exp_ready"], 1)

            def embedded(g, par):
                act.wait_ge(s["emb_mm"], g + 1)
                act.activation(hT[:, cols_of(g, GS)].rearrange("p (b s) -> p b s", s=S)[:, :, S_IMG:S],
                               bank[3][:, 0:GT].rearrange("p (b s) -> p b s", s=S_TXT), ACT.Copy
                               ).then_inc(s["emb_ready"], 1)

            pipelined(act, NG, [(0, hidden), (0, encoded), (1, exps), (3, embedded)])

            def conv_out(g, par):
                act.wait_ge(s["conv_mm"], g + 1)
                free_again(act, s["ctr_mm"], g, 2)
                act.activation(s_a[:, par, 0:GI], bank[0][:, 0:GI], ACT.Identity, bias=col("conv_b")
                               ).then_inc(s["conv_ready"], 1)

            def centred(g, par):
                act.wait_ge(s["ctr_mm"], g + 1)
                free_again(act, s["norm_ready"], g, 2)
                act.activation(s_b[:, par, 0:GI], bank[1][:, 0:GI], ACT.Copy).then_inc(s["ctr_ready"], 1)
                act.activation(s_c[:, par, 0:GI], bank[1][:, 0:GI], ACT.Square).then_inc(s["ctr_ready"], 1)

            def root(g, par):
                act.wait_ge(s["var_mm"], g + 1)
                free_again(act, s["recip_ready"], g, 2)
                act.activation(roots[0:HI, par, 0:2], bank[2][0:HI, 0:2], ACT.Sqrt, bias=eps[0:HI, 0:1]
                               ).then_inc(s["root_ready"], 1)

            def image_out(g, par):
                act.wait_ge(s["dense_mm"], g + 1)
                act.activation(hT[:, cols_of(g, GS)].rearrange("p (b s) -> p b s", s=S)[:, :, 0:S_IMG],
                               bank[4][:, 0:GI].rearrange("p (b s) -> p b s", s=S_IMG), ACT.Identity,
                               bias=dense_bias[:, 0:1]).then_inc(s["img_ready"], 1)

            act.wait_ge(s["bias_ready"], 1)
            act.wait_ge(s_ld["const"], 16 * 4)
            pipelined(act, NG, [(0, conv_out), (1, centred), (2, root), (4, image_out)])

            def centred1(g, par):
                act.wait_ge(s["ctr1_mm"], g + 1)
                free_again(act, s["nx1_ready"], g, 2)
                act.activation(s_b[:, par], bank[0][:, 0:GS], ACT.Copy).then_inc(s["ctr1_ready"], 1)
                act.activation(s_c[:, par], bank[0][:, 0:GS], ACT.Square).then_inc(s["ctr1_ready"], 1)

            def root1(g, par):
                act.wait_ge(s["var1_mm"], g + 1)
                free_again(act, s["recip1_ready"], g, 2)
                v = bank[1][0:S, 0:GB]
                act.activation(roots[0:S, par, 0:GB], v, ACT.Sqrt, bias=eps[0:S, 1:2]
                               ).then_inc(s["root1_ready"], 1)
                act.activation(roots[0:S, par, GB:2 * GB], v, ACT.Sqrt, bias=eps[0:S, 2:3], scale=1.0 + EPS
                               ).then_inc(s["root1_ready"], 1)

            pipelined(act, NG, [(0, centred1), (1, root1)])

            def gates(g, par):
                act.wait_ge(s["pre_mm"], g + 1)
                act.activation(gate_loc[:, cols_of(g, GS)], bank[4 + par][:, 0:GS], ACT.Gelu
                               ).then_inc(s["gate_ready"], 1)
                act.activation(gate_v[:, cols_of(g, GS)], bank[6 + par][:, 0:GS], ACT.Gelu
                               ).then_inc(s["gate_ready"], 1)

            pipelined(act, NG, [(0, gates)])

            def q_out(g, par):
                act.wait_ge(s["qk_mm"], g + 1)
                free_again(act, s["s_mm"], g, 2)
                act.activation(s_a[0:QK, par], bank[0][0:QK, 0:GS], ACT.Copy).then_inc(s["q_ready"], 1)

            def v_out(g, par):
                act.wait_ge(s["vt_mm"], g + 1)
                free_again(act, s["av_mm"], g, 2)
                act.activation(s_v[0:S, par], bank[3][0:S, :], ACT.Copy).then_inc(s["v_ready"], 1)

            def soft_exp(g, par):
                act.wait_ge(s["shifted_ready"], g + 1)
                act.activation(s_d[0:S, par], s_d[0:S, par], ACT.Exp).then_inc(s["expd_ready"], 1)

            def p_out(g, par):
                act.wait_ge(s["pp_mm"], g + 1)
                free_again(act, s["av_mm"], g, 2)
                act.activation(s_c[0:S, par], bank[5][0:S, 0:GS], ACT.Copy).then_inc(s["pp_ready"], 1)

            def attended(g, par):
                act.wait_ge(s["av_mm"], g + 1)
                free_again(act, s["out_mm"], g, 2)
                act.activation(s_e[:, par], bank[6][:, 0:GS], ACT.Copy).then_inc(s["at_ready"], 1)

            pipelined(act, NG, [(0, q_out), (1, soft_exp), (2, v_out), (3, p_out), (4, attended)])

            def centred2(g, par):
                act.wait_ge(s["ctr2_mm"], g + 1)
                free_again(act, s["x2_ready"], g, 2)
                act.activation(s_b[:, par, 0:TT], bank[0][:, 0:TT], ACT.Copy).then_inc(s["ctr2_ready"], 1)
                act.activation(s_c[:, par, 0:TT], bank[0][:, 0:TT], ACT.Square).then_inc(s["ctr2_ready"], 1)

            def root2(g, par):
                act.wait_ge(s["var2_mm"], g + 1)
                free_again(act, s["recip2_ready"], g, 2)
                v = bank[1][:, 0:2]
                act.activation(roots[:, par, 0:2], v, ACT.Sqrt, bias=eps[:, 1:2]).then_inc(s["root2_ready"], 1)
                act.activation(roots[:, par, 2:4], v, ACT.Sqrt, bias=eps[:, 2:3], scale=1.0 + EPS
                               ).then_inc(s["root2_ready"], 1)

            def affine(g, par):
                act.wait_ge(s["x2_ready"], g + 1)
                free_again(act, s["turn_mm"], g, 2)
                act.activation(s_c2[:, par], s_xn[:, par], ACT.Identity, bias=col("ffn_beta"),
                               scale=col("ffn_gamma")).then_inc(s["xf_ready"], 1)
                act.wait_ge(s["xf_ready"], g + 1)
                act.activation(signs[:, par], s_c2[:, par], ACT.Sign).then_inc(s["sign_ready"], 1)

            def turned(g, par):
                act.wait_ge(s["turn_mm"], g + 1)
                act.activation(gate_loc[:, cols_of(g, TT)], bank[4][:, 0:TT], ACT.Copy).then_inc(s["xf_out"], 1)
                act.activation(gate_v[:, cols_of(g, TT)], bank[5][:, 0:TT], ACT.Copy).then_inc(s["res_out"], 1)

            s_xn = s_v[:, :, 0:TT]
            s_c2 = s_a[:, :, 0:TT]
            pipelined(act, NT2, [(0, centred2), (1, root2), (2, affine), (3, turned)])

            def x_out(g, par):
                act.wait_ge(s["turn3_mm"], g + 1)
                free_again(act, s["h3_mm"], g, 2)
                act.activation(s_a[:, par, 0:SI], bank[0][:, 0:SI], ACT.Copy).then_inc(s["x3_ready"], 1)

            def cell(g, par):
                act.wait_ge(s["h3_mm"], g + 1)
                free_again(act, s["spline_ready"], g, 2)
                act.activation(s_b[:, par, 0:SI], bank[1][:, 0:SI], ACT.Sigmoid).then_inc(s["cell_ready"], 1)

            def fill(g, par):
                free_again(act, s["spline_ready"], g, 2)
                for a in range(2):
                    tab = wts[:, par, :, 2 * D + a * GRID:2 * D + (a + 1) * GRID:2]
                    act.activation(look[:, par, a].rearrange("p k (j n) -> p k j n", n=ST),
                                   spread_to(tab.rearrange("p j k -> p k j"), 3, ST),
                                   ACT.Copy).then_inc(s["fill_ready"], 1)

            def y_out(g, par):
                act.wait_ge(s["y_mm"], g + 1)
                if not fixed(g) or g >= 2:
                    act.wait_ge(s_yst[par], (g - par) * 8)
                act.activation(rows_out[:, par, :], bank[2][:, 0:2 * D], ACT.Copy).then_inc(s["y_ready"], 1)
                act.wait_ge(s["y_ready"], g + 1)
                act.dma_start(ys_dram[bass.ds(g * SI, SI), :].rearrange("(a p) d -> p a d", p=P),
                              rows_out[:, par, :].rearrange("p (a d) -> p a d", a=2)).then_inc(s_yst[par], 16)

            pipelined(act, NI, [(0, x_out), (0, cell), (0, fill), (1, y_out)])

        @block.tensor
        def _(pe):
            def mm(o, l, r, start=True, stop=True):
                return pe.matmul(o, l, r, start=start, stop=stop)

            pe.wait_ge(s_ld["text"], 16 * 6)
            pe.wait_ge(s_ld["const"], 16 * 4)

            def encode(g, par):
                pe.wait_ge(s["hid_ready"], g + 1)
                free_again(pe, s["enc_ready"], g, 1)
                mm(bank[0][:, 0:GT], w2[:, :], s_a[:, par, 0:GT]).then_inc(s["enc_mm"], 1)

            def similar(g, par):
                pe.wait_ge(s["enc_ready"], g + 1)
                free_again(pe, s["exp_ready"], g, 1)
                mm(bank[1][:, 0:NB], s_b[:, par, 0:GT], bins_t[:, :]).then_inc(s["sim_mm"], 1)

            def turn_p(g, par):
                pe.wait_ge(s["prob_ready"], g + 1)
                free_again(pe, s["pt_ready"], g, 1)
                pe.transpose(bank[2][:, 0:GT], s_d[:, par, 0:P], ident[:, :]).then_inc(s["pt_mm"], 1)

            def embed(g, par):
                pe.wait_ge(s["pt_ready"], g + 1)
                free_again(pe, s["emb_ready"], g, 1)
                mm(bank[3][:, 0:GT], bins[:, :], s_e[0:BINS, par, 0:GT]).then_inc(s["emb_mm"], 1)

            pipelined(pe, NG, [(0, encode), (1, similar), (2, turn_p), (3, embed)])

            pe.wait_ge(s_ld["image"], 32)
            pe.wait_ge(s["emb_ready"], NG)
            mm(bank[7][:, 0:1], dense[:, :], col("tok_beta")).then_inc(s["bias_mm"], 1)
            pe.wait_ge(s["fold_done"], 1)
            folded = w5[:, 0, :].rearrange("p (k n) -> p k n", k=KCH)

            def conv(g, par):
                r = par % RING
                pe.wait_ge(s_patch[r], (g - par) * (16 // RING) + 16)
                free_again(pe, s["conv_ready"], g, 1)
                for k in range(KCH):
                    last = mm(bank[0][:, 0:GI], folded[:, k, :], patches[:, r, k, :], k == 0, k == KCH - 1)
                last.then_inc(s["conv_mm"], 1)

            def centre_y(g, par):
                pe.wait_ge(s["conv_ready"], g + 1)
                if not fixed(g) or g >= 1:
                    pe.wait_ge(s["ctr_ready"], 2 * g)
                mm(bank[1][:, 0:GI], centre[:, :], s_a[:, par % 2, 0:GI]).then_inc(s["ctr_mm"], 1)

            def variance(g, par):
                pe.wait_ge(s["ctr_ready"], 2 * g + 2)
                free_again(pe, s["root_ready"], g, 1)
                for j in range(2):
                    last = mm(bank[2][0:HI, j:j + 1], s_c[:, par % 2, j * HI:(j + 1) * HI], c128[:, 0:1])
                last.then_inc(s["var_mm"], 1)

            def spread(g, par):
                pe.wait_ge(s["recip_ready"], g + 1)
                free_again(pe, s["norm_ready"], g, 1)
                for j in range(2):
                    last = mm(bank[3][:, j * HI:(j + 1) * HI],
                              recips[0:HI, par % 2, j:j + 1].broadcast_to([HI, P]), ident[0:HI, 0:HI])
                last.then_inc(s["spread_mm"], 1)

            def dense_mm(g, par):
                pe.wait_ge(s["norm_ready"], g + 1)
                free_again(pe, s["img_ready"], g, 1)
                mm(bank[4][:, 0:GI], dense[:, :], s_d[:, par % 2, 0:GI]).then_inc(s["dense_mm"], 1)

            pipelined(pe, NG, [(0, conv), (1, centre_y), (2, variance), (3, spread), (4, dense_mm)], unroll=RING)

            pe.wait_ge(s["img_ready"], NG)

            def centre_h(g, par):
                if not fixed(g) or g >= 1:
                    pe.wait_ge(s["ctr1_ready"], 2 * g)
                mm(bank[0][:, 0:GS], centre[:, :], hT[:, cols_of(g, GS)]).then_inc(s["ctr1_mm"], 1)

            def variance1(g, par):
                pe.wait_ge(s["ctr1_ready"], 2 * g + 2)
                if not fixed(g) or g >= 1:
                    pe.wait_ge(s["root1_ready"], 2 * g)
                for j in range(GB):
                    last = mm(bank[1][0:S, j:j + 1], s_c[:, par, j * S:(j + 1) * S], c128[:, 0:1])
                last.then_inc(s["var1_mm"], 1)

            def spread1(g, par):
                pe.wait_ge(s["recip1_ready"], g + 1)
                free_again(pe, s["nx1_ready"], g, 1)
                for a in range(2):
                    for j in range(GB):
                        last = mm(bank[2 + a][:, j * S:(j + 1) * S],
                                  recips[0:S, par, a * GB + j:a * GB + j + 1].broadcast_to([S, P]),
                                  ident[0:S, 0:S])
                last.then_inc(s["spread1_mm"], 1)

            pipelined(pe, NG, [(0, centre_h), (1, variance1), (2, spread1)])

            pe.wait_ge(s_ld["attn"], 16 * 6)

            def gate_mm(g, par):
                pe.wait_ge(s["nx1_ready"], g + 1)
                if not fixed(g) or g >= 2:
                    pe.wait_ge(s["gate_ready"], 2 * g - 2)
                mm(bank[4 + par][:, 0:GS], expand[:, 2 * P:3 * P], nxT[:, cols_of(g, GS)])
                mm(bank[6 + par][:, 0:GS], expand[:, 3 * P:4 * P], nxT[:, cols_of(g, GS)]
                   ).then_inc(s["pre_mm"], 1)

            pipelined(pe, NG, [(0, gate_mm)])

            pe.wait_ge(s["gate_ready"], 2 * NG)

            def qk_lin(g, par):
                here = nxT[:, cols_of(g, GS)]
                free_again(pe, s["q_ready"], g, 1)
                free_again(pe, s["k_ready"], g, 1)
                mm(bank[0][0:64, 0:GS], expand[:, 4 * P:4 * P + 64], here).then_inc(s["qk_mm"], 1)
                free_again(pe, s["vT_ready"], g, 1)
                mm(bank[1][:, 0:GS], expand[:, 0:P], here)
                mm(bank[2][:, 0:GS], expand[:, P:2 * P], here).then_inc(s["lin_mm"], 1)

            def values_scores(g, par):
                pe.wait_ge(s["vT_ready"], g + 1)
                free_again(pe, s["v_ready"], g, 1)
                for j in range(GB):
                    last = pe.transpose(bank[3][0:S, j * D:(j + 1) * D], s_b[:, par, j * S:(j + 1) * S], ident[:, :])
                last.then_inc(s["vt_mm"], 1)
                pe.wait_ge(s["q_ready"], g + 1)
                pe.wait_ge(s["k_ready"], g + 1)
                if not fixed(g) or g >= 1:
                    pe.wait_ge(s["soft_step"], 2 * g - 1)
                for j in range(GB):
                    at = slice(j * S, (j + 1) * S)
                    last = mm(bank[4][0:S, at], s_a[0:QK, par, at], s_f[0:QK, par, at])
                last.then_inc(s["s_mm"], 1)

            def turn_probs(g, par):
                pe.wait_ge(s["p_ready"], g + 1)
                free_again(pe, s["pp_ready"], g, 1)
                for j in range(GB):
                    at = slice(j * S, (j + 1) * S)
                    last = pe.transpose(bank[5][0:S, at], s_g[0:S, par, at], ident[0:S, 0:S])
                last.then_inc(s["pp_mm"], 1)

            def attend(g, par):
                pe.wait_ge(s["pp_ready"], g + 1)
                pe.wait_ge(s["v_ready"], g + 1)
                free_again(pe, s["at_ready"], g, 1)
                for j in range(GB):
                    at = slice(j * S, (j + 1) * S)
                    last = mm(bank[6][:, at], s_v[0:S, par, j * D:(j + 1) * D], s_c[0:S, par, at])
                last.then_inc(s["av_mm"], 1)

            def project_mm(g, par):
                pe.wait_ge(s["at_ready"], g + 1)
                free_again(pe, s["h2_ready"], g, 1)
                mm(bank[7][:, 0:GS], project[:, 0, :], gate_loc[:, cols_of(g, GS)], True, False)
                mm(bank[7][:, 0:GS], project[:, 1, :], s_e[:, par], False, True).then_inc(s["out_mm"], 1)

            pipelined(pe, NG, [(0, qk_lin), (1, values_scores), (3, turn_probs), (4, attend), (5, project_mm)])

            pe.wait_ge(s["h2_ready"], NG)
            pe.wait_ge(s["sig_ready"], 1)

            def centre_2(g, par):
                if not fixed(g) or g >= 1:
                    pe.wait_ge(s["ctr2_ready"], 2 * g)
                mm(bank[0][:, 0:TT], centre[:, :], h2T[:, cols_of(g, TT)]).then_inc(s["ctr2_mm"], 1)

            def variance2(g, par):
                pe.wait_ge(s["ctr2_ready"], 2 * g + 2)
                if not fixed(g) or g >= 1:
                    pe.wait_ge(s["root2_ready"], 2 * g)
                for j in range(2):
                    last = mm(bank[1][:, j:j + 1], s_c[:, par, j * P:(j + 1) * P], c128[:, 0:1])
                last.then_inc(s["var2_mm"], 1)

            def spread2(g, par):
                pe.wait_ge(s["recip2_ready"], g + 1)
                free_again(pe, s["x2_ready"], g, 1)
                for a in range(2):
                    for j in range(2):
                        last = mm(bank[2 + a][:, j * P:(j + 1) * P],
                                  recips[:, par, 2 * a + j:2 * a + j + 1].broadcast_to([P, P]), ident[:, :])
                last.then_inc(s["spread2_mm"], 1)

            def turn_score(g, par):
                pe.wait_ge(s["xf_ready"], g + 1)
                pe.wait_ge(s["sign_ready"], g + 1)
                pe.wait_ge(s["res_ready"], g + 1)
                free_again(pe, s["res_out"], g, 1)
                if not fixed(g) or g >= 1:
                    pe.wait_ge(s["key_step"], 2 * g - 1)
                for j in range(2):
                    at = slice(j * P, (j + 1) * P)
                    mm(bank[6][:, j * E:(j + 1) * E], signs[:, par, at], w_cl[:, :], True, False)
                    mm(bank[6][:, j * E:(j + 1) * E], signs[:, par, at], w_tile[:, :], False, True
                       ).then_inc(s["score_mm"], 1)
                for j in range(2):
                    at = slice(j * P, (j + 1) * P)
                    pe.transpose(bank[4][:, at], s_a[:, par, at], ident[:, :])
                    last = pe.transpose(bank[5][:, at], s_e[:, par, at], ident[:, :])
                last.then_inc(s["turn_mm"], 1)

            pipelined(pe, NT2, [(0, centre_2), (1, variance2), (2, spread2), (3, turn_score)])

            pe.wait_ge(s["cnt_ready"], 1)
            pe.wait_ge(s_ld["route"], 16 * 6)
            mm(bank[0][0:E, 0:1], cnt[:, :], ones_bf[:, 0:1]).then_inc(s["route_mm"], 1)
            pe.wait_ge(s["route_dve"], 3)
            mm(bank[1][:, 0:E], ntile[:, 1:2].broadcast_to([E, P]), before[0:E, 0:E], True, False)
            mm(bank[1][:, 0:E], before[:, :], cnt[:, :], False, True)
            mm(bank[2][0:E, 0:1], upto[:, :], ntile[:, 0:1]).then_inc(s["route_mm"], 1)
            pe.wait_ge(s["route_dve"], 5)
            mm(bank[3][:, 0:NTILE], ones_bf[0:E, :], started[:, :]).then_inc(s["route_mm"], 1)

            pe.wait_ge(s["res_out"], NT2)

            def turn_rows(g, par):
                pe.wait_ge(s_rows[par], (g - par) * 8 + 16)
                free_again(pe, s["x3_ready"], g, 1)
                for a in range(2):
                    last = pe.transpose(bank[0][:, a * P:(a + 1) * P], rows_in[:, par, a, :], ident[:, :])
                last.then_inc(s["turn3_mm"], 1)

            def down(g, par):
                pe.wait_ge(s_wts[par], (g - par) * 8 * TI + 16 * TI)
                pe.wait_ge(s["x3_ready"], g + 1)
                free_again(pe, s["cell_ready"], g, 1)
                for j in range(TI):
                    at = slice(j * ST, (j + 1) * ST)
                    last = mm(bank[1][:, at], wts[:, par, j, 0:D], s_a[:, par, at])
                last.then_inc(s["h3_mm"], 1)

            def up(g, par):
                pe.wait_ge(s["spline_ready"], g + 1)
                free_again(pe, s["y_ready"], g, 1)
                for j in range(TI):
                    a, q = j // 4, j % 4
                    last = mm(bank[2][q * ST:(q + 1) * ST, a * D:(a + 1) * D],
                              s_c[:, par, j * ST:(j + 1) * ST], wts[:, par, j, D:2 * D])
                last.then_inc(s["y_mm"], 1)

            pipelined(pe, NI, [(0, turn_rows), (0, down), (1, up)])

        @block.vector
        def _(dve):
            dve.wait_ge(s["mask_ready"], 1)
            dve.tensor_tensor(mask[:, :], mask[:, :], causal[:, :], ALU.mult).then_inc(s["setup_step"], 1)
            dve.wait_ge(s["setup_step"], 1)
            dve.tensor_tensor(mask[:, :], mask[:, :], veil[:, :], ALU.add).then_inc(s["setup_step"], 1)
            dve.wait_ge(s_ld["text"], 16 * 6)
            dve.tensor_scalar(is0[:, :], x_col[:, :], 0.0, None, ALU.is_equal).then_inc(s["setup_step"], 1)
            dve.tensor_scalar(not0[:, :], x_col[:, :], 0.0, None, ALU.not_equal).then_inc(s["setup_step"], 1)
            dve.wait_ge(s["setup_step"], 4)

            dve.memset(s_d[:, :, BINS:P], 0.0).then_inc(s["setup_step"], 1)
            dve.wait_ge(s["setup_step"], 5)

            def top(g, par):
                dve.wait_ge(s["sim_mm"], g + 1)
                dve.tensor_reduce(small[:, par, 0:1], bank[1][:, 0:NB], AX.X, ALU.max, negate=True
                                  ).then_inc(s["top_ready"], 1)

            def probs(g, par):
                dve.wait_ge(s["exp_ready"], g + 1)
                free_again(dve, s["pt_mm"], g, 2)
                dve.reciprocal(small[:, par, 2:3], small[:, par, 1:2]).then_inc(s["prob_step"], 1)
                dve.tensor_copy(s_d[:, par, 0:1], is0[:, bass.ds(g, 1)]).then_inc(s["prob_step"], 1)
                dve.tensor_copy(small[:, par, 3:4], not0[:, bass.ds(g, 1)]).then_inc(s["prob_step"], 1)
                dve.wait_ge(s["prob_step"], 3 * g + 3)
                dve.tensor_scalar(s_d[:, par, 1:BINS], s_c[:, par, 0:NB], small[:, par, 2:3],
                                  small[:, par, 3:4], ALU.mult, ALU.mult).then_inc(s["prob_ready"], 1)

            def p_out(g, par):
                dve.wait_ge(s["pt_mm"], g + 1)
                free_again(dve, s["emb_mm"], g, 2)
                dve.tensor_copy(s_e[0:BINS, par, 0:GT], bank[2][0:BINS, 0:GT]).then_inc(s["pt_ready"], 1)

            pipelined(dve, NG, [(1, top), (1, probs), (2, p_out)])

            dve.wait_ge(s_ld["image"], 32)
            for k in range(1, 5):
                if k > 1:
                    dve.wait_ge(s["fold_step"], k - 1)
                dve.tensor_tensor(w5[:, 0, :], w5[:, 0, :], w5[:, k, :], ALU.add
                                  ).then_inc(s["fold_step"] if k < 4 else s["fold_done"], 1)
            dve.wait_ge(s["bias_mm"], 1)
            dve.tensor_tensor(dense_bias[:, :], bank[7][:, 0:1], col("dense_b"), ALU.add
                              ).then_inc(s["bias_ready"], 1)

            def recip(g, par):
                dve.wait_ge(s["root_ready"], g + 1)
                free_again(dve, s["spread_mm"], g, 2)
                dve.reciprocal(recips[0:HI, par, 0:2], roots[0:HI, par, 0:2]).then_inc(s["recip_ready"], 1)

            def norm(g, par):
                dve.wait_ge(s["spread_mm"], g + 1)
                dve.wait_ge(s["ctr_ready"], 2 * g + 2)
                free_again(dve, s["dense_mm"], g, 2)
                dve.scalar_tensor_tensor(out=s_d[:, par, 0:GI], in0=s_b[:, par, 0:GI], scalar=col("tok_gamma"),
                                         in1=bank[3][:, 0:GI], op0=ALU.mult, op1=ALU.mult
                                         ).then_inc(s["norm_ready"], 1)

            pipelined(dve, NG, [(2, recip), (3, norm)])

            dve_sig = sig_sum[:, :]
            for c in range(E // SIG_C):
                dve.wait_ge(s_sig[c % 2], 16 * (c // 2 + 1))
                dve.tensor_reduce(dve_sig[:, c * SIG_C:(c + 1) * SIG_C], sig_buf[:, c % 2], AX.X, ALU.add
                                  ).then_inc(s["sig_red"], 1)
            dve.wait_ge(s["sig_red"], E // SIG_C)

            def sign_of(dst, src, scratch):
                n = sign_of.n
                dve.tensor_scalar(scratch, src, 0.0, None, ALU.is_lt).then_inc(s["sig_step"], 1)
                dve.tensor_scalar(dst, src, 0.0, None, ALU.is_gt).then_inc(s["sig_step"], 1)
                dve.wait_ge(s["sig_step"], n + 2)
                dve.tensor_tensor(dst, dst, scratch, ALU.subtract).then_inc(s["sig_step"], 1)
                dve.wait_ge(s["sig_step"], n + 3)
                sign_of.n = n + 4
            sign_of.n = 0
            scr = keys[:, 0, 0:E]
            sign_of(sig_tile[:, :], sig_sum[:, :], scr)
            dve.tensor_reduce(sig_clsum[:, :], sig_tile[:, :].rearrange("p (c j) -> p c j", j=TPC), AX.X,
                              ALU.add).then_inc(s["sig_step"], 1)
            dve.wait_ge(s["sig_step"], 4)
            sign_of(sig_cl[:, :], sig_clsum[:, :], scr[:, 0:CL])
            dve.tensor_scalar(w_tile[:, :], sig_tile[:, :], float(TPC), None, ALU.mult).then_inc(s["sig_step"], 1)
            dve.tensor_scalar(w_cl[:, :].rearrange("p (c j) -> p c j", j=TPC),
                              spread_to(sig_cl[:, :], 2, TPC), CL * 4096.0, None, ALU.mult
                              ).then_inc(s["sig_ready"], 1)
            dve.wait_ge(s["sig_ready"], 1)

            def recip1(g, par):
                dve.wait_ge(s["root1_ready"], 2 * g + 2)
                free_again(dve, s["spread1_mm"], g, 2)
                dve.reciprocal(recips[0:S, par, :], roots[0:S, par, :]).then_inc(s["recip1_ready"], 1)

            def norm1(g, par):
                dve.wait_ge(s["spread1_mm"], g + 1)
                dve.wait_ge(s["ctr1_ready"], 2 * g + 2)
                free_again(dve, s["hx_ready"], g, 2)
                dve.tensor_tensor(s_d[:, par], s_b[:, par], bank[2][:, 0:GS], ALU.mult).then_inc(s["x1_ready"], 1)
                dve.tensor_tensor(nxT[:, cols_of(g, GS)], s_b[:, par], bank[3][:, 0:GS], ALU.mult
                                  ).then_inc(s["nx1_ready"], 1)

            pipelined(dve, NG, [(1, recip1), (2, norm1)])

            dve.wait_ge(s["hx_ready"], NG)

            def kv(g, par):
                dve.wait_ge(s["qk_mm"], g + 1)
                free_again(dve, s["s_mm"], g, 2)
                dve.tensor_copy(s_f[0:QK, par], bank[0][KOFF:KOFF + QK, 0:GS]).then_inc(s["k_ready"], 1)
                dve.wait_ge(s["lin_mm"], g + 1)
                loc = gate_loc[:, cols_of(g, GS)]
                dve.tensor_tensor(loc, loc, bank[1][:, 0:GS], ALU.mult).then_inc(s["loc_ready"], 1)
                free_again(dve, s["vt_mm"], g, 2)
                dve.tensor_tensor(s_b[:, par], gate_v[:, cols_of(g, GS)], bank[2][:, 0:GS], ALU.mult
                                  ).then_inc(s["vT_ready"], 1)

            def shifted(g, par):
                dve.wait_ge(s["s_mm"], g + 1)
                x = s_d[0:S, par].rearrange("p (b k) -> p b k", k=S)
                free_again(dve, s["p_ready"], g, 2)
                dve.scalar_tensor_tensor(out=x, in0=bank[4][0:S, 0:GS].rearrange("p (b k) -> p b k", k=S),
                                         scalar=float(QK) ** -0.5,
                                         in1=spread_to(mask[:, :], 1, GB),
                                         op0=ALU.mult, op1=ALU.add).then_inc(s["soft_step"], 1)
                dve.wait_ge(s["soft_step"], 2 * g + 1)
                dve.tensor_reduce(small[0:S, par, 0:GB], x, AX.X, ALU.max).then_inc(s["soft_step"], 1)
                dve.wait_ge(s["soft_step"], 2 * g + 2)
                dve.tensor_tensor(x, x, spread_to(small[0:S, par, 0:GB], 2, S), ALU.subtract
                                  ).then_inc(s["shifted_ready"], 1)

            def normalised(g, par):
                dve.wait_ge(s["expd_ready"], g + 1)
                x = s_d[0:S, par].rearrange("p (b k) -> p b k", k=S)
                dve.tensor_reduce(small[0:S, par, 4:8], x, AX.X, ALU.add).then_inc(s["sum_step"], 1)
                dve.wait_ge(s["sum_step"], 2 * g + 1)
                dve.reciprocal(small[0:S, par, 4:8], small[0:S, par, 4:8]).then_inc(s["sum_step"], 1)
                dve.wait_ge(s["sum_step"], 2 * g + 2)
                free_again(dve, s["pp_mm"], g, 2)
                dve.tensor_tensor(s_g[0:S, par].rearrange("p (b k) -> p b k", k=S), x,
                                  spread_to(small[0:S, par, 4:8], 2, S), ALU.mult
                                  ).then_inc(s["p_ready"], 1)

            def add_out(g, par):
                dve.wait_ge(s["out_mm"], g + 1)
                dve.wait_ge(s["hx_ready"], g + 1)
                dve.tensor_tensor(h2T[:, cols_of(g, GS)], hT[:, cols_of(g, GS)], bank[7][:, 0:GS], ALU.add
                                  ).then_inc(s["h2_ready"], 1)

            pipelined(dve, NG, [(0, kv), (1, shifted), (2, normalised), (5, add_out)])

            def recip2(g, par):
                dve.wait_ge(s["root2_ready"], 2 * g + 2)
                free_again(dve, s["spread2_mm"], g, 2)
                dve.reciprocal(recips[:, par, 0:4], roots[:, par, 0:4]).then_inc(s["recip2_ready"], 1)

            def norm2(g, par):
                dve.wait_ge(s["spread2_mm"], g + 1)
                dve.wait_ge(s["ctr2_ready"], 2 * g + 2)
                free_again(dve, s["res_ready"], g, 2)
                dve.tensor_tensor(s_d[:, par, 0:TT], s_b[:, par, 0:TT], bank[2][:, 0:TT], ALU.mult)
                free_again(dve, s["xf_ready"], g, 2)
                dve.tensor_tensor(s_v[:, par, 0:TT], s_b[:, par, 0:TT], bank[3][:, 0:TT], ALU.mult
                                  ).then_inc(s["x2_ready"], 1)

            def choose(g, par):
                dve.wait_ge(s["score_mm"], 2 * g + 2)
                key = keys[:, par].rearrange("p (i e) -> p i e", e=E)
                dve.tensor_tensor(key, bank[6][:, 0:2 * E].rearrange("p (i e) -> p i e", e=E),
                                  spread_to(tie[:, :], 1, 2), ALU.add).then_inc(s["key_step"], 1)
                dve.wait_ge(s["key_step"], 2 * g + 1)
                dve.tensor_reduce(best[:, par], key, AX.X, ALU.max).then_inc(s["key_step"], 1)
                dve.wait_ge(s["key_step"], 2 * g + 2)
                dve.tensor_tensor(onehot[:, :, bass.ds(g * 2, 2)].rearrange("p e i -> p i e"), key,
                                  spread_to(best[:, par], 2, E), ALU.is_equal).then_inc(s["choice_ready"], 1)

            dve.wait_ge(s_ld["route"], 16 * 6)
            pipelined(dve, NT2, [(1, recip2), (2, norm2), (3, choose)])

            dve.wait_ge(s["choice_ready"], NT2)
            with nc.allow_low_precision("counts up to T are exact in bfloat16"):
                dve.tensor_reduce(cnt[:, :], onehot, AX.X, ALU.add).then_inc(s["cnt_ready"], 1)
            flat = hT[:, 0:E * T]
            dve.tensor_tensor_scan(upto_here, flat, flat, 0.0, ALU.add, ALU.max).then_inc(s["scan_ready"], 1)
            dve.wait_ge(s["route_mm"], 1)
            dve.tensor_scalar(tot_i[:, 0:1], bank[0][0:E, 0:1], float(ST - 1), None, ALU.add
                              ).then_inc(s["route_dve"], 1)
            dve.wait_ge(s["route_dve"], 1)
            dve.tensor_scalar(tot_i[:, 1:2], tot_i[:, 0:1], ST.bit_length() - 1, None, ALU.arith_shift_right
                              ).then_inc(s["route_dve"], 1)
            dve.wait_ge(s["route_dve"], 2)
            dve.tensor_copy(ntile[:, 0:1], tot_i[:, 1:2])
            dve.tensor_scalar(ntile[:, 1:2], tot_i[:, 1:2], float(ST), None, ALU.mult).then_inc(s["route_dve"], 1)
            dve.wait_ge(s["route_mm"], 2)
            dve.tensor_copy(ends[:, :], bank[2][0:E, 0:1]).then_inc(s["route_dve"], 1)
            dve.wait_ge(s["route_dve"], 4)
            dve.tensor_scalar(started[:, :], tile_no[:, :], ends[:, 0:1], None, ALU.is_ge
                              ).then_inc(s["route_dve"], 1)
            dve.wait_ge(s["scan_ready"], 1)
            ends_here = upto_here.rearrange("p (e i) -> p e i", i=T)[:, 0:E - 1, T - 1]
            dve.tensor_copy(base[:, 0:1], bank[1][:, 0:1]).then_inc(s["place_step"], 1)
            dve.tensor_tensor(base[:, 1:E], bank[1][:, 1:E], ends_here, ALU.subtract).then_inc(s["place_step"], 1)
            dve.wait_ge(s["place_step"], 2)
            def by_expert(ap):
                return ap.rearrange("p (e i) -> p e i", i=T)
            dve.tensor_tensor(by_expert(place_of), by_expert(upto_here), spread_to(base[:, :], 2, T), ALU.add
                              ).then_inc(s["place_step"], 1)
            dve.wait_ge(s["place_step"], 3)
            dve.tensor_tensor(weighed, place_of, flat, ALU.mult).then_inc(s["place_step"], 1)
            dve.wait_ge(s["place_step"], 4)
            dve.tensor_reduce(slot_f[:, :], by_expert(weighed).rearrange("p e i -> p i e"), AX.X, ALU.add
                              ).then_inc(s["place_step"], 1)
            dve.wait_ge(s["place_step"], 5)
            dve.tensor_scalar(slot_i[:, :], slot_f[:, :], -1.0, None, ALU.add).then_inc(s["slots_ready"], 1)
            dve.wait_ge(s["route_mm"], 3)
            dve.tensor_scalar(owner[:, :], bank[3][:, 0:NTILE], float(E - 1), None, ALU.min
                              ).then_inc(s["owner_ready"], 1)
            dve.tensor_tensor(by_expert(weighed), onehot, spread_to(scale_row[:, :], 2, T), ALU.mult
                              ).then_inc(s["scale_step"], 1)
            dve.wait_ge(s["scale_step"], 1)
            dve.tensor_reduce(scale_tok[:, :], by_expert(weighed).rearrange("p e i -> p i e"), AX.X, ALU.add
                              ).then_inc(s["scale_step"], 1)

            LEVELS = GRID.bit_length() - 1

            def predicated_after(count):
                dve.wait_ge(s["look_step"], count)
                dve.sem_inc(s["wait_carried"], 1)

            def spline(g, par):
                dve.wait_ge(s["fill_ready"], 2 * g + 2)
                dve.wait_ge(s["cell_ready"], g + 1)
                left = s_b[:, par, 0:SI]
                steps = 2 * LEVELS + 5
                for b in range(LEVELS):
                    half = 0.5 ** (b + 1)
                    bit = bits[:, par, LEVELS - 1 - b, :]
                    dve.tensor_scalar(bit, left, half, None, ALU.is_ge).then_inc(s["look_step"], 1)
                    dve.wait_ge(s["look_step"], steps * g + 2 * b + 1)
                    dve.scalar_tensor_tensor(out=rem[:, b], in0=bit, scalar=-half, in1=left, op0=ALU.mult,
                                             op1=ALU.add).then_inc(s["look_step"], 1)
                    dve.wait_ge(s["look_step"], steps * g + 2 * b + 2)
                    left = rem[:, b]
                done = steps * g + 2 * LEVELS
                predicated_after(done)
                for a in range(2):
                    tab = wts[:, par, :, 2 * D + a * GRID + 1:2 * D + (a + 1) * GRID:2]
                    last = dve.copy_predicated(
                        look[:, par, a].rearrange("p k (j n) -> p k j n", n=ST),
                        spread_to(bits[:, par, 0, :].rearrange("p (j n) -> p j n", n=ST), 1, GRID // 2).bitcast(I32),
                        spread_to(tab.rearrange("p j k -> p k j"), 3, ST))
                last.then_inc(s["look_step"], 1)
                predicated_after(done + 1)
                for b in range(1, LEVELS):
                    step = 1 << b
                    both = look[:, par].rearrange("p a k n -> p (a k) n")
                    lo, hi = both[:, 0::step, :], both[:, step // 2::step, :]
                    dve.copy_predicated(lo, spread_to(bits[:, par, b, :], 1, lo.shape[1]).bitcast(I32), hi
                                        ).then_inc(s["look_step"], 1)
                    if b < LEVELS - 1:
                        predicated_after(done + 1 + b)
                dve.wait_ge(s["look_step"], done + LEVELS)
                dve.scalar_tensor_tensor(out=rem[:, LEVELS], in0=look[:, par, 1, 0], scalar=float(GRID), in1=left,
                                         op0=ALU.mult, op1=ALU.mult).then_inc(s["look_step"], 1)
                dve.wait_ge(s["look_step"], done + LEVELS + 1)
                free_again(dve, s["y_mm"], g, 2)
                dve.tensor_tensor(s_c[:, par, 0:SI], look[:, par, 0, 0], rem[:, LEVELS], ALU.add
                                  ).then_inc(s["spline_ready"], 1)

            pipelined(dve, NI, [(1, spline)])

            dve.wait_ge(s["res_out"], NT2)
            dve.wait_ge(s["scale_step"], 2)
            for i in range(T):
                dve.wait_ge(s_fetch[i % YR], 16 * (i // YR + 1))
                dve.scalar_tensor_tensor(out=res_tok[:, i, :], in0=rows_out[:, i % YR, 0:D],
                                         scalar=scale_tok[:, i:i + 1], in1=res_tok[:, i, :],
                                         op0=ALU.mult, op1=ALU.add).then_inc(s["final_out"], 1)


def _layout(x, x_txt, L0_tok_conv_w, L0_tok_conv_b, L0_tok_gamma, L0_tok_beta, L0_tok_dense_w, L0_tok_dense_b,
            L0_txt_bin_embeddings, L0_txt_w1, L0_txt_b1, L0_txt_w2, L0_txt_b2, L0_attn_expand, L0_attn_project,
            L0_attn_position_bias_mult, L0_ffn_gamma, L0_ffn_beta, L0_ffn_Wd, L0_ffn_spline_bases,
            L0_ffn_spline_slopes, L0_ffn_Wu, L0_ffn_scale):
    a = np.asarray
    keep = [i * WIN + j for i in range(WIN) for j in range(WIN)
            if not (i in (0, WIN - 1) and j in (0, WIN - 1))]
    px = np.pad(a(x), ((0, 0), (1, 1), (1, 1), (0, 0)))
    rows = [px[:, i:i + IMG:PATCH, j:j + IMG:PATCH, :][:, 0:GRID_W, 0:GRID_W] for i in range(WIN) for j in range(WIN)]
    win = np.stack([rows[k] for k in keep])
    win = win.transpose(0, 4, 1, 2, 3).reshape(KCH, KP, NG, GI)
    patches = np.ascontiguousarray(win.transpose(2, 1, 0, 3))
    w = a(L0_tok_conv_w)
    w5 = np.zeros((5, WIN, WIN, CH, D), np.float32)
    for k, (di, dj) in enumerate(((0, 0), (0, -1), (0, 1), (-1, 0), (1, 0))):
        w5[k, 1 + di:1 + di + PATCH, 1 + dj:1 + dj + PATCH] = w[:, :, k * CH:(k + 1) * CH, :]
    w5 = w5.reshape(5, WIN * WIN, CH, D)[:, keep].reshape(5, KCH, KP, D)
    w5 = np.ascontiguousarray(w5.transpose(2, 0, 1, 3)).reshape(KP, 5, KCH * D)
    bins = a(L0_txt_bin_embeddings)
    vectors = (a(L0_txt_w1)[0], L0_txt_b1, L0_txt_b2, L0_tok_conv_b, L0_tok_gamma, L0_tok_beta, L0_tok_dense_b,
               L0_ffn_gamma, L0_ffn_beta)
    ex = a(L0_attn_expand)
    qk = np.zeros((D, 64), np.float32)
    qk[:, 0:QK] = ex[:, 0:QK]
    qk[:, KOFF:KOFF + QK] = ex[:, QK:2 * QK]
    expand = np.concatenate([ex[:, 2 * QK:], qk], axis=1)
    packs = np.concatenate([a(L0_ffn_Wd).transpose(0, 2, 1), a(L0_ffn_Wu).transpose(0, 2, 1),
                            a(L0_ffn_spline_bases), a(L0_ffn_spline_slopes)], axis=2)
    at = np.arange(S)
    e = np.arange(E)
    bf = mybir.dt.np(BF16)
    return dict(
        patches=patches, w5=w5, w2=a(L0_txt_w2), bins=bins, bins_t=bins[1:].T, cols=np.stack([a(v) for v in vectors], 1),
        x_row=a(x_txt).reshape(B * S_TXT), x_col=a(x_txt).reshape(NG, GT).T, dense=a(L0_tok_dense_w),
        expand=expand, project=a(L0_attn_project).reshape(2, P, D).transpose(1, 0, 2),
        pbm=a(L0_attn_position_bias_mult).reshape(1), scale=a(L0_ffn_scale), packs=packs,
        ident=np.eye(P, dtype=np.float32),
        centre=(np.eye(P) - 1.0 / P).astype(np.float32),
        c128=np.tile(np.array([1.0 / P, 1.0], np.float32), (P, 1)),
        eps=np.tile(np.array([EPS_TOK, EPS, EPS * EPS], np.float32), (P, 1)),
        rel=(at[None, :] - at[:, None]).astype(np.float32),
        causal=(at[None, :] <= at[:, None]).astype(np.float32),
        veil=np.where(at[None, :] <= at[:, None], 0.0, -HUGE).astype(np.float32),
        before=np.triu(np.ones((P, P)), 1).astype(bf), upto=np.triu(np.ones((E, E))).astype(bf),
        ones_bf=np.ones((P, P)).astype(bf),
        tie=np.tile(((CL - 1 - e // TPC) * 4096 + (TPC - 1 - e % TPC)).astype(np.float32), (P, 1)),
        tile_no=np.tile(np.arange(NTILE, dtype=np.float32), (E, 1)),
    )


def kernel(**inputs):
    import concourse.bacc as bacc
    from concourse.bass_utils import run_bass_kernel_spmd

    arrays = {f"in_{k}": np.ascontiguousarray(v) for k, v in _layout(**inputs).items()}
    nc = bacc.Bacc("TRN2", target_bir_lowering=False, num_devices=1)
    t = {k[3:]: nc.dram_tensor(k, v.shape, mybir.dt.from_np(v.dtype), kind="ExternalInput").ap()
         for k, v in arrays.items()}
    out = nc.dram_tensor("out", (N, D), F32, kind="ExternalOutput").ap()
    build(nc, t, out)
    r = run_bass_kernel_spmd(nc, [arrays], core_ids=[0])
    return r.results[0]["out"].reshape(B, S, D)
```

```python
from contextlib import ExitStack

import numpy as np

import concourse.bass as bass
from concourse import mybir

F32 = mybir.dt.float32
BF16 = mybir.dt.bfloat16
I32 = mybir.dt.int32
ALU = mybir.AluOpType
ACT = mybir.ActivationFunctionType
AX = mybir.AxisListType

P = 128
D = 128
B = 64
IMG = 96
PATCH = 16
CH = 3
GRID_W = IMG // PATCH
S_IMG = GRID_W * GRID_W
S_TXT = 32
S = S_IMG + S_TXT
N = B * S
GB = 4
NG = B // GB
GI = GB * S_IMG
HI = GI // 2
GT = GB * S_TXT
GS = GB * S
WIN = PATCH + 2
KCH = 8
KP = (WIN * WIN - 4) * CH // KCH
BINS = 51
NB = BINS - 1
QK = 16
KOFF = 32
E = 64
CL = 8
TPC = E // CL
GRID = 16
T = N // P
TT = 2 * P
NT2 = N // TT
ST = 32
NTILE = -(-(E + (N - E) // ST) // 8) * 8
TI = 8
SI = TI * ST
NI = NTILE // TI
NI_SURE = -(-(N // ST) // TI)
SLOTS = NTILE * ST
WROW = 2 * D + 2 * GRID
SIG_C = E // NG
EPS_TOK = 1e-3
EPS = 1e-5
HUGE = 3.0e38
RING = 4
WR = 4
ROW = 2 * D + 2
TOK, SCL = 2 * D, 2 * D + 1


def fixed(g):
    return isinstance(g, int)


def pipelined(eng, n, stages, unroll=2, sure=None):
    stages = sorted(stages, key=lambda at: -at[0])
    depth = stages[0][0]
    head = -(-(depth + unroll) // unroll) * unroll
    rest = ((sure or n) - head) // unroll * unroll + head

    def peeled(i):
        for lag, stage in stages:
            if 0 <= i - lag < n:
                stage(i - lag, (i - lag) % unroll)

    for i in range(head):
        peeled(i)
    with eng.Fori(head // unroll, rest // unroll) as turn:
        for u in range(unroll):
            for lag, stage in stages:
                stage(turn * unroll + (u - lag), (u - lag) % unroll)
    for i in range(rest, n + depth):
        peeled(i)


def free_again(eng, sem, g, slots):
    if not fixed(g) or g >= slots:
        eng.wait_ge(sem, g - slots + 1)


def where_used(eng, tiles, stage):
    def run(g, par):
        if not fixed(g) or g < NI_SURE:
            stage(g, par)
        else:
            with eng.If(tiles > g * TI):
                stage(g, par)
    return run


def spread_to(ap, dim, count):
    ap = ap.unsqueeze(dim)
    return ap.broadcast_to([count if i == dim else n for i, n in enumerate(ap.shape)])


def build(nc, t, out):
    with ExitStack() as ctx:
        def sb(name, shape, dt=F32):
            return ctx.enter_context(nc.sbuf_tensor(name, shape, dt))

        def sem(name):
            return ctx.enter_context(nc.semaphore(name))

        bank = [ctx.enter_context(nc.psum_tensor(f"bank{i}", [P, 512], F32)) for i in range(8)]

        slots = nc.dram_tensor("slots", (SLOTS, ROW), F32).ap()

        ident = sb("ident", [P, P])
        centre = sb("centre", [P, P])
        c128 = sb("c128", [P, 2])
        before = sb("before", [P, P], BF16)
        upto = sb("upto", [E, E], BF16)
        ones_bf = sb("ones_bf", [P, P], BF16)
        tie = sb("tie", [P, E])
        tile_no = sb("tile_no", [E, NTILE])
        rel = sb("rel", [S, S])
        causal = sb("causal", [S, S])
        veil = sb("veil", [S, S])
        mask = sb("mask", [S, S])
        pbm = sb("pbm", [P, 1])
        eps = sb("eps", [P, 3])
        cols = sb("cols", [P, 9])
        w2 = sb("w2", [P, D])
        bins_t = sb("bins_t", [P, NB])
        bins = sb("bins", [BINS, D])
        x_col = sb("x_col", [GT, NG], I32)
        is0 = sb("is0", [GT, NG])
        not0 = sb("not0", [GT, NG])
        dense = sb("dense", [P, D])
        dense_bias = sb("dense_bias", [P, 1])
        expand = sb("expand", [P, 4 * P + 64])
        project = sb("project", [P, 2, D])
        scale_row = sb("scale_row", [P, E])

        hT = sb("hT", [P, N])
        nxT = sb("nxT", [P, N])
        gates_all = sb("gates_all", [P, T * ROW])
        gate_loc = gates_all[:, 0:N]
        gate_v = gates_all[:, N:2 * N]
        h2T = sb("h2T", [P, N])
        x_txt = h2T[:, 0:B * S_TXT].bitcast(I32)
        ctr1 = h2T
        ctr2 = nxT
        rows = gates_all[:, :].rearrange("p (i c) -> p i c", c=ROW)
        onehot = hT[:, 0:E * T].rearrange("p (e i) -> p e i", i=T)
        weighed = hT[:, E * T:2 * E * T]
        upto_here = nxT[:, 0:E * T]
        place_of = nxT[:, E * T:2 * E * T]

        big = sb("big", [P, RING * KCH * GI + 5 * KCH * D])
        patches = big[0:KP, 0:RING * KCH * GI].rearrange("p (r k n) -> p r k n", r=RING, k=KCH)
        w5 = big[0:KP, RING * KCH * GI:].rearrange("p (s k) -> p s k", s=5)
        LOOK = 2 * GRID // 2 * SI
        look = big[:, 0:2 * LOOK].rearrange("p (r a k n) -> p r a k n", r=2, a=2, k=GRID // 2)

        s_a = sb("s_a", [P, 2, GS])
        s_b = sb("s_b", [P, 2, GS])
        s_c = sb("s_c", [P, 2, GS])
        s_d = sb("s_d", [P, 2, GS])
        s_e = sb("s_e", [P, 2, GS])
        s_f = sb("s_f", [P, 2, GS])
        s_g = sb("s_g", [P, 2, GS])
        s_v = sb("s_v", [P, 2, GB * D])
        roots = sb("roots", [P, 2, 8])
        recips = sb("recips", [P, 2, 8])
        signs = sb("signs", [P, 2, TT], BF16)
        keys = sb("keys", [P, 2, 2 * E])
        best = sb("best", [P, 2, 2])
        small = sb("small", [P, 2, 8])

        sig_sum = sb("sig_sum", [P, E])
        sig_tile = sb("sig_tile", [P, E])
        sig_clsum = sb("sig_clsum", [P, CL])
        sig_cl = sb("sig_cl", [P, CL])
        w_tile = sb("w_tile", [P, E], BF16)
        w_cl = sb("w_cl", [P, E], BF16)
        cnt = sb("cnt", [P, E], BF16)
        tot_i = sb("tot_i", [E, 2], I32)
        ntile = sb("ntile", [E, 2], BF16)
        ends = sb("ends", [E, 1])
        started = sb("started", [E, NTILE], BF16)
        owner = sb("owner", [P, NTILE], I32)
        used = sb("used", [P, 1], I32)
        base = sb("base", [P, E])
        slot_f = sb("slot_f", [P, T])
        slot_i = sb("slot_i", [P, T], I32)
        token_no = sb("token_no", [P, T], I32)
        scaled = sb("scaled", [P, 2, 2 * E])

        wts = sb("wts", [P, WR, TI, WROW])
        rows_in = sb("rows_in", [P, WR, 2, ROW])
        blank = rows_in[:, :, :, :].rearrange("p r a c -> p (r a) c")
        rows_out = sb("rows_out", [P, 2, 2, D])
        bits = h2T[:, 0:4 * SI].bitcast(I32).rearrange("p (b n) -> p b n", n=SI)
        plus1 = h2T[:, 4 * SI:5 * SI]
        cell_at = h2T[:, 5 * SI:6 * SI]
        below = h2T[:, 6 * SI:7 * SI]
        inside = h2T[:, 7 * SI:8 * SI]

        s_ld = {k: sem(f"ld_{k}") for k in ("const", "text", "image", "attn", "route")}
        s_patch = [sem(f"patch{i}") for i in range(RING)]
        names = """conv_used fold_done fold_step setup_step mask_ready
            hid_ready enc_mm enc_ready sim_mm top_ready exp_ready prob_step prob_ready pt_mm pt_ready
            emb_mm emb_ready txt_cols
            conv_mm conv_ready ctr_mm ctr_ready var_mm root_ready recip_ready spread_mm norm_ready
            dense_mm img_ready bias_mm bias_ready
            ctr1_mm ctr1_ready var1_mm root1_ready recip1_ready spread1_mm x1_ready nx1_ready hx_ready
            pre_mm gate_ready
            qk_mm q_ready k_ready lin_mm loc_ready vT_ready vt_mm v_ready s_mm soft_step sum_step shifted_ready
            expd_ready p_ready pp_mm pp_ready av_mm at_ready out_mm h2_ready
            ctr2_mm ctr2_ready var2_mm root2_ready recip2_ready spread2_mm x2_ready res_ready xf_ready sign_ready
            turn_mm xf_out res_out score_mm key_step choice_ready
            sig_used sig_red sig_step sig_ready
            cnt_ready scan_ready place_step route_mm route_dve used_ready owner_ready slots_ready zero_set zero_filled scattered scale_step
            turn3_mm x3_ready h3_mm cell_ready fill_ready wait_carried look_step spline_ready y_mm y_ready
            row_ready row_waited scale_ready numbered blank_set""".split()
        s = {name: sem(name) for name in names}
        s_sig = [sem(f"sig{i}") for i in range(WR)]
        s_rows = [sem(f"rows{i}") for i in range(WR)]
        s_wts = [sem(f"wts{i}") for i in range(WR)]
        s_stored = [sem(f"stored{i}") for i in range(WR)]

        COLS = dict(w1=0, b1=1, b2=2, conv_b=3, tok_gamma=4, tok_beta=5, dense_b=6, ffn_gamma=7, ffn_beta=8)

        def col(name):
            return cols[:, COLS[name]:COLS[name] + 1]

        def cols_of(g, width):
            return bass.ds(g * width, width)

        sig_buf = wts[:, :, 0:SIG_C, 0:D]
        block = ctx.enter_context(nc.Block())

        @block.sync
        def _(sp):
            sp.dma_start(x_txt[:, :], t["x_row"].partition_broadcast(P)).then_inc(s_ld["text"], 16)
            for name, dst in (("cols", cols), ("w2", w2), ("bins_t", bins_t), ("x_col", x_col), ("bins", bins)):
                sp.dma_start(dst[:, :], t[name]).then_inc(s_ld["text"], 16)
            sp.dma_start(ident[:, :], t["ident"]).then_inc(s_ld["const"], 16)
            sp.dma_start(centre[:, :], t["centre"]).then_inc(s_ld["const"], 16)
            sp.dma_start(c128[:, :], t["c128"]).then_inc(s_ld["const"], 16)
            sp.dma_start(eps[:, :], t["eps"]).then_inc(s_ld["const"], 16)
            sp.dma_start(w5, t["w5"]).then_inc(s_ld["image"], 16)
            sp.dma_start(dense[:, :], t["dense"]).then_inc(s_ld["image"], 16)
            def load_sig(c):
                if c >= WR:
                    sp.wait_ge(s["sig_red"], c - WR + 1)
                sp.dma_start(sig_buf[:, c % WR],
                             t["packs"][c * SIG_C:(c + 1) * SIG_C, :, 0:D].rearrange("e p h -> p e h")
                             ).then_inc(s_sig[c % WR], 16)

            for c in range(WR):
                load_sig(c)
            for g in range(NG):
                if g == RING:
                    for c in range(WR, NG):
                        load_sig(c)
                if g >= RING:
                    sp.wait_ge(s["conv_mm"], g - RING + 1)
                sp.dma_start(patches[:, g % RING], t["patches"][g]).then_inc(s_patch[g % RING], 16)
            sp.wait_ge(s["owner_ready"], 1)
            sp.wait_ge(s["sig_red"], NG)

            def load_packs(g, par):
                free_again(sp, s["y_mm"], g, WR)
                for j in range(TI):
                    e = sp.value_load(owner[0:1, bass.ds(g * TI + j, 1)], min_val=0, max_val=E - 1)
                    sp.dma_start(wts[:, par, j, :], t["packs"][bass.ds(e, 1)].rearrange("e p w -> (e p) w")
                                 ).then_inc(s_wts[par], 16)

            def load_rows(g, par):
                if fixed(g) and g == 0:
                    sp.wait_ge(s["scattered"], 16 * T)
                if not fixed(g) or g >= WR:
                    sp.wait_ge(s_stored[par], (g - par) * (32 // WR))
                sp.dma_start(rows_in[:, par],
                             slots[bass.ds(g * SI, SI), :].rearrange("(a p) c -> p a c", p=P)
                             ).then_inc(s_rows[par], 16)

            sp.wait_ge(s["used_ready"], 1)
            tiles = sp.value_load(used[0:1, 0:1], min_val=NI_SURE * TI - TI + 1, max_val=NTILE)
            pipelined(sp, NI, [(0, where_used(sp, tiles, load_packs)), (1, where_used(sp, tiles, load_rows))],
                      unroll=WR, sure=NI_SURE)

            def stored(g, par):
                sp.wait_ge(s_stored[par], 32 * (g // WR + 1))

            for g in range(NI_SURE - WR, NI):
                where_used(sp, tiles, stored)(g, g % WR)

        @block.gpsimd
        def _(pool):
            for name, dst in (("before", before), ("upto", upto), ("ones_bf", ones_bf), ("tie", tie),
                              ("tile_no", tile_no), ("token_no", token_no)):
                pool.dma_start(dst[:, :], t[name]).then_inc(s_ld["route"], 16)
            pool.dma_start(scale_row[:, :], t["scale"].partition_broadcast(P)).then_inc(s_ld["route"], 16)

            pool.wait_ge(s_ld["image"], 32)
            for k in range(1, 5):
                if k > 1:
                    pool.wait_ge(s["fold_step"], k - 1)
                pool.tensor_tensor(w5[:, 0, :], w5[:, 0, :], w5[:, k, :], ALU.add
                                   ).then_inc(s["fold_step"] if k < 4 else s["fold_done"], 1)

            def add_norm(g, par):
                pool.wait_ge(s["x1_ready"], g + 1)
                here = hT[:, cols_of(g, TT)]
                pool.tensor_tensor(here, here, s_d[:, par, 0:TT], ALU.add).then_inc(s["hx_ready"], 1)

            pipelined(pool, NT2, [(3, add_norm)])

            pool.memset(blank, 0.0).then_inc(s["zero_set"], 1)
            pool.wait_ge(s["zero_set"], 1)
            pool.memset(blank[:, :, TOK:TOK + 1].bitcast(I32), N).then_inc(s["blank_set"], 1)
            pool.wait_ge(s["blank_set"], 1)
            some = P * 2 * WR
            for c in range(0, SLOTS, some):
                n = min(some, SLOTS - c)
                pool.dma_start(slots[c:c + n, :].rearrange("(p a) c -> p a c", p=P),
                               blank[:, 0:n // P, :]).then_inc(s["zero_filled"], 16)
            n_zero = -(-SLOTS // some)

            def add_res(g, par):
                pool.wait_ge(s["x2_ready"], g + 1)
                free_again(pool, s["turn_mm"], g, 2)
                pool.tensor_tensor(s_e[:, par, 0:TT], h2T[:, cols_of(g, TT)], s_d[:, par, 0:TT],
                                   ALU.add).then_inc(s["res_ready"], 1)

            pipelined(pool, NT2, [(4, add_res)])

            pool.wait_ge(s["zero_filled"], 16 * n_zero)
            pool.wait_ge(s["slots_ready"], 1)
            pool.wait_ge(s["res_out"], NT2)
            pool.wait_ge(s["scale_ready"], NT2)
            pool.wait_ge(s["numbered"], 1)
            for i in range(T):
                pool.indirect_dma_start(slots[:, :], bass.IndirectOffsetOnAxis(ap=slot_i[:, i:i + 1], axis=0),
                                        rows[:, i, :], None).then_inc(s["scattered"], 16)

            def store(g, par):
                pool.wait_ge(s["y_ready"], 2 * g + 2)
                here = rows_out[:, par % 2]
                pool.tensor_tensor(here, here, rows_in[:, par, :, D:2 * D], ALU.add).then_inc(s["row_ready"], 1)
                pool.wait_ge(s["row_ready"], g + 1)
                pool.sem_inc(s["row_waited"], 1)
                for a in range(2):
                    pool.indirect_dma_start(
                        out[:, :], bass.IndirectOffsetOnAxis(ap=rows_in[:, par, a, TOK:TOK + 1].bitcast(I32), axis=0),
                        here[:, a, :], None, bounds_check=N - 1, oob_is_err=False).then_inc(s_stored[par], 16)

            pool.wait_ge(s["used_ready"], 1)
            tiles = pool.value_load(used[0:1, 0:1], min_val=NI_SURE * TI - TI + 1, max_val=NTILE)
            pipelined(pool, NI, [(2, where_used(pool, tiles, store))], unroll=WR, sure=NI_SURE)

        @block.scalar
        def _(act):
            for name, dst in (("rel", rel), ("causal", causal), ("veil", veil), ("expand", expand)):
                act.dma_start(dst[:, :], t[name]).then_inc(s_ld["attn"], 16)
            act.dma_start(project[:, :, :], t["project"]).then_inc(s_ld["attn"], 16)
            act.dma_start(pbm[:, :], t["pbm"].partition_broadcast(P)).then_inc(s_ld["attn"], 16)
            act.wait_ge(s_ld["text"], 16 * 6)

            def hidden(g, par):
                free_again(act, s["enc_mm"], g, 2)
                act.activation(s_a[:, par, 0:GT], x_txt[:, cols_of(g, GT)], ACT.Relu, bias=col("b1"),
                               scale=col("w1")).then_inc(s["hid_ready"], 1)

            def encoded(g, par):
                act.wait_ge(s["enc_mm"], g + 1)
                free_again(act, s["sim_mm"], g, 2)
                act.activation(s_b[:, par, 0:GT], bank[0][:, 0:GT], ACT.Identity, bias=col("b2")
                               ).then_inc(s["enc_ready"], 1)

            def exps(g, par):
                act.wait_ge(s["top_ready"], g + 1)
                free_again(act, s["prob_ready"], g, 2)
                act.activation(s_c[:, par, 0:NB], bank[4 + par][:, 0:NB], ACT.Exp, bias=small[:, par, 0:1],
                               accum_out=small[:, par, 1:2]).then_inc(s["exp_ready"], 1)

            def embedded(g, par):
                act.wait_ge(s["emb_mm"], g + 1)
                act.activation(hT[:, cols_of(g, GS)].rearrange("p (b s) -> p b s", s=S)[:, :, S_IMG:S],
                               bank[3][:, 0:GT].rearrange("p (b s) -> p b s", s=S_TXT), ACT.Copy
                               ).then_inc(s["emb_ready"], 1)

            pipelined(act, NG, [(0, hidden), (1, encoded), (3, exps), (5, embedded)])

            def conv_out(g, par):
                act.wait_ge(s["conv_mm"], g + 1)
                free_again(act, s["ctr_mm"], g, 2)
                act.activation(s_a[:, par, 0:GI], bank[0][:, 0:GI], ACT.Identity, bias=col("conv_b")
                               ).then_inc(s["conv_ready"], 1)

            def centred(g, par):
                act.wait_ge(s["ctr_mm"], g + 1)
                free_again(act, s["norm_ready"], g, 2)
                act.activation(s_b[:, par, 0:GI], bank[1][:, 0:GI], ACT.Copy).then_inc(s["ctr_ready"], 1)
                act.activation(s_c[:, par, 0:GI], bank[1][:, 0:GI], ACT.Square).then_inc(s["ctr_ready"], 1)

            def root(g, par):
                act.wait_ge(s["var_mm"], g + 1)
                free_again(act, s["recip_ready"], g, 2)
                act.activation(roots[0:HI, par, 0:2], bank[2][0:HI, 0:2], ACT.Sqrt, bias=eps[0:HI, 0:1]
                               ).then_inc(s["root_ready"], 1)

            def image_out(g, par):
                act.wait_ge(s["dense_mm"], g + 1)
                act.activation(hT[:, cols_of(g, GS)].rearrange("p (b s) -> p b s", s=S)[:, :, 0:S_IMG],
                               bank[4][:, 0:GI].rearrange("p (b s) -> p b s", s=S_IMG), ACT.Identity,
                               bias=dense_bias[:, 0:1]).then_inc(s["img_ready"], 1)

            act.wait_ge(s_ld["attn"], 16 * 6)
            act.activation(mask[:, :], rel[:, :], ACT.Sigmoid, bias=pbm[0:S, :]).then_inc(s["mask_ready"], 1)
            act.wait_ge(s["bias_ready"], 1)
            act.wait_ge(s_ld["const"], 16 * 4)
            pipelined(act, NG, [(0, conv_out), (1, centred), (2, root), (4, image_out)])

            def centred1(g, par):
                act.wait_ge(s["ctr1_mm"], g + 1)
                act.activation(ctr1[:, cols_of(g, TT)], bank[0][:, 0:TT], ACT.Copy).then_inc(s["ctr1_ready"], 1)
                free_again(act, s["var1_mm"], g, 2)
                act.activation(s_c[:, par, 0:TT], bank[0][:, 0:TT], ACT.Square).then_inc(s["ctr1_ready"], 1)

            def root1(g, par):
                act.wait_ge(s["var1_mm"], g + 1)
                free_again(act, s["recip1_ready"], g, 2)
                v = bank[1][:, 0:2]
                act.activation(roots[:, par, 0:2], v, ACT.Sqrt, bias=eps[:, 1:2]).then_inc(s["root1_ready"], 1)
                act.activation(roots[:, par, 2:4], v, ACT.Sqrt, bias=eps[:, 2:3], scale=1.0 + EPS
                               ).then_inc(s["root1_ready"], 1)

            pipelined(act, NT2, [(0, centred1), (1, root1)])

            def gates(g, par):
                act.wait_ge(s["pre_mm"], g + 1)
                act.activation(gate_loc[:, cols_of(g, GS)], bank[4 + par][:, 0:GS], ACT.Gelu
                               ).then_inc(s["gate_ready"], 1)
                act.activation(gate_v[:, cols_of(g, GS)], bank[6 + par][:, 0:GS], ACT.Gelu
                               ).then_inc(s["gate_ready"], 1)

            pipelined(act, NG, [(0, gates)])

            def q_out(g, par):
                act.wait_ge(s["qk_mm"], g + 1)
                free_again(act, s["s_mm"], g, 2)
                act.activation(s_a[0:QK, par], bank[0][0:QK, 0:GS], ACT.Copy).then_inc(s["q_ready"], 1)

            def v_out(g, par):
                act.wait_ge(s["vt_mm"], g + 1)
                free_again(act, s["av_mm"], g, 2)
                act.activation(s_v[0:S, par], bank[3][0:S, :], ACT.Copy).then_inc(s["v_ready"], 1)

            def soft_exp(g, par):
                act.wait_ge(s["shifted_ready"], g + 1)
                act.activation(s_d[0:S, par], s_d[0:S, par], ACT.Exp).then_inc(s["expd_ready"], 1)

            def p_out(g, par):
                act.wait_ge(s["pp_mm"], g + 1)
                free_again(act, s["av_mm"], g, 2)
                act.activation(s_c[0:S, par], bank[5][0:S, 0:GS], ACT.Copy).then_inc(s["pp_ready"], 1)

            def attended(g, par):
                act.wait_ge(s["av_mm"], g + 1)
                free_again(act, s["out_mm"], g, 2)
                act.activation(s_e[:, par], bank[6][:, 0:GS], ACT.Copy).then_inc(s["at_ready"], 1)

            pipelined(act, NG, [(0, q_out), (2, soft_exp), (3, v_out), (4, p_out), (5, attended)])

            def centred2(g, par):
                act.wait_ge(s["ctr2_mm"], g + 1)
                act.activation(ctr2[:, cols_of(g, TT)], bank[0][:, 0:TT], ACT.Copy).then_inc(s["ctr2_ready"], 1)
                free_again(act, s["var2_mm"], g, 2)
                act.activation(s_c[:, par, 0:TT], bank[0][:, 0:TT], ACT.Square).then_inc(s["ctr2_ready"], 1)

            def root2(g, par):
                act.wait_ge(s["var2_mm"], g + 1)
                free_again(act, s["recip2_ready"], g, 2)
                v = bank[1][:, 0:2]
                act.activation(roots[:, par, 0:2], v, ACT.Sqrt, bias=eps[:, 1:2]).then_inc(s["root2_ready"], 1)
                act.activation(roots[:, par, 2:4], v, ACT.Sqrt, bias=eps[:, 2:3], scale=1.0 + EPS
                               ).then_inc(s["root2_ready"], 1)

            def affine(g, par):
                act.wait_ge(s["x2_ready"], g + 1)
                free_again(act, s["turn_mm"], g, 2)
                act.activation(s_c2[:, par], s_xn[:, par], ACT.Identity, bias=col("ffn_beta"),
                               scale=col("ffn_gamma")).then_inc(s["xf_ready"], 1)
                act.wait_ge(s["xf_ready"], g + 1)
                act.activation(signs[:, par], s_c2[:, par], ACT.Sign).then_inc(s["sign_ready"], 1)

            def turned(g, par):
                act.wait_ge(s["turn_mm"], g + 1)
                pair = rows[:, bass.ds(g * 2, 2), :]
                act.activation(pair[:, :, 0:D], bank[4][:, 0:TT].rearrange("p (i d) -> p i d", d=D), ACT.Copy
                               ).then_inc(s["xf_out"], 1)
                act.activation(pair[:, :, D:2 * D], bank[5][:, 0:TT].rearrange("p (i d) -> p i d", d=D), ACT.Copy
                               ).then_inc(s["res_out"], 1)

            s_xn = s_v[:, :, 0:TT]
            s_c2 = s_a[:, :, 0:TT]
            pipelined(act, NT2, [(0, centred2), (1, root2), (4, affine), (6, turned)])

            def x_out(g, par):
                act.wait_ge(s["turn3_mm"], g + 1)
                free_again(act, s["h3_mm"], g, 2)
                act.activation(s_a[:, par % 2, 0:SI], bank[0][:, 0:SI], ACT.Copy).then_inc(s["x3_ready"], 1)

            def cell(g, par):
                act.wait_ge(s["h3_mm"], g + 1)
                free_again(act, s["spline_ready"], g, 2)
                act.activation(s_b[:, par % 2, 0:SI], bank[1][:, 0:SI], ACT.Sigmoid).then_inc(s["cell_ready"], 1)

            def fill(g, par):
                for a in range(2):
                    tab = wts[:, par, :, 2 * D + a * GRID:2 * D + (a + 1) * GRID:2]
                    act.activation(look[:, par % 2, a].rearrange("p k (j n) -> p k j n", n=ST),
                                   spread_to(tab.rearrange("p j k -> p k j"), 3, ST),
                                   ACT.Copy).then_inc(s["fill_ready"], 1)

            def y_out(g, par):
                act.wait_ge(s["y_mm"], g + 1)
                if not fixed(g) or g >= 2:
                    before_last = (par - 2) % WR
                    act.wait_ge(s_stored[before_last], (g - 2 - before_last) * (32 // WR) + 32)
                for a in range(2):
                    act.activation(rows_out[:, par % 2, a], bank[2][:, a * D:(a + 1) * D], ACT.Copy,
                                   scale=rows_in[:, par, a, SCL:SCL + 1]).then_inc(s["y_ready"], 1)

            act.wait_ge(s["used_ready"], 1)
            tiles = act.value_load(used[0:1, 0:1], min_val=NI_SURE * TI - TI + 1, max_val=NTILE)
            pipelined(act, NI, [(lag, where_used(act, tiles, stage)) for lag, stage in
                                ((0, x_out), (0, cell), (0, fill), (2, y_out))], unroll=WR, sure=NI_SURE)

        @block.tensor
        def _(pe):
            def mm(o, l, r, start=True, stop=True):
                return pe.matmul(o, l, r, start=start, stop=stop)

            pe.wait_ge(s_ld["text"], 16 * 6)
            pe.wait_ge(s_ld["const"], 16 * 4)

            def encode(g, par):
                pe.wait_ge(s["hid_ready"], g + 1)
                free_again(pe, s["enc_ready"], g, 1)
                mm(bank[0][:, 0:GT], w2[:, :], s_a[:, par, 0:GT]).then_inc(s["enc_mm"], 1)

            def similar(g, par):
                pe.wait_ge(s["enc_ready"], g + 1)
                free_again(pe, s["exp_ready"], g, 2)
                mm(bank[4 + par][:, 0:NB], s_b[:, par, 0:GT], bins_t[:, :]).then_inc(s["sim_mm"], 1)

            def turn_p(g, par):
                pe.wait_ge(s["prob_ready"], g + 1)
                free_again(pe, s["pt_ready"], g, 1)
                pe.transpose(bank[2][:, 0:GT], s_d[:, par, 0:P], ident[:, :]).then_inc(s["pt_mm"], 1)

            def embed(g, par):
                pe.wait_ge(s["pt_ready"], g + 1)
                free_again(pe, s["emb_ready"], g, 1)
                mm(bank[3][:, 0:GT], bins[:, :], s_e[0:BINS, par, 0:GT]).then_inc(s["emb_mm"], 1)

            pipelined(pe, NG, [(0, encode), (2, similar), (4, turn_p), (5, embed)])

            pe.wait_ge(s_ld["image"], 32)
            pe.wait_ge(s["emb_ready"], NG)
            mm(bank[7][:, 0:1], dense[:, :], col("tok_beta")).then_inc(s["bias_mm"], 1)
            pe.wait_ge(s["fold_done"], 1)
            folded = w5[:, 0, :].rearrange("p (k n) -> p k n", k=KCH)

            def conv(g, par):
                r = par % RING
                pe.wait_ge(s_patch[r], (g - par) * (16 // RING) + 16)
                free_again(pe, s["conv_ready"], g, 1)
                for k in range(KCH):
                    last = mm(bank[0][:, 0:GI], folded[:, k, :], patches[:, r, k, :], k == 0, k == KCH - 1)
                last.then_inc(s["conv_mm"], 1)

            def centre_y(g, par):
                pe.wait_ge(s["conv_ready"], g + 1)
                if not fixed(g) or g >= 1:
                    pe.wait_ge(s["ctr_ready"], 2 * g)
                mm(bank[1][:, 0:GI], centre[:, :], s_a[:, par % 2, 0:GI]).then_inc(s["ctr_mm"], 1)

            def variance(g, par):
                pe.wait_ge(s["ctr_ready"], 2 * g + 2)
                free_again(pe, s["root_ready"], g, 1)
                for j in range(2):
                    last = mm(bank[2][0:HI, j:j + 1], s_c[:, par % 2, j * HI:(j + 1) * HI], c128[:, 0:1])
                last.then_inc(s["var_mm"], 1)

            def spread(g, par):
                pe.wait_ge(s["recip_ready"], g + 1)
                free_again(pe, s["norm_ready"], g, 1)
                for j in range(2):
                    last = mm(bank[3][:, j * HI:(j + 1) * HI],
                              recips[0:HI, par % 2, j:j + 1].broadcast_to([HI, P]), ident[0:HI, 0:HI])
                last.then_inc(s["spread_mm"], 1)

            def dense_mm(g, par):
                pe.wait_ge(s["norm_ready"], g + 1)
                free_again(pe, s["img_ready"], g, 1)
                mm(bank[4][:, 0:GI], dense[:, :], s_d[:, par % 2, 0:GI]).then_inc(s["dense_mm"], 1)

            pipelined(pe, NG, [(0, conv), (1, centre_y), (2, variance), (3, spread), (4, dense_mm)], unroll=RING)

            pe.wait_ge(s["img_ready"], NG)

            def centre_h(g, par):
                if not fixed(g) or g >= 1:
                    pe.wait_ge(s["ctr1_ready"], 2 * g)
                mm(bank[0][:, 0:TT], centre[:, :], hT[:, cols_of(g, TT)]).then_inc(s["ctr1_mm"], 1)

            def variance1(g, par):
                pe.wait_ge(s["ctr1_ready"], 2 * g + 2)
                if not fixed(g) or g >= 1:
                    pe.wait_ge(s["root1_ready"], 2 * g)
                for j in range(2):
                    last = mm(bank[1][:, j:j + 1], s_c[:, par, j * P:(j + 1) * P], c128[:, 0:1])
                last.then_inc(s["var1_mm"], 1)

            def spread1(g, par):
                pe.wait_ge(s["recip1_ready"], g + 1)
                free_again(pe, s["nx1_ready"], g, 2)
                for a in range(2):
                    for j in range(2):
                        last = mm(bank[2 + 2 * par + a][:, j * P:(j + 1) * P],
                                  recips[:, par, 2 * a + j:2 * a + j + 1].broadcast_to([P, P]), ident[:, :])
                last.then_inc(s["spread1_mm"], 1)

            pipelined(pe, NT2, [(0, centre_h), (1, variance1), (3, spread1)])

            pe.wait_ge(s_ld["attn"], 16 * 6)

            pe.wait_ge(s["nx1_ready"], NT2)

            def gate_mm(g, par):
                if not fixed(g) or g >= 2:
                    pe.wait_ge(s["gate_ready"], 2 * g - 2)
                mm(bank[4 + par][:, 0:GS], expand[:, 2 * P:3 * P], nxT[:, cols_of(g, GS)])
                mm(bank[6 + par][:, 0:GS], expand[:, 3 * P:4 * P], nxT[:, cols_of(g, GS)]
                   ).then_inc(s["pre_mm"], 1)

            pipelined(pe, NG, [(0, gate_mm)])

            pe.wait_ge(s["gate_ready"], 2 * NG)

            def qk_lin(g, par):
                here = nxT[:, cols_of(g, GS)]
                free_again(pe, s["q_ready"], g, 1)
                free_again(pe, s["k_ready"], g, 1)
                mm(bank[0][0:64, 0:GS], expand[:, 4 * P:4 * P + 64], here).then_inc(s["qk_mm"], 1)
                free_again(pe, s["vT_ready"], g, 1)
                mm(bank[1][:, 0:GS], expand[:, 0:P], here)
                mm(bank[2][:, 0:GS], expand[:, P:2 * P], here).then_inc(s["lin_mm"], 1)

            def values_scores(g, par):
                pe.wait_ge(s["vT_ready"], g + 1)
                free_again(pe, s["v_ready"], g, 1)
                for j in range(GB):
                    last = pe.transpose(bank[3][0:S, j * D:(j + 1) * D], s_b[:, par, j * S:(j + 1) * S], ident[:, :])
                last.then_inc(s["vt_mm"], 1)
                pe.wait_ge(s["q_ready"], g + 1)
                pe.wait_ge(s["k_ready"], g + 1)
                if not fixed(g) or g >= 1:
                    pe.wait_ge(s["soft_step"], 2 * g - 1)
                for j in range(GB):
                    at = slice(j * S, (j + 1) * S)
                    last = mm(bank[4][0:S, at], s_a[0:QK, par, at], s_f[0:QK, par, at])
                last.then_inc(s["s_mm"], 1)

            def turn_probs(g, par):
                pe.wait_ge(s["p_ready"], g + 1)
                free_again(pe, s["pp_ready"], g, 1)
                for j in range(GB):
                    at = slice(j * S, (j + 1) * S)
                    last = pe.transpose(bank[5][0:S, at], s_g[0:S, par, at], ident[0:S, 0:S])
                last.then_inc(s["pp_mm"], 1)

            def attend(g, par):
                pe.wait_ge(s["pp_ready"], g + 1)
                pe.wait_ge(s["v_ready"], g + 1)
                free_again(pe, s["at_ready"], g, 1)
                for j in range(GB):
                    at = slice(j * S, (j + 1) * S)
                    last = mm(bank[6][:, at], s_v[0:S, par, j * D:(j + 1) * D], s_c[0:S, par, at])
                last.then_inc(s["av_mm"], 1)

            def project_mm(g, par):
                pe.wait_ge(s["at_ready"], g + 1)
                free_again(pe, s["h2_ready"], g, 1)
                mm(bank[7][:, 0:GS], project[:, 0, :], gate_loc[:, cols_of(g, GS)], True, False)
                mm(bank[7][:, 0:GS], project[:, 1, :], s_e[:, par], False, True).then_inc(s["out_mm"], 1)

            pipelined(pe, NG, [(0, qk_lin), (2, values_scores), (4, turn_probs), (5, attend), (6, project_mm)])

            pe.wait_ge(s["h2_ready"], NG)
            pe.wait_ge(s["sig_ready"], 1)

            def centre_2(g, par):
                if not fixed(g) or g >= 1:
                    pe.wait_ge(s["ctr2_ready"], 2 * g)
                mm(bank[0][:, 0:TT], centre[:, :], h2T[:, cols_of(g, TT)]).then_inc(s["ctr2_mm"], 1)

            def variance2(g, par):
                pe.wait_ge(s["ctr2_ready"], 2 * g + 2)
                if not fixed(g) or g >= 1:
                    pe.wait_ge(s["root2_ready"], 2 * g)
                for j in range(2):
                    last = mm(bank[1][:, j:j + 1], s_c[:, par, j * P:(j + 1) * P], c128[:, 0:1])
                last.then_inc(s["var2_mm"], 1)

            def spread2(g, par):
                pe.wait_ge(s["recip2_ready"], g + 1)
                free_again(pe, s["x2_ready"], g, 1)
                for a in range(2):
                    for j in range(2):
                        last = mm(bank[2 + a][:, j * P:(j + 1) * P],
                                  recips[:, par, 2 * a + j:2 * a + j + 1].broadcast_to([P, P]), ident[:, :])
                last.then_inc(s["spread2_mm"], 1)

            def turn_score(g, par):
                pe.wait_ge(s["xf_ready"], g + 1)
                pe.wait_ge(s["sign_ready"], g + 1)
                pe.wait_ge(s["res_ready"], g + 1)
                free_again(pe, s["res_out"], g, 1)
                if not fixed(g) or g >= 1:
                    pe.wait_ge(s["key_step"], 2 * g - 1)
                for j in range(2):
                    at = slice(j * P, (j + 1) * P)
                    mm(bank[6][:, j * E:(j + 1) * E], signs[:, par, at], w_cl[:, :], True, False)
                    mm(bank[6][:, j * E:(j + 1) * E], signs[:, par, at], w_tile[:, :], False, True
                       ).then_inc(s["score_mm"], 1)
                for j in range(2):
                    at = slice(j * P, (j + 1) * P)
                    pe.transpose(bank[4][:, at], s_a[:, par, at], ident[:, :])
                    last = pe.transpose(bank[5][:, at], s_e[:, par, at], ident[:, :])
                last.then_inc(s["turn_mm"], 1)

            pipelined(pe, NT2, [(0, centre_2), (1, variance2), (3, spread2), (5, turn_score)])

            pe.wait_ge(s["cnt_ready"], 1)
            pe.wait_ge(s_ld["route"], 16 * 7)
            mm(bank[0][0:E, 0:1], cnt[:, :], ones_bf[:, 0:1]).then_inc(s["route_mm"], 1)
            pe.wait_ge(s["route_dve"], 3)
            mm(bank[1][:, 0:E], ntile[:, 1:2].broadcast_to([E, P]), before[0:E, 0:E], True, False)
            mm(bank[1][:, 0:E], before[:, :], cnt[:, :], False, True)
            mm(bank[7][:, 0:1], ones_bf[0:E, :], ntile[:, 0:1])
            mm(bank[2][0:E, 0:1], upto[:, :], ntile[:, 0:1]).then_inc(s["route_mm"], 1)
            pe.wait_ge(s["route_dve"], 5)
            mm(bank[3][:, 0:NTILE], ones_bf[0:E, :], started[:, :]).then_inc(s["route_mm"], 1)

            pe.wait_ge(s["res_out"], NT2)

            def turn_rows(g, par):
                pe.wait_ge(s_rows[par], (g - par) * (16 // WR) + 16)
                free_again(pe, s["x3_ready"], g, 1)
                for a in range(2):
                    last = pe.transpose(bank[0][:, a * P:(a + 1) * P], rows_in[:, par, a, 0:D], ident[:, :])
                last.then_inc(s["turn3_mm"], 1)

            def down(g, par):
                pe.wait_ge(s_wts[par], (g - par) * (16 * TI // WR) + 16 * TI)
                pe.wait_ge(s["x3_ready"], g + 1)
                free_again(pe, s["cell_ready"], g, 1)
                for j in range(TI):
                    at = slice(j * ST, (j + 1) * ST)
                    last = mm(bank[1][:, at], wts[:, par, j, 0:D], s_a[:, par % 2, at])
                last.then_inc(s["h3_mm"], 1)

            def up(g, par):
                pe.wait_ge(s["spline_ready"], g + 1)
                if not fixed(g) or g >= 1:
                    pe.wait_ge(s["y_ready"], 2 * g)
                for j in range(TI):
                    a, q = j // 4, j % 4
                    last = mm(bank[2][q * ST:(q + 1) * ST, a * D:(a + 1) * D],
                              s_c[:, par % 2, j * ST:(j + 1) * ST], wts[:, par, j, D:2 * D])
                last.then_inc(s["y_mm"], 1)

            pe.wait_ge(s["used_ready"], 1)
            tiles = pe.value_load(used[0:1, 0:1], min_val=NI_SURE * TI - TI + 1, max_val=NTILE)
            pipelined(pe, NI, [(lag, where_used(pe, tiles, stage)) for lag, stage in
                               ((0, turn_rows), (0, down), (2, up))], unroll=WR, sure=NI_SURE)

        @block.vector
        def _(dve):
            dve.wait_ge(s_ld["text"], 16 * 6)
            dve.tensor_scalar(is0[:, :], x_col[:, :], 0.0, None, ALU.is_equal).then_inc(s["setup_step"], 1)
            dve.tensor_scalar(not0[:, :], x_col[:, :], 0.0, None, ALU.not_equal).then_inc(s["setup_step"], 1)
            dve.wait_ge(s["setup_step"], 2)

            dve.memset(s_d[:, :, BINS:P], 0.0).then_inc(s["setup_step"], 1)
            dve.wait_ge(s["setup_step"], 3)

            def top(g, par):
                dve.wait_ge(s["sim_mm"], g + 1)
                dve.tensor_reduce(small[:, par, 0:1], bank[4 + par][:, 0:NB], AX.X, ALU.max, negate=True
                                  ).then_inc(s["top_ready"], 1)

            def probs(g, par):
                dve.wait_ge(s["exp_ready"], g + 1)
                free_again(dve, s["pt_mm"], g, 2)
                dve.reciprocal(small[:, par, 2:3], small[:, par, 1:2]).then_inc(s["prob_step"], 1)
                dve.tensor_copy(s_d[:, par, 0:1], is0[:, bass.ds(g, 1)]).then_inc(s["prob_step"], 1)
                dve.tensor_copy(small[:, par, 3:4], not0[:, bass.ds(g, 1)]).then_inc(s["prob_step"], 1)
                dve.wait_ge(s["prob_step"], 3 * g + 3)
                dve.tensor_scalar(s_d[:, par, 1:BINS], s_c[:, par, 0:NB], small[:, par, 2:3],
                                  small[:, par, 3:4], ALU.mult, ALU.mult).then_inc(s["prob_ready"], 1)

            def p_out(g, par):
                dve.wait_ge(s["pt_mm"], g + 1)
                free_again(dve, s["emb_mm"], g, 2)
                dve.tensor_copy(s_e[0:BINS, par, 0:GT], bank[2][0:BINS, 0:GT]).then_inc(s["pt_ready"], 1)

            def sum_wd(g, par):
                dve.wait_ge(s_sig[par], (g - par) * (16 // WR) + 16)
                dve.tensor_reduce(sig_sum[:, bass.ds(g * SIG_C, SIG_C)], sig_buf[:, par], AX.X, ALU.add
                                  ).then_inc(s["sig_red"], 1)

            pipelined(dve, NG, [(2, lambda g, par: top(g, par % 2)), (3, lambda g, par: probs(g, par % 2)),
                                (4, lambda g, par: p_out(g, par % 2)), (4, sum_wd)], unroll=WR)

            dve.wait_ge(s["sig_red"], NG)

            def sign_of(dst, src, scratch):
                n = sign_of.n
                dve.tensor_scalar(scratch, src, 0.0, None, ALU.is_lt).then_inc(s["sig_step"], 1)
                dve.tensor_scalar(dst, src, 0.0, None, ALU.is_gt).then_inc(s["sig_step"], 1)
                dve.wait_ge(s["sig_step"], n + 2)
                dve.tensor_tensor(dst, dst, scratch, ALU.subtract).then_inc(s["sig_step"], 1)
                dve.wait_ge(s["sig_step"], n + 3)
                sign_of.n = n + 4
            sign_of.n = 0
            scr = keys[:, 0, 0:E]
            sign_of(sig_tile[:, :], sig_sum[:, :], scr)
            dve.tensor_reduce(sig_clsum[:, :], sig_tile[:, :].rearrange("p (c j) -> p c j", j=TPC), AX.X,
                              ALU.add).then_inc(s["sig_step"], 1)
            dve.wait_ge(s["sig_step"], 4)
            sign_of(sig_cl[:, :], sig_clsum[:, :], scr[:, 0:CL])
            dve.tensor_scalar(w_tile[:, :], sig_tile[:, :], float(TPC), None, ALU.mult).then_inc(s["sig_step"], 1)
            dve.tensor_scalar(w_cl[:, :].rearrange("p (c j) -> p c j", j=TPC),
                              spread_to(sig_cl[:, :], 2, TPC), CL * 4096.0, None, ALU.mult
                              ).then_inc(s["sig_ready"], 1)
            dve.wait_ge(s["sig_ready"], 1)

            dve.wait_ge(s["bias_mm"], 1)
            dve.tensor_tensor(dense_bias[:, :], bank[7][:, 0:1], col("dense_b"), ALU.add
                              ).then_inc(s["bias_ready"], 1)

            dve.wait_ge(s["mask_ready"], 1)
            dve.tensor_tensor(mask[:, :], mask[:, :], causal[:, :], ALU.mult).then_inc(s["setup_step"], 1)
            dve.wait_ge(s["setup_step"], 4)
            dve.tensor_tensor(mask[:, :], mask[:, :], veil[:, :], ALU.add).then_inc(s["setup_step"], 1)

            def recip(g, par):
                dve.wait_ge(s["root_ready"], g + 1)
                free_again(dve, s["spread_mm"], g, 2)
                dve.reciprocal(recips[0:HI, par, 0:2], roots[0:HI, par, 0:2]).then_inc(s["recip_ready"], 1)

            def norm(g, par):
                dve.wait_ge(s["spread_mm"], g + 1)
                dve.wait_ge(s["ctr_ready"], 2 * g + 2)
                free_again(dve, s["dense_mm"], g, 2)
                dve.scalar_tensor_tensor(out=s_d[:, par, 0:GI], in0=s_b[:, par, 0:GI], scalar=col("tok_gamma"),
                                         in1=bank[3][:, 0:GI], op0=ALU.mult, op1=ALU.mult
                                         ).then_inc(s["norm_ready"], 1)

            pipelined(dve, NG, [(2, recip), (3, norm)])

            def recip1(g, par):
                dve.wait_ge(s["root1_ready"], 2 * g + 2)
                free_again(dve, s["spread1_mm"], g, 2)
                dve.reciprocal(recips[:, par, 0:4], roots[:, par, 0:4]).then_inc(s["recip1_ready"], 1)

            def norm1(g, par):
                dve.wait_ge(s["spread1_mm"], g + 1)
                dve.wait_ge(s["ctr1_ready"], 2 * g + 2)
                free_again(dve, s["hx_ready"], g, 2)
                dve.tensor_tensor(s_d[:, par, 0:TT], ctr1[:, cols_of(g, TT)], bank[2 + 2 * par][:, 0:TT], ALU.mult).then_inc(s["x1_ready"], 1)
                dve.tensor_tensor(nxT[:, cols_of(g, TT)], ctr1[:, cols_of(g, TT)], bank[3 + 2 * par][:, 0:TT], ALU.mult
                                  ).then_inc(s["nx1_ready"], 1)

            pipelined(dve, NT2, [(1, recip1), (3, norm1)])

            dve.wait_ge(s["hx_ready"], NT2)

            def kv(g, par):
                dve.wait_ge(s["qk_mm"], g + 1)
                free_again(dve, s["s_mm"], g, 2)
                dve.tensor_copy(s_f[0:QK, par], bank[0][KOFF:KOFF + QK, 0:GS]).then_inc(s["k_ready"], 1)
                dve.wait_ge(s["lin_mm"], g + 1)
                loc = gate_loc[:, cols_of(g, GS)]
                dve.tensor_tensor(loc, loc, bank[1][:, 0:GS], ALU.mult).then_inc(s["loc_ready"], 1)
                free_again(dve, s["vt_mm"], g, 2)
                dve.tensor_tensor(s_b[:, par], gate_v[:, cols_of(g, GS)], bank[2][:, 0:GS], ALU.mult
                                  ).then_inc(s["vT_ready"], 1)

            def shifted(g, par):
                dve.wait_ge(s["s_mm"], g + 1)
                x = s_d[0:S, par].rearrange("p (b k) -> p b k", k=S)
                free_again(dve, s["p_ready"], g, 2)
                dve.scalar_tensor_tensor(out=x, in0=bank[4][0:S, 0:GS].rearrange("p (b k) -> p b k", k=S),
                                         scalar=float(QK) ** -0.5,
                                         in1=spread_to(mask[:, :], 1, GB),
                                         op0=ALU.mult, op1=ALU.add).then_inc(s["soft_step"], 1)
                dve.wait_ge(s["soft_step"], 2 * g + 1)
                dve.tensor_reduce(small[0:S, par, 0:GB], x, AX.X, ALU.max).then_inc(s["soft_step"], 1)
                dve.wait_ge(s["soft_step"], 2 * g + 2)
                dve.tensor_tensor(x, x, spread_to(small[0:S, par, 0:GB], 2, S), ALU.subtract
                                  ).then_inc(s["shifted_ready"], 1)

            def normalised(g, par):
                dve.wait_ge(s["expd_ready"], g + 1)
                x = s_d[0:S, par].rearrange("p (b k) -> p b k", k=S)
                dve.tensor_reduce(small[0:S, par, 4:8], x, AX.X, ALU.add).then_inc(s["sum_step"], 1)
                dve.wait_ge(s["sum_step"], 2 * g + 1)
                dve.reciprocal(small[0:S, par, 4:8], small[0:S, par, 4:8]).then_inc(s["sum_step"], 1)
                dve.wait_ge(s["sum_step"], 2 * g + 2)
                free_again(dve, s["pp_mm"], g, 2)
                dve.tensor_tensor(s_g[0:S, par].rearrange("p (b k) -> p b k", k=S), x,
                                  spread_to(small[0:S, par, 4:8], 2, S), ALU.mult
                                  ).then_inc(s["p_ready"], 1)

            def add_out(g, par):
                dve.wait_ge(s["out_mm"], g + 1)
                dve.tensor_tensor(h2T[:, cols_of(g, GS)], hT[:, cols_of(g, GS)], bank[7][:, 0:GS], ALU.add
                                  ).then_inc(s["h2_ready"], 1)

            pipelined(dve, NG, [(0, kv), (2, shifted), (3, normalised), (6, add_out)])

            def recip2(g, par):
                dve.wait_ge(s["root2_ready"], 2 * g + 2)
                free_again(dve, s["spread2_mm"], g, 2)
                dve.reciprocal(recips[:, par, 0:4], roots[:, par, 0:4]).then_inc(s["recip2_ready"], 1)

            def norm2(g, par):
                dve.wait_ge(s["spread2_mm"], g + 1)
                dve.wait_ge(s["ctr2_ready"], 2 * g + 2)
                free_again(dve, s["res_ready"], g, 2)
                dve.tensor_tensor(s_d[:, par, 0:TT], ctr2[:, cols_of(g, TT)], bank[2][:, 0:TT], ALU.mult)
                free_again(dve, s["xf_ready"], g, 2)
                dve.tensor_tensor(s_v[:, par, 0:TT], ctr2[:, cols_of(g, TT)], bank[3][:, 0:TT], ALU.mult
                                  ).then_inc(s["x2_ready"], 1)

            def choose(g, par):
                dve.wait_ge(s["score_mm"], 2 * g + 2)
                key = keys[:, par].rearrange("p (i e) -> p i e", e=E)
                dve.tensor_tensor(key, bank[6][:, 0:2 * E].rearrange("p (i e) -> p i e", e=E),
                                  spread_to(tie[:, :], 1, 2), ALU.add).then_inc(s["key_step"], 1)
                dve.wait_ge(s["key_step"], 2 * g + 1)
                dve.tensor_reduce(best[:, par], key, AX.X, ALU.max).then_inc(s["key_step"], 1)
                dve.wait_ge(s["key_step"], 2 * g + 2)
                dve.tensor_tensor(onehot[:, :, bass.ds(g * 2, 2)].rearrange("p e i -> p i e"), key,
                                  spread_to(best[:, par], 2, E), ALU.is_equal).then_inc(s["choice_ready"], 1)
                dve.wait_ge(s["choice_ready"], g + 1)
                mine = scaled[:, par].rearrange("p (i e) -> p i e", e=E)
                dve.tensor_tensor(mine, onehot[:, :, bass.ds(g * 2, 2)].rearrange("p e i -> p i e"),
                                  spread_to(scale_row[:, :], 1, 2), ALU.mult).then_inc(s["scale_step"], 1)
                dve.wait_ge(s["scale_step"], g + 1)
                dve.tensor_reduce(rows[:, bass.ds(g * 2, 2), SCL], mine, AX.X, ALU.add).then_inc(s["scale_ready"], 1)

            dve.wait_ge(s_ld["route"], 16 * 7)
            dve.tensor_copy(rows[:, :, TOK].bitcast(I32), token_no[:, :]).then_inc(s["numbered"], 1)
            pipelined(dve, NT2, [(1, recip2), (3, norm2), (6, choose)])

            dve.wait_ge(s["choice_ready"], NT2)
            with nc.allow_low_precision("counts up to T are exact in bfloat16"):
                dve.tensor_reduce(cnt[:, :], onehot, AX.X, ALU.add).then_inc(s["cnt_ready"], 1)
            flat = hT[:, 0:E * T]
            dve.tensor_tensor_scan(upto_here, flat, flat, 0.0, ALU.add, ALU.max).then_inc(s["scan_ready"], 1)
            dve.wait_ge(s["route_mm"], 1)
            dve.tensor_scalar(tot_i[:, 0:1], bank[0][0:E, 0:1], float(ST - 1), None, ALU.add
                              ).then_inc(s["route_dve"], 1)
            dve.wait_ge(s["route_dve"], 1)
            dve.tensor_scalar(tot_i[:, 1:2], tot_i[:, 0:1], ST.bit_length() - 1, None, ALU.arith_shift_right
                              ).then_inc(s["route_dve"], 1)
            dve.wait_ge(s["route_dve"], 2)
            dve.tensor_copy(ntile[:, 0:1], tot_i[:, 1:2])
            dve.tensor_scalar(ntile[:, 1:2], tot_i[:, 1:2], float(ST), None, ALU.mult).then_inc(s["route_dve"], 1)
            dve.wait_ge(s["route_mm"], 2)
            dve.tensor_copy(ends[:, :], bank[2][0:E, 0:1]).then_inc(s["route_dve"], 1)
            dve.wait_ge(s["route_dve"], 4)
            dve.tensor_scalar(started[:, :], tile_no[:, :], ends[:, 0:1], None, ALU.is_ge
                              ).then_inc(s["route_dve"], 1)
            dve.tensor_copy(used[:, :], bank[7][:, 0:1]).then_inc(s["used_ready"], 1)
            dve.wait_ge(s["scan_ready"], 1)
            ends_here = upto_here.rearrange("p (e i) -> p e i", i=T)[:, 0:E - 1, T - 1]
            dve.tensor_copy(base[:, 0:1], bank[1][:, 0:1]).then_inc(s["place_step"], 1)
            dve.tensor_tensor(base[:, 1:E], bank[1][:, 1:E], ends_here, ALU.subtract).then_inc(s["place_step"], 1)
            dve.wait_ge(s["place_step"], 2)
            def by_expert(ap):
                return ap.rearrange("p (e i) -> p e i", i=T)
            dve.tensor_tensor(by_expert(place_of), by_expert(upto_here), spread_to(base[:, :], 2, T), ALU.add
                              ).then_inc(s["place_step"], 1)
            dve.wait_ge(s["place_step"], 3)
            dve.tensor_tensor(weighed, place_of, flat, ALU.mult).then_inc(s["place_step"], 1)
            dve.wait_ge(s["place_step"], 4)
            dve.tensor_reduce(slot_f[:, :], by_expert(weighed).rearrange("p e i -> p i e"), AX.X, ALU.add
                              ).then_inc(s["place_step"], 1)
            dve.wait_ge(s["place_step"], 5)
            dve.tensor_scalar(slot_i[:, :], slot_f[:, :], -1.0, None, ALU.add).then_inc(s["slots_ready"], 1)
            dve.wait_ge(s["route_mm"], 3)
            dve.tensor_scalar(owner[:, :], bank[3][:, 0:NTILE], float(E - 1), None, ALU.min
                              ).then_inc(s["owner_ready"], 1)
            LEVELS = GRID.bit_length() - 1

            def predicated_after(count):
                dve.wait_ge(s["look_step"], count)
                dve.sem_inc(s["wait_carried"], 1)

            low = 23 - LEVELS
            steps = LEVELS + 4

            def spline(g, par):
                dve.wait_ge(s["fill_ready"], 2 * g + 2)
                dve.wait_ge(s["cell_ready"], g + 1)
                x, table, half = s_b[:, par % 2, 0:SI], look[:, par % 2], par % 2
                dve.tensor_scalar(plus1, x, 1.0, 2.0 - 2.0 ** -23, ALU.add, ALU.min).then_inc(s["look_step"], 1)
                dve.wait_ge(s["look_step"], steps * g + 1)
                for b in range(LEVELS):
                    dve.tensor_scalar(bits[:, b, :], plus1.bitcast(I32), 1 << (low + b), None, ALU.bitwise_and)
                dve.tensor_scalar(cell_at.bitcast(I32), plus1.bitcast(I32), -(1 << low), None, ALU.bitwise_and
                                  ).then_inc(s["look_step"], 1)
                dve.wait_ge(s["look_step"], steps * g + 2)
                dve.scalar_tensor_tensor(out=below, in0=cell_at, scalar=1.0, in1=x, op0=ALU.subtract,
                                         op1=ALU.subtract).then_inc(s["look_step"], 1)
                for a in range(2):
                    tab = wts[:, par, :, 2 * D + a * GRID + 1:2 * D + (a + 1) * GRID:2]
                    last = dve.copy_predicated(
                        table[:, a].rearrange("p k (j n) -> p k j n", n=ST),
                        spread_to(bits[:, 0, :].rearrange("p (j n) -> p j n", n=ST), 1, GRID // 2),
                        spread_to(tab.rearrange("p j k -> p k j"), 3, ST))
                last.then_inc(s["look_step"], 1)
                for b in range(1, LEVELS):
                    predicated_after(steps * g + 3 + b)
                    step = 1 << b
                    both = table.rearrange("p a k n -> p (a k) n")
                    lo, hi = both[:, 0::step, :], both[:, step // 2::step, :]
                    dve.copy_predicated(lo, spread_to(bits[:, b, :], 1, lo.shape[1]), hi
                                        ).then_inc(s["look_step"], 1)
                dve.wait_ge(s["look_step"], steps * g + 3 + LEVELS)
                dve.scalar_tensor_tensor(out=inside, in0=table[:, 1, 0], scalar=-float(GRID), in1=below,
                                         op0=ALU.mult, op1=ALU.mult).then_inc(s["look_step"], 1)
                dve.wait_ge(s["look_step"], steps * g + 4 + LEVELS)
                free_again(dve, s["y_mm"], g, 2)
                dve.tensor_tensor(s_c[:, half, 0:SI], table[:, 0, 0], inside, ALU.add
                                  ).then_inc(s["spline_ready"], 1)

            dve.wait_ge(s["used_ready"], 1)
            tiles = dve.value_load(used[0:1, 0:1], min_val=NI_SURE * TI - TI + 1, max_val=NTILE)
            pipelined(dve, NI, [(1, where_used(dve, tiles, spline))], unroll=WR, sure=NI_SURE)


def _layout(x, x_txt, L0_tok_conv_w, L0_tok_conv_b, L0_tok_gamma, L0_tok_beta, L0_tok_dense_w, L0_tok_dense_b,
            L0_txt_bin_embeddings, L0_txt_w1, L0_txt_b1, L0_txt_w2, L0_txt_b2, L0_attn_expand, L0_attn_project,
            L0_attn_position_bias_mult, L0_ffn_gamma, L0_ffn_beta, L0_ffn_Wd, L0_ffn_spline_bases,
            L0_ffn_spline_slopes, L0_ffn_Wu, L0_ffn_scale):
    a = np.asarray
    keep = [i * WIN + j for i in range(WIN) for j in range(WIN)
            if not (i in (0, WIN - 1) and j in (0, WIN - 1))]
    px = np.pad(a(x), ((0, 0), (1, 1), (1, 1), (0, 0)))
    rows = [px[:, i:i + IMG:PATCH, j:j + IMG:PATCH, :][:, 0:GRID_W, 0:GRID_W] for i in range(WIN) for j in range(WIN)]
    win = np.stack([rows[k] for k in keep])
    win = win.transpose(0, 4, 1, 2, 3).reshape(KCH, KP, NG, GI)
    patches = np.ascontiguousarray(win.transpose(2, 1, 0, 3))
    w = a(L0_tok_conv_w)
    w5 = np.zeros((5, WIN, WIN, CH, D), np.float32)
    for k, (di, dj) in enumerate(((0, 0), (0, -1), (0, 1), (-1, 0), (1, 0))):
        w5[k, 1 + di:1 + di + PATCH, 1 + dj:1 + dj + PATCH] = w[:, :, k * CH:(k + 1) * CH, :]
    w5 = w5.reshape(5, WIN * WIN, CH, D)[:, keep].reshape(5, KCH, KP, D)
    w5 = np.ascontiguousarray(w5.transpose(2, 0, 1, 3)).reshape(KP, 5, KCH * D)
    bins = a(L0_txt_bin_embeddings)
    vectors = (a(L0_txt_w1)[0], L0_txt_b1, L0_txt_b2, L0_tok_conv_b, L0_tok_gamma, L0_tok_beta, L0_tok_dense_b,
               L0_ffn_gamma, L0_ffn_beta)
    ex = a(L0_attn_expand)
    qk = np.zeros((D, 64), np.float32)
    qk[:, 0:QK] = ex[:, 0:QK]
    qk[:, KOFF:KOFF + QK] = ex[:, QK:2 * QK]
    expand = np.concatenate([ex[:, 2 * QK:], qk], axis=1)
    packs = np.concatenate([a(L0_ffn_Wd).transpose(0, 2, 1), a(L0_ffn_Wu).transpose(0, 2, 1),
                            a(L0_ffn_spline_bases), a(L0_ffn_spline_slopes)], axis=2)
    at = np.arange(S)
    e = np.arange(E)
    bf = mybir.dt.np(BF16)
    return dict(
        patches=patches, w5=w5, w2=a(L0_txt_w2), bins=bins, bins_t=bins[1:].T, cols=np.stack([a(v) for v in vectors], 1),
        x_row=a(x_txt).reshape(B * S_TXT), x_col=a(x_txt).reshape(NG, GT).T, dense=a(L0_tok_dense_w),
        expand=expand, project=a(L0_attn_project).reshape(2, P, D).transpose(1, 0, 2),
        pbm=a(L0_attn_position_bias_mult).reshape(1), scale=a(L0_ffn_scale), packs=packs,
        ident=np.eye(P, dtype=np.float32),
        centre=(np.eye(P) - 1.0 / P).astype(np.float32),
        c128=np.tile(np.array([1.0 / P, 1.0], np.float32), (P, 1)),
        eps=np.tile(np.array([EPS_TOK, EPS, EPS * EPS], np.float32), (P, 1)),
        rel=(at[None, :] - at[:, None]).astype(np.float32),
        causal=(at[None, :] <= at[:, None]).astype(np.float32),
        veil=np.where(at[None, :] <= at[:, None], 0.0, -HUGE).astype(np.float32),
        before=np.triu(np.ones((P, P)), 1).astype(bf), upto=np.triu(np.ones((E, E))).astype(bf),
        ones_bf=np.ones((P, P)).astype(bf),
        tie=np.tile(((CL - 1 - e // TPC) * 4096 + (TPC - 1 - e % TPC)).astype(np.float32), (P, 1)),
        token_no=np.arange(N, dtype=np.int32).reshape(T, P).T,
        tile_no=np.tile(np.arange(NTILE, dtype=np.float32), (E, 1)),
    )


def kernel(**inputs):
    import concourse.bacc as bacc
    from concourse.bass_utils import run_bass_kernel_spmd

    arrays = {f"in_{k}": np.ascontiguousarray(v) for k, v in _layout(**inputs).items()}
    nc = bacc.Bacc("TRN2", target_bir_lowering=False, num_devices=1)
    t = {k[3:]: nc.dram_tensor(k, v.shape, mybir.dt.from_np(v.dtype), kind="ExternalInput").ap()
         for k, v in arrays.items()}
    out = nc.dram_tensor("out", (N, D), F32, kind="ExternalOutput").ap()
    build(nc, t, out)
    r = run_bass_kernel_spmd(nc, [arrays], core_ids=[0])
    return r.results[0]["out"].reshape(B, S, D)
```

```python
from contextlib import ExitStack

import numpy as np

import concourse.bass as bass
from concourse import mybir

F32 = mybir.dt.float32
BF16 = mybir.dt.bfloat16
I32 = mybir.dt.int32
ALU = mybir.AluOpType
ACT = mybir.ActivationFunctionType
AX = mybir.AxisListType

P = 128
D = 128
B = 64
IMG = 96
PATCH = 16
CH = 3
GRID_W = IMG // PATCH
S_IMG = GRID_W * GRID_W
S_TXT = 32
S = S_IMG + S_TXT
N = B * S
GB = 4
NG = B // GB
GI = GB * S_IMG
HI = GI // 2
GT = GB * S_TXT
GS = GB * S
WIN = PATCH + 2
KCH = 8
KP = (WIN * WIN - 4) * CH // KCH
BINS = 51
NB = BINS - 1
QK = 16
KOFF = 32
E = 64
CL = 8
TPC = E // CL
GRID = 16
T = N // P
TT = 2 * P
NT2 = N // TT
ST = 32
NTILE = -(-(E + (N - E) // ST) // 8) * 8
TI = 8
SI = TI * ST
NI = NTILE // TI
NI_SURE = -(-(N // ST) // TI)
SLOTS = NTILE * ST
LEVELS = GRID.bit_length() - 1
WROW = 2 * D + 2 * GRID
SIG_C = E // NG
EPS_TOK = 1e-3
EPS = 1e-5
HUGE = 3.0e38
RING = 4
WR = 4
ROW = 2 * D + 1
SCL = 2 * D
SC = SLOTS // P


def fixed(g):
    return isinstance(g, int)


def pipelined(eng, n, stages, unroll=2, sure=None, ordered=False):
    if not ordered:
        stages = sorted(stages, key=lambda at: -at[0])
    depth = max(lag for lag, _ in stages)
    head = -(-(depth + unroll) // unroll) * unroll
    rest = ((sure or n) - head) // unroll * unroll + head

    def peeled(i):
        for lag, stage in stages:
            if 0 <= i - lag < n:
                stage(i - lag, (i - lag) % unroll)

    for i in range(head):
        peeled(i)
    with eng.Fori(head // unroll, rest // unroll) as turn:
        for u in range(unroll):
            for lag, stage in stages:
                stage(turn * unroll + (u - lag), (u - lag) % unroll)
    for i in range(rest, n + depth):
        peeled(i)


def free_again(eng, sem, g, slots):
    if not fixed(g) or g >= slots:
        eng.wait_ge(sem, g - slots + 1)


def where_used(eng, tiles, stage):
    def run(g, par):
        if not fixed(g) or g < NI_SURE:
            stage(g, par)
        else:
            with eng.If(tiles > g * TI):
                stage(g, par)
    return run


def spread_to(ap, dim, count):
    ap = ap.unsqueeze(dim)
    return ap.broadcast_to([count if i == dim else n for i, n in enumerate(ap.shape)])


def build(nc, t, out):
    with ExitStack() as ctx:
        def sb(name, shape, dt=F32):
            return ctx.enter_context(nc.sbuf_tensor(name, shape, dt))

        def sem(name):
            return ctx.enter_context(nc.semaphore(name))

        bank = [ctx.enter_context(nc.psum_tensor(f"bank{i}", [P, 512], F32)) for i in range(8)]

        token_rows = nc.dram_tensor("token_rows", (N, ROW), F32).ap()

        ident = sb("ident", [P, P])
        centre = sb("centre", [P, P])
        c128 = sb("c128", [P, 2])
        before = sb("before", [P, P], BF16)
        upto = sb("upto", [E, E], BF16)
        ones_bf = sb("ones_bf", [P, P], BF16)
        tie = sb("tie", [P, E])
        tile_no = sb("tile_no", [E, NTILE])
        rel = sb("rel", [S, S])
        causal = sb("causal", [S, S])
        veil = sb("veil", [S, S])
        mask = sb("mask", [S, S])
        pbm = sb("pbm", [P, 1])
        eps = sb("eps", [P, 3])
        cols = sb("cols", [P, 9])
        w2 = sb("w2", [P, D])
        bins_t = sb("bins_t", [P, NB])
        bins = sb("bins", [BINS, D])
        x_col = sb("x_col", [GT, NG], I32)
        is0 = sb("is0", [GT, NG])
        not0 = sb("not0", [GT, NG])
        dense = sb("dense", [P, D])
        dense_bias = sb("dense_bias", [P, 1])
        expand = sb("expand", [P, 4 * P + 64])
        project = sb("project", [P, 2, D])
        scale_row = sb("scale_row", [P, E])

        hT = sb("hT", [P, N])
        nxT = sb("nxT", [P, N])
        gates_all = sb("gates_all", [P, T * ROW])
        gate_loc = gates_all[:, 0:N]
        gate_v = gates_all[:, N:2 * N]
        h2T = sb("h2T", [P, N])
        x_txt = h2T[:, 0:B * S_TXT].bitcast(I32)
        ctr1 = h2T
        ctr2 = nxT
        rows = gates_all[:, :].rearrange("p (i c) -> p i c", c=ROW)
        onehot = hT[:, 0:E * T].rearrange("p (e i) -> p e i", i=T)
        weighed = hT[:, E * T:2 * E * T]
        upto_here = nxT[:, 0:E * T]
        place_of = nxT[:, E * T:2 * E * T]

        big = sb("big", [P, RING * KCH * GI + 5 * KCH * D])
        patches = big[0:KP, 0:RING * KCH * GI].rearrange("p (r k n) -> p r k n", r=RING, k=KCH)
        w5 = big[0:KP, RING * KCH * GI:].rearrange("p (s k) -> p s k", s=5)
        LOOK = 2 * GRID // 2 * SI
        look = big[:, 0:2 * LOOK].rearrange("p (r a k n) -> p r a k n", r=2, a=2, k=GRID // 2)

        s_a = sb("s_a", [P, 2, GS])
        s_b = sb("s_b", [P, 2, GS])
        s_c = sb("s_c", [P, 2, GS])
        s_d = sb("s_d", [P, 2, GS])
        s_e = sb("s_e", [P, 2, GS])
        s_f = sb("s_f", [P, 2, GS])
        s_g = sb("s_g", [P, 2, GS])
        s_v = sb("s_v", [P, 2, GB * D])
        roots = sb("roots", [P, 2, 8])
        recips = sb("recips", [P, 2, 8])
        signs = sb("signs", [P, 2, TT], BF16)
        keys = sb("keys", [P, 2, 2 * E])
        best = sb("best", [P, 2, 2])
        small = sb("small", [P, 2, 8])

        sig_sum = sb("sig_sum", [P, E])
        sig_tile = sb("sig_tile", [P, E])
        sig_clsum = sb("sig_clsum", [P, CL])
        sig_cl = sb("sig_cl", [P, CL])
        w_tile = sb("w_tile", [P, E], BF16)
        w_cl = sb("w_cl", [P, E], BF16)
        cnt = sb("cnt", [P, E], BF16)
        tot_i = sb("tot_i", [E, 2], I32)
        ntile = sb("ntile", [E, 2], BF16)
        ends = sb("ends", [E, 1])
        started = sb("started", [E, NTILE], BF16)
        owner = sb("owner", [P, NTILE], I32)
        used = sb("used", [P, 1], I32)
        base = sb("base", [P, E])
        slot_f = sb("slot_f", [P, T])
        slot_i = sb("slot_i", [P, T], I32)
        slot_part = sb("slot_part", [P, 2, T], I32)
        slot_part_f = sb("slot_part_f", [P, 2, T])
        count_up = sb("count_up", [P, P])
        p_plus1 = sb("p_plus1", [P, 1])
        token1 = sb("token1", [P, 2, SC])
        fetch_at = sb("fetch_at", [P, SC], I32)
        store_at = sb("store_at", [P, SC], I32)
        at_now = sb("at_now", [P, WR, 4], I32)
        scaled = sb("scaled", [P, 2, 2 * E])

        wts = sb("wts", [P, WR, TI, WROW])
        rows_in = sb("rows_in", [P, WR, 2, ROW])
        rows_out = sb("rows_out", [P, 2, 2, D])
        place_1h = h2T[:, 0:T * P // 2].bitcast(BF16).rearrange("p (i c) -> p i c", c=P)
        col_1h = nxT[:, 0:T * SC // 2].bitcast(BF16).rearrange("p (i c) -> p i c", c=SC)
        col_tok = nxT[:, T * SC // 2:T * SC // 2 + T * SC].bitcast(BF16).rearrange("p (i c) -> p i c", c=2 * SC)
        bits = h2T[:, 0:8 * SI].bitcast(I32).rearrange("p (r b n) -> p r b n", r=2, n=SI)
        plus1, cell_at, frac, inside = (h2T[:, k * SI:(k + 2) * SI].rearrange("p (r n) -> p r n", n=SI)
                                        for k in range(8, 16, 2))

        s_ld = {k: sem(f"ld_{k}") for k in ("const", "text", "image", "attn", "route")}
        s_patch = [sem(f"patch{i}") for i in range(RING)]
        names = """fold_done fold_step setup_step mask_ready
            hid_ready enc_mm enc_ready sim_mm top_ready exp_ready prob_step prob_ready pt_mm pt_ready
            emb_mm emb_ready
            conv_mm conv_ready ctr_mm ctr_ready var_mm root_ready recip_ready spread_mm norm_ready
            dense_mm img_ready bias_mm bias_ready
            ctr1_mm ctr1_ready var1_mm root1_ready recip1_ready spread1_mm x1_ready nx1_ready hx_ready
            pre_mm gate_ready
            qk_mm q_ready k_ready lin_mm loc_ready vT_ready vt_mm v_ready s_mm soft_step sum_step shifted_ready
            expd_ready p_ready pp_mm pp_ready av_mm at_ready out_mm h2_ready
            ctr2_mm ctr2_ready var2_mm root2_ready recip2_ready spread2_mm x2_ready res_ready xf_ready sign_ready
            turn_mm xf_out res_out score_mm key_step choice_ready
            sig_red sig_step sig_ready
            cnt_ready scan_ready place_step route_mm route_dve used_ready owner_ready slots_ready
            rows_stored fetch_ready index_ready slot_waited slot_step place_1h token_mm scale_step
            turn3_mm x3_ready h3_mm cell_ready fill_ready wait_carried look_step prep_step start_ready
            frac_ready inside_ready spline_ready y_mm y_ready
            row_ready row_waited scale_ready""".split()
        s = {name: sem(name) for name in names}
        s_sig = [sem(f"sig{i}") for i in range(WR)]
        s_rows = [sem(f"rows{i}") for i in range(WR)]
        s_wts = [sem(f"wts{i}") for i in range(WR)]
        s_stored = [sem(f"stored{i}") for i in range(WR)]

        COLS = dict(w1=0, b1=1, b2=2, conv_b=3, tok_gamma=4, tok_beta=5, dense_b=6, ffn_gamma=7, ffn_beta=8)

        def col(name):
            return cols[:, COLS[name]:COLS[name] + 1]

        def cols_of(g, width):
            return bass.ds(g * width, width)

        sig_buf = wts[:, :, 0:SIG_C, 0:D]
        block = ctx.enter_context(nc.Block())

        @block.sync
        def _(sp):
            sp.dma_start(x_txt[:, :], t["x_row"].partition_broadcast(P)).then_inc(s_ld["text"], 16)
            for name, dst in (("cols", cols), ("w2", w2), ("bins_t", bins_t), ("x_col", x_col), ("bins", bins)):
                sp.dma_start(dst[:, :], t[name]).then_inc(s_ld["text"], 16)
            sp.dma_start(ident[:, :], t["ident"]).then_inc(s_ld["const"], 16)
            sp.dma_start(centre[:, :], t["centre"]).then_inc(s_ld["const"], 16)
            sp.dma_start(c128[:, :], t["c128"]).then_inc(s_ld["const"], 16)
            sp.dma_start(eps[:, :], t["eps"]).then_inc(s_ld["const"], 16)
            sp.dma_start(w5, t["w5"]).then_inc(s_ld["image"], 16)
            sp.dma_start(dense[:, :], t["dense"]).then_inc(s_ld["image"], 16)
            def load_sig(c):
                if c >= WR:
                    sp.wait_ge(s["sig_red"], c - WR + 1)
                sp.dma_start(sig_buf[:, c % WR],
                             t["packs"][c * SIG_C:(c + 1) * SIG_C, :, 0:D].rearrange("e p h -> p e h")
                             ).then_inc(s_sig[c % WR], 16)

            for c in range(WR):
                load_sig(c)
            for g in range(NG):
                if g == RING:
                    for c in range(WR, NG):
                        load_sig(c)
                if g >= RING:
                    sp.wait_ge(s["conv_mm"], g - RING + 1)
                sp.dma_start(patches[:, g % RING], t["patches"][g]).then_inc(s_patch[g % RING], 16)
            for g in range(NT2):
                sp.wait_ge(s["res_out"], g + 1)
                sp.wait_ge(s["scale_ready"], g + 1)
                sp.dma_start(token_rows[g * TT:(g + 1) * TT, :].rearrange("(i p) c -> p i c", p=P),
                             rows[:, 2 * g:2 * g + 2, :]).then_inc(s["rows_stored"], 16)

            sp.wait_ge(s["owner_ready"], 1)
            sp.wait_ge(s["sig_red"], NG)

            def load_packs(g, par):
                free_again(sp, s["y_mm"], g, WR)
                for j in range(TI):
                    e = sp.value_load(owner[0:1, bass.ds(g * TI + j, 1)], min_val=0, max_val=E - 1)
                    sp.dma_start(wts[:, par, j, :], t["packs"][bass.ds(e, 1)].rearrange("e p w -> (e p) w")
                                 ).then_inc(s_wts[par], 16)

            sp.wait_ge(s["used_ready"], 1)
            tiles = sp.value_load(used[0:1, 0:1], min_val=NI_SURE * TI - TI + 1, max_val=NTILE)
            pipelined(sp, NI, [(0, where_used(sp, tiles, load_packs))], unroll=WR, sure=NI_SURE)

            def stored(g, par):
                sp.wait_ge(s_stored[par], 32 * (g // WR + 1))

            for g in range(NI_SURE - WR, NI):
                where_used(sp, tiles, stored)(g, g % WR)

        @block.gpsimd
        def _(pool):
            for name, dst in (("before", before), ("upto", upto), ("ones_bf", ones_bf), ("tie", tie),
                              ("tile_no", tile_no), ("count_up", count_up),
                              ("p_plus1", p_plus1)):
                pool.dma_start(dst[:, :], t[name]).then_inc(s_ld["route"], 16)
            pool.dma_start(scale_row[:, :], t["scale"].partition_broadcast(P)).then_inc(s_ld["route"], 16)

            pool.wait_ge(s_ld["image"], 32)
            for k in range(1, 5):
                if k > 1:
                    pool.wait_ge(s["fold_step"], k - 1)
                pool.tensor_tensor(w5[:, 0, :], w5[:, 0, :], w5[:, k, :], ALU.add
                                   ).then_inc(s["fold_step"] if k < 4 else s["fold_done"], 1)

            def add_norm(g, par):
                pool.wait_ge(s["x1_ready"], g + 1)
                here = hT[:, cols_of(g, TT)]
                pool.tensor_tensor(here, here, s_d[:, par, 0:TT], ALU.add).then_inc(s["hx_ready"], 1)

            pipelined(pool, NT2, [(3, add_norm)])

            def add_res(g, par):
                pool.wait_ge(s["x2_ready"], g + 1)
                free_again(pool, s["turn_mm"], g, 2)
                pool.tensor_tensor(s_e[:, par, 0:TT], h2T[:, cols_of(g, TT)], s_d[:, par, 0:TT],
                                   ALU.add).then_inc(s["res_ready"], 1)

            pipelined(pool, NT2, [(5, add_res)])

            pool.wait_ge(s["rows_stored"], 16 * NT2)
            pool.wait_ge(s["fetch_ready"], 1)

            def fetch(g, par):
                if not fixed(g) or g >= WR:
                    pool.wait_ge(s_stored[par], (g - par) * (32 // WR))
                    pool.sem_inc(s["slot_waited"], 1)
                for k, src in enumerate((fetch_at, store_at)):
                    pool.tensor_copy(at_now[:, par, 2 * k:2 * k + 2], src[:, bass.ds(g * 2, 2)]
                                     ).then_inc(s["index_ready"], 1)
                pool.wait_ge(s["index_ready"], 2 * g + 2)
                pool.sem_inc(s["slot_waited"], 1)
                for a in range(2):
                    pool.indirect_dma_start(
                        rows_in[:, par, a, :], None, token_rows[:, :],
                        bass.IndirectOffsetOnAxis(ap=at_now[:, par, a:a + 1], axis=0)).then_inc(s_rows[par], 16)

            def position(g, par):
                pool.wait_ge(s["prep_step"], 2 * g + 2)
                free_again(pool, s["inside_ready"], g, 2)
                here = frac[:, par % 2]
                pool.tensor_tensor(here, cell_at[:, par % 2], c128[:, 1:2].broadcast_to([P, SI]), ALU.subtract
                                   ).then_inc(s["start_ready"], 1)
                pool.wait_ge(s["start_ready"], g + 1)
                pool.tensor_tensor(here, s_b[:, par % 2, 0:SI], here, ALU.subtract).then_inc(s["frac_ready"], 1)

            def inside_cell(g, par):
                pool.wait_ge(s["look_step"], LEVELS * g + LEVELS)
                pool.wait_ge(s["frac_ready"], g + 1)
                free_again(pool, s["spline_ready"], g, 2)
                pool.tensor_tensor(inside[:, par % 2], frac[:, par % 2], look[:, par % 2, 1, 0], ALU.mult
                                   ).then_inc(s["inside_ready"], 1)

            def store(g, par):
                pool.wait_ge(s["y_ready"], 2 * g + 2)
                here = rows_out[:, par % 2]
                pool.tensor_tensor(here, here, rows_in[:, par, :, D:2 * D], ALU.add).then_inc(s["row_ready"], 1)
                pool.wait_ge(s["row_ready"], g + 1)
                pool.sem_inc(s["row_waited"], 1)
                for a in range(2):
                    pool.indirect_dma_start(
                        out[:, :], bass.IndirectOffsetOnAxis(ap=at_now[:, par, 2 + a:3 + a], axis=0),
                        here[:, a, :], None, bounds_check=N - 1, oob_is_err=False).then_inc(s_stored[par], 16)

            pool.wait_ge(s["used_ready"], 1)
            tiles = pool.value_load(used[0:1, 0:1], min_val=NI_SURE * TI - TI + 1, max_val=NTILE)
            pipelined(pool, NI, [(lag, where_used(pool, tiles, stage)) for lag, stage in
                                 ((2, position), (4, store), (3, inside_cell), (0, fetch))],
                      unroll=WR, sure=NI_SURE, ordered=True)

        @block.scalar
        def _(act):
            for name, dst in (("rel", rel), ("causal", causal), ("veil", veil), ("expand", expand)):
                act.dma_start(dst[:, :], t[name]).then_inc(s_ld["attn"], 16)
            act.dma_start(project[:, :, :], t["project"]).then_inc(s_ld["attn"], 16)
            act.dma_start(pbm[:, :], t["pbm"].partition_broadcast(P)).then_inc(s_ld["attn"], 16)
            act.wait_ge(s_ld["text"], 16 * 6)

            def hidden(g, par):
                free_again(act, s["enc_mm"], g, 2)
                act.activation(s_a[:, par, 0:GT], x_txt[:, cols_of(g, GT)], ACT.Relu, bias=col("b1"),
                               scale=col("w1")).then_inc(s["hid_ready"], 1)

            def encoded(g, par):
                act.wait_ge(s["enc_mm"], g + 1)
                free_again(act, s["sim_mm"], g, 2)
                act.activation(s_b[:, par, 0:GT], bank[6 * par][:, 0:GT], ACT.Identity, bias=col("b2")
                               ).then_inc(s["enc_ready"], 1)

            def exps(g, par):
                act.wait_ge(s["top_ready"], g + 1)
                free_again(act, s["prob_ready"], g, 2)
                act.activation(s_c[:, par, 0:NB], bank[4 + par][:, 0:NB], ACT.Exp, bias=small[:, par, 0:1],
                               accum_out=small[:, par, 1:2]).then_inc(s["exp_ready"], 1)

            def embedded(g, par):
                act.wait_ge(s["emb_mm"], g + 1)
                act.activation(hT[:, cols_of(g, GS)].rearrange("p (b s) -> p b s", s=S)[:, :, S_IMG:S],
                               bank[3][:, 0:GT].rearrange("p (b s) -> p b s", s=S_TXT), ACT.Copy
                               ).then_inc(s["emb_ready"], 1)

            pipelined(act, NG, [(0, hidden), (2, encoded), (4, exps), (6, embedded)])

            def conv_out(g, par):
                act.wait_ge(s["conv_mm"], g + 1)
                free_again(act, s["ctr_mm"], g, 2)
                act.activation(s_a[:, par, 0:GI], bank[0][:, 0:GI], ACT.Identity, bias=col("conv_b")
                               ).then_inc(s["conv_ready"], 1)

            def centred(g, par):
                act.wait_ge(s["ctr_mm"], g + 1)
                free_again(act, s["norm_ready"], g, 2)
                act.activation(s_b[:, par, 0:GI], bank[1][:, 0:GI], ACT.Copy).then_inc(s["ctr_ready"], 1)
                act.activation(s_c[:, par, 0:GI], bank[1][:, 0:GI], ACT.Square).then_inc(s["ctr_ready"], 1)

            def root(g, par):
                act.wait_ge(s["var_mm"], g + 1)
                free_again(act, s["recip_ready"], g, 2)
                act.activation(roots[0:HI, par, 0:2], bank[2][0:HI, 0:2], ACT.Sqrt, bias=eps[0:HI, 0:1]
                               ).then_inc(s["root_ready"], 1)

            def image_out(g, par):
                act.wait_ge(s["dense_mm"], g + 1)
                act.activation(hT[:, cols_of(g, GS)].rearrange("p (b s) -> p b s", s=S)[:, :, 0:S_IMG],
                               bank[4][:, 0:GI].rearrange("p (b s) -> p b s", s=S_IMG), ACT.Identity,
                               bias=dense_bias[:, 0:1]).then_inc(s["img_ready"], 1)

            act.wait_ge(s_ld["attn"], 16 * 6)
            act.activation(mask[:, :], rel[:, :], ACT.Sigmoid, bias=pbm[0:S, :]).then_inc(s["mask_ready"], 1)
            act.wait_ge(s["bias_ready"], 1)
            act.wait_ge(s_ld["const"], 16 * 4)
            pipelined(act, NG, [(0, conv_out), (1, centred), (2, root), (4, image_out)])

            def centred1(g, par):
                act.wait_ge(s["ctr1_mm"], g + 1)
                act.activation(ctr1[:, cols_of(g, TT)], bank[0][:, 0:TT], ACT.Copy).then_inc(s["ctr1_ready"], 1)
                free_again(act, s["var1_mm"], g, 2)
                act.activation(s_c[:, par, 0:TT], bank[0][:, 0:TT], ACT.Square).then_inc(s["ctr1_ready"], 1)

            def root1(g, par):
                act.wait_ge(s["var1_mm"], g + 1)
                free_again(act, s["recip1_ready"], g, 2)
                v = bank[1][:, 0:2]
                act.activation(roots[:, par, 0:2], v, ACT.Sqrt, bias=eps[:, 1:2]).then_inc(s["root1_ready"], 1)
                act.activation(roots[:, par, 2:4], v, ACT.Sqrt, bias=eps[:, 2:3], scale=1.0 + EPS
                               ).then_inc(s["root1_ready"], 1)

            pipelined(act, NT2, [(0, centred1), (1, root1)])

            def gates(g, par):
                act.wait_ge(s["pre_mm"], g + 1)
                act.activation(gate_loc[:, cols_of(g, GS)], bank[4 + par][:, 0:GS], ACT.Gelu
                               ).then_inc(s["gate_ready"], 1)
                act.activation(gate_v[:, cols_of(g, GS)], bank[6 + par][:, 0:GS], ACT.Gelu
                               ).then_inc(s["gate_ready"], 1)

            pipelined(act, NG, [(0, gates)])

            def q_out(g, par):
                act.wait_ge(s["qk_mm"], g + 1)
                free_again(act, s["s_mm"], g, 2)
                act.activation(s_a[0:QK, par], bank[0][0:QK, 0:GS], ACT.Copy).then_inc(s["q_ready"], 1)

            def v_out(g, par):
                act.wait_ge(s["vt_mm"], g + 1)
                free_again(act, s["av_mm"], g, 2)
                act.activation(s_v[0:S, par], bank[3][0:S, :], ACT.Copy).then_inc(s["v_ready"], 1)

            def soft_exp(g, par):
                act.wait_ge(s["shifted_ready"], g + 1)
                act.activation(s_d[0:S, par], s_d[0:S, par], ACT.Exp).then_inc(s["expd_ready"], 1)

            def p_out(g, par):
                act.wait_ge(s["pp_mm"], g + 1)
                free_again(act, s["av_mm"], g, 2)
                act.activation(s_c[0:S, par], bank[5][0:S, 0:GS], ACT.Copy).then_inc(s["pp_ready"], 1)

            def attended(g, par):
                act.wait_ge(s["av_mm"], g + 1)
                free_again(act, s["out_mm"], g, 2)
                act.activation(s_e[:, par], bank[6][:, 0:GS], ACT.Copy).then_inc(s["at_ready"], 1)

            pipelined(act, NG, [(5, attended), (3, v_out), (4, p_out), (2, soft_exp), (0, q_out)], ordered=True)

            def centred2(g, par):
                act.wait_ge(s["ctr2_mm"], g + 1)
                act.activation(ctr2[:, cols_of(g, TT)], bank[0][:, 0:TT], ACT.Copy).then_inc(s["ctr2_ready"], 1)
                free_again(act, s["var2_mm"], g, 2)
                act.activation(s_c[:, par, 0:TT], bank[0][:, 0:TT], ACT.Square).then_inc(s["ctr2_ready"], 1)

            def root2(g, par):
                act.wait_ge(s["var2_mm"], g + 1)
                free_again(act, s["recip2_ready"], g, 2)
                v = bank[1][:, 0:2]
                act.activation(roots[:, par, 0:2], v, ACT.Sqrt, bias=eps[:, 1:2]).then_inc(s["root2_ready"], 1)
                act.activation(roots[:, par, 2:4], v, ACT.Sqrt, bias=eps[:, 2:3], scale=1.0 + EPS
                               ).then_inc(s["root2_ready"], 1)

            def affine(g, par):
                act.wait_ge(s["x2_ready"], g + 1)
                free_again(act, s["turn_mm"], g, 2)
                act.activation(s_c2[:, par], s_xn[:, par], ACT.Identity, bias=col("ffn_beta"),
                               scale=col("ffn_gamma")).then_inc(s["xf_ready"], 1)
                act.wait_ge(s["xf_ready"], g + 1)
                act.activation(signs[:, par], s_c2[:, par], ACT.Sign).then_inc(s["sign_ready"], 1)

            def turned(g, par):
                act.wait_ge(s["turn_mm"], g + 1)
                pair = rows[:, bass.ds(g * 2, 2), :]
                act.activation(pair[:, :, 0:D], bank[4][:, 0:TT].rearrange("p (i d) -> p i d", d=D), ACT.Copy
                               ).then_inc(s["xf_out"], 1)
                act.activation(pair[:, :, D:2 * D], bank[5][:, 0:TT].rearrange("p (i d) -> p i d", d=D), ACT.Copy
                               ).then_inc(s["res_out"], 1)

            s_xn = s_v[:, :, 0:TT]
            s_c2 = s_a[:, :, 0:TT]
            pipelined(act, NT2, [(1, centred2), (3, root2), (5, affine), (7, turned)])

            def x_out(g, par):
                act.wait_ge(s["turn3_mm"], g + 1)
                free_again(act, s["h3_mm"], g, 2)
                act.activation(s_a[:, par % 2, 0:SI], bank[0][:, 0:SI], ACT.Copy).then_inc(s["x3_ready"], 1)

            def cell(g, par):
                act.wait_ge(s["h3_mm"], g + 1)
                free_again(act, s["frac_ready"], g, 2)
                act.activation(s_b[:, par % 2, 0:SI], bank[1][:, 0:SI], ACT.Sigmoid).then_inc(s["cell_ready"], 1)

            def fill(g, par):
                free_again(act, s["spline_ready"], g, 2)
                for a in range(2):
                    tab = wts[:, par, :, 2 * D + a * GRID:2 * D + (a + 1) * GRID:2]
                    act.activation(look[:, par % 2, a].rearrange("p k (j n) -> p k j n", n=ST),
                                   spread_to(tab.rearrange("p j k -> p k j"), 3, ST),
                                   ACT.Copy).then_inc(s["fill_ready"], 1)

            def y_out(g, par):
                act.wait_ge(s["y_mm"], g + 1)
                if not fixed(g) or g >= 2:
                    before_last = (par - 2) % WR
                    act.wait_ge(s_stored[before_last], (g - 2 - before_last) * (32 // WR) + 32)
                for a in range(2):
                    act.activation(rows_out[:, par % 2, a], bank[2][:, a * D:(a + 1) * D], ACT.Copy,
                                   scale=rows_in[:, par, a, SCL:SCL + 1]).then_inc(s["y_ready"], 1)

            act.wait_ge(s["used_ready"], 1)
            tiles = act.value_load(used[0:1, 0:1], min_val=NI_SURE * TI - TI + 1, max_val=NTILE)
            pipelined(act, NI, [(lag, where_used(act, tiles, stage)) for lag, stage in
                                ((0, x_out), (0, cell), (0, fill), (2, y_out))],
                      unroll=WR, sure=NI_SURE, ordered=True)

        @block.tensor
        def _(pe):
            def mm(o, l, r, start=True, stop=True):
                return pe.matmul(o, l, r, start=start, stop=stop)

            pe.wait_ge(s_ld["text"], 16 * 6)
            pe.wait_ge(s_ld["const"], 16 * 4)

            def encode(g, par):
                pe.wait_ge(s["hid_ready"], g + 1)
                free_again(pe, s["enc_ready"], g, 2)
                mm(bank[6 * par][:, 0:GT], w2[:, :], s_a[:, par, 0:GT]).then_inc(s["enc_mm"], 1)

            def similar(g, par):
                pe.wait_ge(s["enc_ready"], g + 1)
                free_again(pe, s["exp_ready"], g, 2)
                mm(bank[4 + par][:, 0:NB], s_b[:, par, 0:GT], bins_t[:, :]).then_inc(s["sim_mm"], 1)

            def turn_p(g, par):
                pe.wait_ge(s["prob_ready"], g + 1)
                free_again(pe, s["pt_ready"], g, 1)
                pe.transpose(bank[2][:, 0:GT], s_d[:, par, 0:P], ident[:, :]).then_inc(s["pt_mm"], 1)

            def embed(g, par):
                pe.wait_ge(s["pt_ready"], g + 1)
                free_again(pe, s["emb_ready"], g, 1)
                mm(bank[3][:, 0:GT], bins[:, :], s_e[0:BINS, par, 0:GT]).then_inc(s["emb_mm"], 1)

            pipelined(pe, NG, [(1, encode), (3, similar), (5, turn_p), (6, embed)])

            pe.wait_ge(s_ld["image"], 32)
            pe.wait_ge(s["emb_ready"], NG)
            mm(bank[7][:, 0:1], dense[:, :], col("tok_beta")).then_inc(s["bias_mm"], 1)
            pe.wait_ge(s["fold_done"], 1)
            folded = w5[:, 0, :].rearrange("p (k n) -> p k n", k=KCH)

            def conv(g, par):
                r = par % RING
                pe.wait_ge(s_patch[r], (g - par) * (16 // RING) + 16)
                free_again(pe, s["conv_ready"], g, 1)
                for k in range(KCH):
                    last = mm(bank[0][:, 0:GI], folded[:, k, :], patches[:, r, k, :], k == 0, k == KCH - 1)
                last.then_inc(s["conv_mm"], 1)

            def centre_y(g, par):
                pe.wait_ge(s["conv_ready"], g + 1)
                if not fixed(g) or g >= 1:
                    pe.wait_ge(s["ctr_ready"], 2 * g)
                mm(bank[1][:, 0:GI], centre[:, :], s_a[:, par % 2, 0:GI]).then_inc(s["ctr_mm"], 1)

            def variance(g, par):
                pe.wait_ge(s["ctr_ready"], 2 * g + 2)
                free_again(pe, s["root_ready"], g, 1)
                for j in range(2):
                    last = mm(bank[2][0:HI, j:j + 1], s_c[:, par % 2, j * HI:(j + 1) * HI], c128[:, 0:1])
                last.then_inc(s["var_mm"], 1)

            def spread(g, par):
                pe.wait_ge(s["recip_ready"], g + 1)
                free_again(pe, s["norm_ready"], g, 1)
                for j in range(2):
                    last = mm(bank[3][:, j * HI:(j + 1) * HI],
                              recips[0:HI, par % 2, j:j + 1].broadcast_to([HI, P]), ident[0:HI, 0:HI])
                last.then_inc(s["spread_mm"], 1)

            def dense_mm(g, par):
                pe.wait_ge(s["norm_ready"], g + 1)
                free_again(pe, s["img_ready"], g, 1)
                mm(bank[4][:, 0:GI], dense[:, :], s_d[:, par % 2, 0:GI]).then_inc(s["dense_mm"], 1)

            pipelined(pe, NG, [(0, conv), (1, centre_y), (2, variance), (3, spread), (4, dense_mm)], unroll=RING)

            pe.wait_ge(s["img_ready"], NG)

            def centre_h(g, par):
                if not fixed(g) or g >= 1:
                    pe.wait_ge(s["ctr1_ready"], 2 * g)
                mm(bank[0][:, 0:TT], centre[:, :], hT[:, cols_of(g, TT)]).then_inc(s["ctr1_mm"], 1)

            def variance1(g, par):
                pe.wait_ge(s["ctr1_ready"], 2 * g + 2)
                if not fixed(g) or g >= 1:
                    pe.wait_ge(s["root1_ready"], 2 * g)
                for j in range(2):
                    last = mm(bank[1][:, j:j + 1], s_c[:, par, j * P:(j + 1) * P], c128[:, 0:1])
                last.then_inc(s["var1_mm"], 1)

            def spread1(g, par):
                pe.wait_ge(s["recip1_ready"], g + 1)
                free_again(pe, s["nx1_ready"], g, 2)
                for a in range(2):
                    for j in range(2):
                        last = mm(bank[2 + 2 * par + a][:, j * P:(j + 1) * P],
                                  recips[:, par, 2 * a + j:2 * a + j + 1].broadcast_to([P, P]), ident[:, :])
                last.then_inc(s["spread1_mm"], 1)

            pipelined(pe, NT2, [(0, centre_h), (1, variance1), (3, spread1)])

            pe.wait_ge(s_ld["attn"], 16 * 6)

            pe.wait_ge(s["nx1_ready"], NT2)

            def gate_mm(g, par):
                if not fixed(g) or g >= 2:
                    pe.wait_ge(s["gate_ready"], 2 * g - 2)
                mm(bank[4 + par][:, 0:GS], expand[:, 2 * P:3 * P], nxT[:, cols_of(g, GS)])
                mm(bank[6 + par][:, 0:GS], expand[:, 3 * P:4 * P], nxT[:, cols_of(g, GS)]
                   ).then_inc(s["pre_mm"], 1)

            pipelined(pe, NG, [(0, gate_mm)])

            pe.wait_ge(s["gate_ready"], 2 * NG)

            def qk_lin(g, par):
                here = nxT[:, cols_of(g, GS)]
                free_again(pe, s["q_ready"], g, 1)
                free_again(pe, s["k_ready"], g, 1)
                mm(bank[0][0:64, 0:GS], expand[:, 4 * P:4 * P + 64], here).then_inc(s["qk_mm"], 1)
                free_again(pe, s["vT_ready"], g, 1)
                mm(bank[1][:, 0:GS], expand[:, 0:P], here)
                mm(bank[2][:, 0:GS], expand[:, P:2 * P], here).then_inc(s["lin_mm"], 1)

            def values_scores(g, par):
                pe.wait_ge(s["vT_ready"], g + 1)
                free_again(pe, s["v_ready"], g, 1)
                for j in range(GB):
                    last = pe.transpose(bank[3][0:S, j * D:(j + 1) * D], s_b[:, par, j * S:(j + 1) * S], ident[:, :])
                last.then_inc(s["vt_mm"], 1)
                pe.wait_ge(s["q_ready"], g + 1)
                pe.wait_ge(s["k_ready"], g + 1)
                if not fixed(g) or g >= 1:
                    pe.wait_ge(s["soft_step"], 2 * g - 1)
                for j in range(GB):
                    at = slice(j * S, (j + 1) * S)
                    last = mm(bank[4][0:S, at], s_a[0:QK, par, at], s_f[0:QK, par, at])
                last.then_inc(s["s_mm"], 1)

            def turn_probs(g, par):
                pe.wait_ge(s["p_ready"], g + 1)
                free_again(pe, s["pp_ready"], g, 1)
                for j in range(GB):
                    at = slice(j * S, (j + 1) * S)
                    last = pe.transpose(bank[5][0:S, at], s_g[0:S, par, at], ident[0:S, 0:S])
                last.then_inc(s["pp_mm"], 1)

            def attend(g, par):
                pe.wait_ge(s["pp_ready"], g + 1)
                pe.wait_ge(s["v_ready"], g + 1)
                free_again(pe, s["at_ready"], g, 1)
                for j in range(GB):
                    at = slice(j * S, (j + 1) * S)
                    last = mm(bank[6][:, at], s_v[0:S, par, j * D:(j + 1) * D], s_c[0:S, par, at])
                last.then_inc(s["av_mm"], 1)

            def project_mm(g, par):
                pe.wait_ge(s["at_ready"], g + 1)
                free_again(pe, s["h2_ready"], g, 1)
                mm(bank[7][:, 0:GS], project[:, 0, :], gate_loc[:, cols_of(g, GS)], True, False)
                mm(bank[7][:, 0:GS], project[:, 1, :], s_e[:, par], False, True).then_inc(s["out_mm"], 1)

            pipelined(pe, NG, [(5, attend), (4, turn_probs), (6, project_mm), (2, values_scores), (0, qk_lin)],
                      ordered=True)

            pe.wait_ge(s["h2_ready"], NG)
            pe.wait_ge(s["sig_ready"], 1)

            def centre_2(g, par):
                if not fixed(g) or g >= 1:
                    pe.wait_ge(s["ctr2_ready"], 2 * g)
                mm(bank[0][:, 0:TT], centre[:, :], h2T[:, cols_of(g, TT)]).then_inc(s["ctr2_mm"], 1)

            def variance2(g, par):
                pe.wait_ge(s["ctr2_ready"], 2 * g + 2)
                if not fixed(g) or g >= 1:
                    pe.wait_ge(s["root2_ready"], 2 * g)
                for j in range(2):
                    last = mm(bank[1][:, j:j + 1], s_c[:, par, j * P:(j + 1) * P], c128[:, 0:1])
                last.then_inc(s["var2_mm"], 1)

            def spread2(g, par):
                pe.wait_ge(s["recip2_ready"], g + 1)
                free_again(pe, s["x2_ready"], g, 1)
                for a in range(2):
                    for j in range(2):
                        last = mm(bank[2 + a][:, j * P:(j + 1) * P],
                                  recips[:, par, 2 * a + j:2 * a + j + 1].broadcast_to([P, P]), ident[:, :])
                last.then_inc(s["spread2_mm"], 1)

            def turn_score(g, par):
                pe.wait_ge(s["xf_ready"], g + 1)
                pe.wait_ge(s["sign_ready"], g + 1)
                pe.wait_ge(s["res_ready"], g + 1)
                free_again(pe, s["res_out"], g, 1)
                if not fixed(g) or g >= 1:
                    pe.wait_ge(s["key_step"], 2 * g - 1)
                for j in range(2):
                    at = slice(j * P, (j + 1) * P)
                    mm(bank[6][:, j * E:(j + 1) * E], signs[:, par, at], w_cl[:, :], True, False)
                    mm(bank[6][:, j * E:(j + 1) * E], signs[:, par, at], w_tile[:, :], False, True
                       ).then_inc(s["score_mm"], 1)
                for j in range(2):
                    at = slice(j * P, (j + 1) * P)
                    pe.transpose(bank[4][:, at], s_a[:, par, at], ident[:, :])
                    last = pe.transpose(bank[5][:, at], s_e[:, par, at], ident[:, :])
                last.then_inc(s["turn_mm"], 1)

            pipelined(pe, NT2, [(4, spread2), (6, turn_score), (2, variance2), (0, centre_2)], ordered=True)

            pe.wait_ge(s["cnt_ready"], 2)
            pe.wait_ge(s_ld["route"], 16 * 8)
            mm(bank[0][0:E, 0:1], cnt[:, :], ones_bf[:, 0:1]).then_inc(s["route_mm"], 1)
            pe.wait_ge(s["route_dve"], 3)
            mm(bank[1][:, 0:E], ntile[:, 1:2].broadcast_to([E, P]), before[0:E, 0:E], True, False)
            mm(bank[1][:, 0:E], before[:, :], cnt[:, :], False, True)
            mm(bank[7][:, 0:1], ones_bf[0:E, :], ntile[:, 0:1])
            mm(bank[2][0:E, 0:1], upto[:, :], ntile[:, 0:1]).then_inc(s["route_mm"], 1)
            pe.wait_ge(s["route_dve"], 5)
            mm(bank[3][:, 0:NTILE], ones_bf[0:E, :], started[:, :]).then_inc(s["route_mm"], 1)

            pe.wait_ge(s["res_out"], NT2)
            for i in range(T):
                pe.wait_ge(s["place_1h"], 1 if i < T // 2 else 2)
                last = mm(bank[4][:, 0:2 * SC], place_1h[:, i, :], col_tok[:, i, :], i == 0, i == T - 1)
            last.then_inc(s["token_mm"], 1)


            def turn_rows(g, par):
                pe.wait_ge(s_rows[par], (g - par) * (32 // WR) + 32)
                free_again(pe, s["x3_ready"], g, 1)
                for a in range(2):
                    last = pe.transpose(bank[0][:, a * P:(a + 1) * P], rows_in[:, par, a, 0:D], ident[:, :])
                last.then_inc(s["turn3_mm"], 1)

            def down(g, par):
                pe.wait_ge(s_wts[par], (g - par) * (16 * TI // WR) + 16 * TI)
                pe.wait_ge(s["x3_ready"], g + 1)
                free_again(pe, s["cell_ready"], g, 1)
                for j in range(TI):
                    at = slice(j * ST, (j + 1) * ST)
                    last = mm(bank[1][:, at], wts[:, par, j, 0:D], s_a[:, par % 2, at])
                last.then_inc(s["h3_mm"], 1)

            def up(g, par):
                pe.wait_ge(s["spline_ready"], g + 1)
                if not fixed(g) or g >= 1:
                    pe.wait_ge(s["y_ready"], 2 * g)
                for j in range(TI):
                    a, q = j // 4, j % 4
                    last = mm(bank[2][q * ST:(q + 1) * ST, a * D:(a + 1) * D],
                              s_c[:, par % 2, j * ST:(j + 1) * ST], wts[:, par, j, D:2 * D])
                last.then_inc(s["y_mm"], 1)

            pe.wait_ge(s["used_ready"], 1)
            tiles = pe.value_load(used[0:1, 0:1], min_val=NI_SURE * TI - TI + 1, max_val=NTILE)
            pipelined(pe, NI, [(lag, where_used(pe, tiles, stage)) for lag, stage in
                               ((0, turn_rows), (0, down), (2, up))],
                      unroll=WR, sure=NI_SURE, ordered=True)

        @block.vector
        def _(dve):
            dve.wait_ge(s_ld["text"], 16 * 6)
            dve.tensor_scalar(is0[:, :], x_col[:, :], 0.0, None, ALU.is_equal).then_inc(s["setup_step"], 1)
            dve.tensor_scalar(not0[:, :], x_col[:, :], 0.0, None, ALU.not_equal).then_inc(s["setup_step"], 1)
            dve.wait_ge(s["setup_step"], 2)

            dve.memset(s_d[:, :, BINS:P], 0.0).then_inc(s["setup_step"], 1)
            dve.wait_ge(s["setup_step"], 3)

            def top(g, par):
                dve.wait_ge(s["sim_mm"], g + 1)
                dve.tensor_reduce(small[:, par, 0:1], bank[4 + par][:, 0:NB], AX.X, ALU.max, negate=True
                                  ).then_inc(s["top_ready"], 1)

            def probs(g, par):
                dve.wait_ge(s["exp_ready"], g + 1)
                free_again(dve, s["pt_mm"], g, 2)
                dve.reciprocal(small[:, par, 2:3], small[:, par, 1:2]).then_inc(s["prob_step"], 1)
                dve.tensor_copy(s_d[:, par, 0:1], is0[:, bass.ds(g, 1)]).then_inc(s["prob_step"], 1)
                dve.tensor_copy(small[:, par, 3:4], not0[:, bass.ds(g, 1)]).then_inc(s["prob_step"], 1)
                dve.wait_ge(s["prob_step"], 3 * g + 3)
                dve.tensor_scalar(s_d[:, par, 1:BINS], s_c[:, par, 0:NB], small[:, par, 2:3],
                                  small[:, par, 3:4], ALU.mult, ALU.mult).then_inc(s["prob_ready"], 1)

            def p_out(g, par):
                dve.wait_ge(s["pt_mm"], g + 1)
                free_again(dve, s["emb_mm"], g, 2)
                dve.tensor_copy(s_e[0:BINS, par, 0:GT], bank[2][0:BINS, 0:GT]).then_inc(s["pt_ready"], 1)

            def sum_wd(g, par):
                dve.wait_ge(s_sig[par], (g - par) * (16 // WR) + 16)
                dve.tensor_reduce(sig_sum[:, bass.ds(g * SIG_C, SIG_C)], sig_buf[:, par], AX.X, ALU.add
                                  ).then_inc(s["sig_red"], 1)

            pipelined(dve, NG, [(3, lambda g, par: top(g, par % 2)), (4, lambda g, par: probs(g, par % 2)),
                                (5, lambda g, par: p_out(g, par % 2)), (4, sum_wd)], unroll=WR)

            dve.wait_ge(s["sig_red"], NG)

            def sign_of(dst, src, scratch):
                n = sign_of.n
                dve.tensor_scalar(scratch, src, 0.0, None, ALU.is_lt).then_inc(s["sig_step"], 1)
                dve.tensor_scalar(dst, src, 0.0, None, ALU.is_gt).then_inc(s["sig_step"], 1)
                dve.wait_ge(s["sig_step"], n + 2)
                dve.tensor_tensor(dst, dst, scratch, ALU.subtract).then_inc(s["sig_step"], 1)
                dve.wait_ge(s["sig_step"], n + 3)
                sign_of.n = n + 4
            sign_of.n = 0
            scr = keys[:, 0, 0:E]
            sign_of(sig_tile[:, :], sig_sum[:, :], scr)
            dve.tensor_reduce(sig_clsum[:, :], sig_tile[:, :].rearrange("p (c j) -> p c j", j=TPC), AX.X,
                              ALU.add).then_inc(s["sig_step"], 1)
            dve.wait_ge(s["sig_step"], 4)
            sign_of(sig_cl[:, :], sig_clsum[:, :], scr[:, 0:CL])
            dve.tensor_scalar(w_tile[:, :], sig_tile[:, :], float(TPC), None, ALU.mult).then_inc(s["sig_step"], 1)
            dve.tensor_scalar(w_cl[:, :].rearrange("p (c j) -> p c j", j=TPC),
                              spread_to(sig_cl[:, :], 2, TPC), CL * 4096.0, None, ALU.mult
                              ).then_inc(s["sig_ready"], 1)
            dve.wait_ge(s["sig_ready"], 1)

            dve.wait_ge(s["bias_mm"], 1)
            dve.tensor_tensor(dense_bias[:, :], bank[7][:, 0:1], col("dense_b"), ALU.add
                              ).then_inc(s["bias_ready"], 1)

            dve.wait_ge(s["mask_ready"], 1)
            dve.tensor_tensor(mask[:, :], mask[:, :], causal[:, :], ALU.mult).then_inc(s["setup_step"], 1)
            dve.wait_ge(s["setup_step"], 4)
            dve.tensor_tensor(mask[:, :], mask[:, :], veil[:, :], ALU.add).then_inc(s["setup_step"], 1)

            def recip(g, par):
                dve.wait_ge(s["root_ready"], g + 1)
                free_again(dve, s["spread_mm"], g, 2)
                dve.reciprocal(recips[0:HI, par, 0:2], roots[0:HI, par, 0:2]).then_inc(s["recip_ready"], 1)

            def norm(g, par):
                dve.wait_ge(s["spread_mm"], g + 1)
                dve.wait_ge(s["ctr_ready"], 2 * g + 2)
                free_again(dve, s["dense_mm"], g, 2)
                dve.scalar_tensor_tensor(out=s_d[:, par, 0:GI], in0=s_b[:, par, 0:GI], scalar=col("tok_gamma"),
                                         in1=bank[3][:, 0:GI], op0=ALU.mult, op1=ALU.mult
                                         ).then_inc(s["norm_ready"], 1)

            pipelined(dve, NG, [(2, recip), (3, norm)])

            def recip1(g, par):
                dve.wait_ge(s["root1_ready"], 2 * g + 2)
                free_again(dve, s["spread1_mm"], g, 2)
                dve.reciprocal(recips[:, par, 0:4], roots[:, par, 0:4]).then_inc(s["recip1_ready"], 1)

            def norm1(g, par):
                dve.wait_ge(s["spread1_mm"], g + 1)
                dve.wait_ge(s["ctr1_ready"], 2 * g + 2)
                free_again(dve, s["hx_ready"], g, 2)
                dve.tensor_tensor(s_d[:, par, 0:TT], ctr1[:, cols_of(g, TT)], bank[2 + 2 * par][:, 0:TT], ALU.mult
                                  ).then_inc(s["x1_ready"], 1)
                dve.tensor_tensor(nxT[:, cols_of(g, TT)], ctr1[:, cols_of(g, TT)], bank[3 + 2 * par][:, 0:TT], ALU.mult
                                  ).then_inc(s["nx1_ready"], 1)

            pipelined(dve, NT2, [(1, recip1), (3, norm1)])

            dve.wait_ge(s["hx_ready"], NT2)

            def kv(g, par):
                dve.wait_ge(s["qk_mm"], g + 1)
                free_again(dve, s["s_mm"], g, 2)
                dve.tensor_copy(s_f[0:QK, par], bank[0][KOFF:KOFF + QK, 0:GS]).then_inc(s["k_ready"], 1)
                dve.wait_ge(s["lin_mm"], g + 1)
                loc = gate_loc[:, cols_of(g, GS)]
                dve.tensor_tensor(loc, loc, bank[1][:, 0:GS], ALU.mult).then_inc(s["loc_ready"], 1)
                free_again(dve, s["vt_mm"], g, 2)
                dve.tensor_tensor(s_b[:, par], gate_v[:, cols_of(g, GS)], bank[2][:, 0:GS], ALU.mult
                                  ).then_inc(s["vT_ready"], 1)

            def shifted(g, par):
                dve.wait_ge(s["s_mm"], g + 1)
                x = s_d[0:S, par].rearrange("p (b k) -> p b k", k=S)
                free_again(dve, s["p_ready"], g, 2)
                dve.scalar_tensor_tensor(out=x, in0=bank[4][0:S, 0:GS].rearrange("p (b k) -> p b k", k=S),
                                         scalar=float(QK) ** -0.5,
                                         in1=spread_to(mask[:, :], 1, GB),
                                         op0=ALU.mult, op1=ALU.add).then_inc(s["soft_step"], 1)
                dve.wait_ge(s["soft_step"], 2 * g + 1)
                dve.tensor_reduce(small[0:S, par, 0:GB], x, AX.X, ALU.max).then_inc(s["soft_step"], 1)
                dve.wait_ge(s["soft_step"], 2 * g + 2)
                dve.tensor_tensor(x, x, spread_to(small[0:S, par, 0:GB], 2, S), ALU.subtract
                                  ).then_inc(s["shifted_ready"], 1)

            def normalised(g, par):
                dve.wait_ge(s["expd_ready"], g + 1)
                x = s_d[0:S, par].rearrange("p (b k) -> p b k", k=S)
                dve.tensor_reduce(small[0:S, par, 4:8], x, AX.X, ALU.add).then_inc(s["sum_step"], 1)
                dve.wait_ge(s["sum_step"], 2 * g + 1)
                dve.reciprocal(small[0:S, par, 4:8], small[0:S, par, 4:8]).then_inc(s["sum_step"], 1)
                dve.wait_ge(s["sum_step"], 2 * g + 2)
                free_again(dve, s["pp_mm"], g, 2)
                dve.tensor_tensor(s_g[0:S, par].rearrange("p (b k) -> p b k", k=S), x,
                                  spread_to(small[0:S, par, 4:8], 2, S), ALU.mult
                                  ).then_inc(s["p_ready"], 1)

            def add_out(g, par):
                dve.wait_ge(s["out_mm"], g + 1)
                dve.tensor_tensor(h2T[:, cols_of(g, GS)], hT[:, cols_of(g, GS)], bank[7][:, 0:GS], ALU.add
                                  ).then_inc(s["h2_ready"], 1)

            pipelined(dve, NG, [(3, normalised), (6, add_out), (2, shifted), (0, kv)], ordered=True)

            def recip2(g, par):
                dve.wait_ge(s["root2_ready"], 2 * g + 2)
                free_again(dve, s["spread2_mm"], g, 2)
                dve.reciprocal(recips[:, par, 0:4], roots[:, par, 0:4]).then_inc(s["recip2_ready"], 1)

            def norm2(g, par):
                dve.wait_ge(s["spread2_mm"], g + 1)
                dve.wait_ge(s["ctr2_ready"], 2 * g + 2)
                free_again(dve, s["res_ready"], g, 2)
                dve.tensor_tensor(s_d[:, par, 0:TT], ctr2[:, cols_of(g, TT)], bank[2][:, 0:TT], ALU.mult)
                free_again(dve, s["xf_ready"], g, 2)
                dve.tensor_tensor(s_v[:, par, 0:TT], ctr2[:, cols_of(g, TT)], bank[3][:, 0:TT], ALU.mult
                                  ).then_inc(s["x2_ready"], 1)

            def choose(g, par):
                dve.wait_ge(s["score_mm"], 2 * g + 2)
                key = keys[:, par].rearrange("p (i e) -> p i e", e=E)
                dve.tensor_tensor(key, bank[6][:, 0:2 * E].rearrange("p (i e) -> p i e", e=E),
                                  spread_to(tie[:, :], 1, 2), ALU.add).then_inc(s["key_step"], 1)
                dve.wait_ge(s["key_step"], 2 * g + 1)
                dve.tensor_reduce(best[:, par], key, AX.X, ALU.max).then_inc(s["key_step"], 1)
                dve.wait_ge(s["key_step"], 2 * g + 2)
                dve.tensor_tensor(onehot[:, :, bass.ds(g * 2, 2)].rearrange("p e i -> p i e"), key,
                                  spread_to(best[:, par], 2, E), ALU.is_equal).then_inc(s["choice_ready"], 1)
                dve.wait_ge(s["choice_ready"], g + 1)
                mine = scaled[:, par].rearrange("p (i e) -> p i e", e=E)
                dve.tensor_tensor(mine, onehot[:, :, bass.ds(g * 2, 2)].rearrange("p e i -> p i e"),
                                  spread_to(scale_row[:, :], 1, 2), ALU.mult).then_inc(s["scale_step"], 1)
                dve.wait_ge(s["scale_step"], g + 1)
                dve.tensor_reduce(rows[:, bass.ds(g * 2, 2), SCL], mine, AX.X, ALU.add).then_inc(s["scale_ready"], 1)

            dve.wait_ge(s_ld["route"], 16 * 8)
            pipelined(dve, NT2, [(7, choose), (3, recip2), (4, norm2)], ordered=True)

            dve.wait_ge(s["choice_ready"], NT2)
            flat = hT[:, 0:E * T]
            dve.tensor_tensor_scan(upto_here, flat, flat, 0.0, ALU.add, ALU.max).then_inc(s["scan_ready"], 1)
            dve.wait_ge(s["scan_ready"], 1)
            last_tile = upto_here.rearrange("p (e i) -> p e i", i=T)[:, :, T - 1]
            dve.tensor_copy(cnt[:, 0:1], last_tile[:, 0:1]).then_inc(s["cnt_ready"], 1)
            dve.tensor_tensor(cnt[:, 1:E], last_tile[:, 1:E], last_tile[:, 0:E - 1], ALU.subtract
                              ).then_inc(s["cnt_ready"], 1)
            dve.wait_ge(s["route_mm"], 1)
            dve.tensor_scalar(tot_i[:, 0:1], bank[0][0:E, 0:1], float(ST - 1), None, ALU.add
                              ).then_inc(s["route_dve"], 1)
            dve.wait_ge(s["route_dve"], 1)
            dve.tensor_scalar(tot_i[:, 1:2], tot_i[:, 0:1], ST.bit_length() - 1, None, ALU.arith_shift_right
                              ).then_inc(s["route_dve"], 1)
            dve.wait_ge(s["route_dve"], 2)
            dve.tensor_copy(ntile[:, 0:1], tot_i[:, 1:2])
            dve.tensor_scalar(ntile[:, 1:2], tot_i[:, 1:2], float(ST), None, ALU.mult).then_inc(s["route_dve"], 1)
            dve.wait_ge(s["route_mm"], 2)
            dve.tensor_copy(ends[:, :], bank[2][0:E, 0:1]).then_inc(s["route_dve"], 1)
            dve.wait_ge(s["route_dve"], 4)
            dve.tensor_scalar(started[:, :], tile_no[:, :], ends[:, 0:1], None, ALU.is_ge
                              ).then_inc(s["route_dve"], 1)
            dve.tensor_copy(used[:, :], bank[7][:, 0:1]).then_inc(s["used_ready"], 1)
            dve.tensor_copy(base[:, 0:1], bank[1][:, 0:1]).then_inc(s["place_step"], 1)
            dve.tensor_tensor(base[:, 1:E], bank[1][:, 1:E], last_tile[:, 0:E - 1], ALU.subtract).then_inc(s["place_step"], 1)
            dve.wait_ge(s["place_step"], 2)
            def by_expert(ap):
                return ap.rearrange("p (e i) -> p e i", i=T)
            dve.tensor_tensor(by_expert(place_of), by_expert(upto_here), spread_to(base[:, :], 2, T), ALU.add
                              ).then_inc(s["place_step"], 1)
            dve.wait_ge(s["place_step"], 3)
            dve.tensor_tensor(weighed, place_of, flat, ALU.mult).then_inc(s["place_step"], 1)
            dve.wait_ge(s["place_step"], 4)
            dve.tensor_reduce(slot_f[:, :], by_expert(weighed).rearrange("p e i -> p i e"), AX.X, ALU.add
                              ).then_inc(s["place_step"], 1)
            dve.wait_ge(s["place_step"], 5)
            dve.tensor_scalar(slot_i[:, :], slot_f[:, :], -1.0, None, ALU.add).then_inc(s["slots_ready"], 1)
            dve.wait_ge(s["route_mm"], 3)
            dve.tensor_scalar(owner[:, :], bank[3][:, 0:NTILE], float(E - 1), None, ALU.min
                              ).then_inc(s["owner_ready"], 1)
            dve.wait_ge(s["slots_ready"], 1)
            dve.tensor_scalar(slot_part[:, 0], slot_i[:, :], P.bit_length() - 1, None, ALU.arith_shift_right)
            dve.tensor_scalar(slot_part[:, 1], slot_i[:, :], P - 1, None, ALU.bitwise_and).then_inc(s["slot_step"], 1)
            dve.wait_ge(s["slot_step"], 1)
            dve.tensor_copy(slot_part_f[:, :, :], slot_part[:, :, :]).then_inc(s["slot_step"], 1)
            dve.wait_ge(s["slot_step"], 2)
            dve.tensor_tensor(col_1h, spread_to(count_up[:, 0:SC], 1, T), spread_to(slot_part_f[:, 0], 2, SC),
                              ALU.is_equal).then_inc(s["slot_step"], 1)
            dve.wait_ge(s["slot_step"], 3)
            dve.tensor_tensor(col_tok[:, :, 0:SC], col_1h, spread_to(count_up[:, 0:T], 2, SC), ALU.mult)
            dve.tensor_scalar(col_tok[:, :, SC:2 * SC], col_1h, p_plus1[:, 0:1], None, ALU.mult)
            for half in range(2):
                at = slice(half * T // 2, (half + 1) * T // 2)
                dve.tensor_tensor(place_1h[:, at], spread_to(count_up[:, :], 1, T // 2),
                                  spread_to(slot_part_f[:, 1, at], 2, P), ALU.is_equal).then_inc(s["place_1h"], 1)
            dve.wait_ge(s["token_mm"], 1)
            dve.tensor_copy(token1[:, 1], bank[4][:, SC:2 * SC]).then_inc(s["slot_step"], 1)
            dve.wait_ge(s["slot_step"], 4)
            dve.scalar_tensor_tensor(out=token1[:, 0], in0=bank[4][:, 0:SC], scalar=float(P), in1=token1[:, 1],
                                     op0=ALU.mult, op1=ALU.add).then_inc(s["slot_step"], 1)
            dve.wait_ge(s["slot_step"], 5)
            dve.tensor_scalar(fetch_at[:, :], token1[:, 0], -1.0, 0.0, ALU.add, ALU.max)
            dve.tensor_scalar(token1[:, 1], token1[:, 0], 0.0, float(N + 1), ALU.is_equal, ALU.mult
                              ).then_inc(s["slot_step"], 1)
            dve.wait_ge(s["slot_step"], 6)
            dve.scalar_tensor_tensor(out=store_at[:, :], in0=token1[:, 0], scalar=-1.0, in1=token1[:, 1],
                                     op0=ALU.add, op1=ALU.add).then_inc(s["fetch_ready"], 1)

            def predicated_after(signal, count):
                dve.wait_ge(signal, count)
                dve.sem_inc(s["wait_carried"], 1)

            low = 23 - LEVELS

            def add_one(g, par):
                dve.wait_ge(s["cell_ready"], g + 1)
                dve.tensor_scalar(plus1[:, par % 2], s_b[:, par % 2, 0:SI], 1.0, 2.0 - 2.0 ** -23, ALU.add, ALU.min
                                  ).then_inc(s["prep_step"], 1)

            def split(g, par):
                dve.wait_ge(s["prep_step"], 2 * g + 1)
                whole = plus1[:, par % 2].bitcast(I32)
                for b in range(LEVELS):
                    dve.tensor_scalar(bits[:, par % 2, b], whole, 1 << (low + b), None, ALU.bitwise_and)
                free_again(dve, s["frac_ready"], g, 2)
                dve.tensor_scalar(cell_at[:, par % 2].bitcast(I32), whole, -(1 << low), None, ALU.bitwise_and
                                  ).then_inc(s["prep_step"], 1)

            def halve_first(g, par):
                dve.wait_ge(s["prep_step"], 2 * g + 2)
                predicated_after(s["fill_ready"], 2 * g + 2)
                for a in range(2):
                    tab = wts[:, par, :, 2 * D + a * GRID + 1:2 * D + (a + 1) * GRID:2]
                    last = dve.copy_predicated(
                        look[:, par % 2, a].rearrange("p k (j n) -> p k j n", n=ST),
                        spread_to(bits[:, par % 2, 0].rearrange("p (j n) -> p j n", n=ST), 1, GRID // 2),
                        spread_to(tab.rearrange("p j k -> p k j"), 3, ST))
                last.then_inc(s["look_step"], 1)

            def halve(b):
                def run(g, par):
                    predicated_after(s["look_step"], LEVELS * g + b)
                    step = 1 << b
                    both = look[:, par % 2].rearrange("p a k n -> p (a k) n")
                    lo, hi = both[:, 0::step, :], both[:, step // 2::step, :]
                    dve.copy_predicated(lo, spread_to(bits[:, par % 2, b], 1, lo.shape[1]), hi
                                        ).then_inc(s["look_step"], 1)
                return run

            def value(g, par):
                dve.wait_ge(s["inside_ready"], g + 1)
                free_again(dve, s["y_mm"], g, 2)
                dve.scalar_tensor_tensor(out=s_c[:, par % 2, 0:SI], in0=inside[:, par % 2], scalar=float(GRID),
                                         in1=look[:, par % 2, 0, 0], op0=ALU.mult, op1=ALU.add
                                         ).then_inc(s["spline_ready"], 1)

            dve.wait_ge(s["used_ready"], 1)
            tiles = dve.value_load(used[0:1, 0:1], min_val=NI_SURE * TI - TI + 1, max_val=NTILE)
            pipelined(dve, NI, [(lag, where_used(dve, tiles, stage)) for lag, stage in
                                ((1, halve_first), (2, value), (1, halve(1)), (0, add_one), (1, halve(2)),
                                 (0, split), (1, halve(3)))], unroll=WR, sure=NI_SURE, ordered=True)


def _layout(x, x_txt, L0_tok_conv_w, L0_tok_conv_b, L0_tok_gamma, L0_tok_beta, L0_tok_dense_w, L0_tok_dense_b,
            L0_txt_bin_embeddings, L0_txt_w1, L0_txt_b1, L0_txt_w2, L0_txt_b2, L0_attn_expand, L0_attn_project,
            L0_attn_position_bias_mult, L0_ffn_gamma, L0_ffn_beta, L0_ffn_Wd, L0_ffn_spline_bases,
            L0_ffn_spline_slopes, L0_ffn_Wu, L0_ffn_scale):
    a = np.asarray
    keep = [i * WIN + j for i in range(WIN) for j in range(WIN)
            if not (i in (0, WIN - 1) and j in (0, WIN - 1))]
    px = np.pad(a(x), ((0, 0), (1, 1), (1, 1), (0, 0)))
    rows = [px[:, i:i + IMG:PATCH, j:j + IMG:PATCH, :][:, 0:GRID_W, 0:GRID_W] for i in range(WIN) for j in range(WIN)]
    win = np.stack([rows[k] for k in keep])
    win = win.transpose(0, 4, 1, 2, 3).reshape(KCH, KP, NG, GI)
    patches = np.ascontiguousarray(win.transpose(2, 1, 0, 3))
    w = a(L0_tok_conv_w)
    w5 = np.zeros((5, WIN, WIN, CH, D), np.float32)
    for k, (di, dj) in enumerate(((0, 0), (0, -1), (0, 1), (-1, 0), (1, 0))):
        w5[k, 1 + di:1 + di + PATCH, 1 + dj:1 + dj + PATCH] = w[:, :, k * CH:(k + 1) * CH, :]
    w5 = w5.reshape(5, WIN * WIN, CH, D)[:, keep].reshape(5, KCH, KP, D)
    w5 = np.ascontiguousarray(w5.transpose(2, 0, 1, 3)).reshape(KP, 5, KCH * D)
    bins = a(L0_txt_bin_embeddings)
    vectors = (a(L0_txt_w1)[0], L0_txt_b1, L0_txt_b2, L0_tok_conv_b, L0_tok_gamma, L0_tok_beta, L0_tok_dense_b,
               L0_ffn_gamma, L0_ffn_beta)
    ex = a(L0_attn_expand)
    qk = np.zeros((D, 64), np.float32)
    qk[:, 0:QK] = ex[:, 0:QK]
    qk[:, KOFF:KOFF + QK] = ex[:, QK:2 * QK]
    expand = np.concatenate([ex[:, 2 * QK:], qk], axis=1)
    packs = np.concatenate([a(L0_ffn_Wd).transpose(0, 2, 1), a(L0_ffn_Wu).transpose(0, 2, 1),
                            a(L0_ffn_spline_bases), a(L0_ffn_spline_slopes)], axis=2)
    at = np.arange(S)
    e = np.arange(E)
    bf = mybir.dt.np(BF16)
    return dict(
        patches=patches, w5=w5, w2=a(L0_txt_w2), bins=bins, bins_t=bins[1:].T, cols=np.stack([a(v) for v in vectors], 1),
        x_row=a(x_txt).reshape(B * S_TXT), x_col=a(x_txt).reshape(NG, GT).T, dense=a(L0_tok_dense_w),
        expand=expand, project=a(L0_attn_project).reshape(2, P, D).transpose(1, 0, 2),
        pbm=a(L0_attn_position_bias_mult).reshape(1), scale=a(L0_ffn_scale), packs=packs,
        ident=np.eye(P, dtype=np.float32),
        centre=(np.eye(P) - 1.0 / P).astype(np.float32),
        c128=np.tile(np.array([1.0 / P, 1.0], np.float32), (P, 1)),
        eps=np.tile(np.array([EPS_TOK, EPS, EPS * EPS], np.float32), (P, 1)),
        rel=(at[None, :] - at[:, None]).astype(np.float32),
        causal=(at[None, :] <= at[:, None]).astype(np.float32),
        veil=np.where(at[None, :] <= at[:, None], 0.0, -HUGE).astype(np.float32),
        before=np.triu(np.ones((P, P)), 1).astype(bf), upto=np.triu(np.ones((E, E))).astype(bf),
        ones_bf=np.ones((P, P)).astype(bf),
        tie=np.tile(((CL - 1 - e // TPC) * 4096 + (TPC - 1 - e % TPC)).astype(np.float32), (P, 1)),
        count_up=np.tile(np.arange(P, dtype=np.float32), (P, 1)),
        p_plus1=np.arange(1, P + 1, dtype=np.float32).reshape(P, 1),
        tile_no=np.tile(np.arange(NTILE, dtype=np.float32), (E, 1)),
    )


def kernel(**inputs):
    import concourse.bacc as bacc
    from concourse.bass_utils import run_bass_kernel_spmd

    arrays = {f"in_{k}": np.ascontiguousarray(v) for k, v in _layout(**inputs).items()}
    nc = bacc.Bacc("TRN2", target_bir_lowering=False, num_devices=1)
    t = {k[3:]: nc.dram_tensor(k, v.shape, mybir.dt.from_np(v.dtype), kind="ExternalInput").ap()
         for k, v in arrays.items()}
    out = nc.dram_tensor("out", (N, D), F32, kind="ExternalOutput").ap()
    build(nc, t, out)
    r = run_bass_kernel_spmd(nc, [arrays], core_ids=[0])
    return r.results[0]["out"].reshape(B, S, D)
```
